# Optimizing a Trainium2 kernel written in Bass

```python
import numpy as np
import jax
import jax.numpy as jnp

def _softmax(x, axis=-1):
    return jax.nn.softmax(x, axis=axis)

def _gelu(x):
    return jax.nn.gelu(x, approximate=True)

def _silu(x):
    return jax.nn.silu(x)

def _sigmoid(x):
    return jax.nn.sigmoid(x)

def _layernorm(x, axis=-1, eps=1e-05):
    m = jnp.mean(x, axis=axis, keepdims=True)
    v = jnp.var(x, axis=axis, keepdims=True)
    return (x - m) / jnp.sqrt(v + eps)

def _scatter_add(tgt, idx, src, axis=0):
    return tgt.at[idx].add(src)

def _segment_sum(src, seg, n):
    return jax.ops.segment_sum(src, seg, n)
kernel_name = 'mk_adj_resnorm_d4_adj_r2_f2558d'

def setup_inputs(seed: int=0):
    np.random.seed(seed)
    _w = jnp.asarray

    def _rec_inputs():
        import jax
        import jax.numpy as jnp
        _gk = jax.random.key(seed)
        x = -0.0005207 + 1.001 * jax.random.normal(jax.random.fold_in(_gk, 1), (4096, 128), jnp.float32)
        _a = jax.random.bernoulli(jax.random.fold_in(_gk, 2), 0.00195312, (4096, 4096))
        _a = jnp.logical_or(_a, jnp.swapaxes(_a, -1, -2))
        _a = jnp.logical_or(_a, jnp.eye(4096, dtype=bool))
        _af = _a.astype(jnp.float32)
        adj = _af
        return (x, adj)
    x, adj = _rec_inputs()

    def _L0_gnn_setup():
        import jax, jax.numpy as jnp
        import numpy as np
        NEG_BIG = -9000000000000000.0
        ALPHA = 0.2
        key = jax.random.key(seed)
        k1, k2, k3, k4 = jax.random.split(key, 4)
        N, F_in, F_out = (4096, 128, 128)
        h = jax.random.normal(k1, (N, F_in), dtype=jnp.float32)
        adj = jax.random.randint(k2, (N, N), 0, 2).astype(jnp.float32)
        W = jax.random.normal(k3, (F_in, F_out), dtype=jnp.float32) * (1.414 / np.sqrt(F_in))
        a = jax.random.normal(k4, (2 * F_out, 1), dtype=jnp.float32) * (1.414 / np.sqrt(2 * F_out))
        return {'h': h, 'adj': adj, 'W': W, 'a': a}
    _L0_gnn_all = _L0_gnn_setup()
    _L0_gnn_in = {k: v for k, v in _L0_gnn_all.items() if k in ('W', 'a')}
    del _L0_gnn_all

    def _L1_gnn_setup():
        import jax, jax.numpy as jnp
        import numpy as np
        from jax import lax
        D_MODEL = 128
        D_STATE = 16
        D_CONV = 4
        EXPAND = 2
        D_INNER = EXPAND * D_MODEL
        DT_RANK = (D_MODEL + 15) // 16
        N = 2048
        EPS = 1e-05

        def _mamba(h, w_in, conv_w, conv_b, w_xp, w_dt, b_dt, A_log, D_skip, w_out):
            L = h.shape[0]
            xz = h @ w_in
            xc, z = (xz[:, :D_INNER], xz[:, D_INNER:])
            xpad = jnp.pad(xc, ((D_CONV - 1, 0), (0, 0)))
            xconv = sum((xpad[k:k + L] * conv_w[:, k] for k in range(D_CONV))) + conv_b
            u = jax.nn.silu(xconv)
            dbc = u @ w_xp
            dt = jax.nn.softplus(dbc[:, :DT_RANK] @ w_dt + b_dt)
            B = dbc[:, DT_RANK:DT_RANK + D_STATE]
            C = dbc[:, DT_RANK + D_STATE:]
            A = -jnp.exp(A_log)
            dA = jnp.exp(dt[:, :, None] * A[None])
            dBu = dt[:, :, None] * B[:, None, :] * u[:, :, None]

            def step(hst, inp):
                dAt, dBut, Ct = inp
                hst = dAt * hst + dBut
                return (hst, hst @ Ct)
            _, ys = lax.scan(step, jnp.zeros((D_INNER, D_STATE), h.dtype), (dA, dBu, C))
            y = ys + u * D_skip
            y = y * jax.nn.silu(z)
            return y @ w_out
        key = jax.random.key(seed)
        ks = jax.random.split(key, 16)
        x = jax.random.normal(ks[0], (N, D_MODEL), dtype=jnp.float32)
        a = jax.random.uniform(ks[1], (N, N), dtype=jnp.float32)
        adj = a / a.sum(axis=1, keepdims=True)
        s = lambda fi, fo: 1.0 / np.sqrt(fi)
        gcn_w = jax.random.uniform(ks[2], (D_MODEL, D_MODEL), jnp.float32, -s(D_MODEL, 0), s(D_MODEL, 0))
        gcn_b = jnp.zeros((D_MODEL,), jnp.float32)
        ln_g = jnp.ones((D_MODEL,), jnp.float32)
        ln_b = jnp.zeros((D_MODEL,), jnp.float32)
        w_in = jax.random.normal(ks[3], (D_MODEL, 2 * D_INNER), jnp.float32) * s(D_MODEL, 0)
        conv_w = jax.random.normal(ks[4], (D_INNER, D_CONV), jnp.float32) * s(D_CONV, 0)
        conv_b = jnp.zeros((D_INNER,), jnp.float32)
        w_xp = jax.random.normal(ks[5], (D_INNER, DT_RANK + 2 * D_STATE), jnp.float32) * s(D_INNER, 0)
        w_dt = jax.random.normal(ks[6], (DT_RANK, D_INNER), jnp.float32) * s(DT_RANK, 0)
        b_dt = jnp.log(jnp.expm1(jnp.exp(jax.random.uniform(ks[7], (D_INNER,), jnp.float32, np.log(0.001), np.log(0.1)))))
        A_log = jnp.log(jnp.broadcast_to(jnp.arange(1, D_STATE + 1, dtype=jnp.float32), (D_INNER, D_STATE)))
        D_skip = jnp.ones((D_INNER,), jnp.float32)
        w_out = jax.random.normal(ks[8], (D_INNER, D_MODEL), jnp.float32) * s(D_INNER, 0)
        return dict(x=x, adj=adj, gcn_w=gcn_w, gcn_b=gcn_b, ln_g=ln_g, ln_b=ln_b, w_in=w_in, conv_w=conv_w, conv_b=conv_b, w_xp=w_xp, w_dt=w_dt, b_dt=b_dt, A_log=A_log, D_skip=D_skip, w_out=w_out)
    _L1_gnn_all = _L1_gnn_setup()
    _L1_gnn_in = {k: v for k, v in _L1_gnn_all.items() if k in ('gcn_w', 'gcn_b', 'ln_g', 'ln_b', 'w_in', 'conv_w', 'conv_b', 'w_xp', 'w_dt', 'b_dt', 'A_log', 'D_skip', 'w_out')}
    del _L1_gnn_all

    def _L2_gnn_setup():
        import jax, jax.numpy as jnp
        import numpy as np
        import math
        N = 4096
        FIN = 128
        FOUT = 128
        key = jax.random.key(seed)
        k1, k2, k3, k4 = jax.random.split(key, 4)
        x = jax.random.normal(k1, (N, FIN), dtype=jnp.float32)
        adj = jax.random.uniform(k2, (N, N), dtype=jnp.float32)
        stdv = 1.0 / math.sqrt(FOUT)
        W = jax.random.uniform(k3, (FIN, FOUT), minval=-stdv, maxval=stdv, dtype=jnp.float32)
        b = jax.random.uniform(k4, (FOUT,), minval=-stdv, maxval=stdv, dtype=jnp.float32)
        return {'input': x, 'adj': adj, 'W': W, 'b': b}
    _L2_gnn_all = _L2_gnn_setup()
    _L2_gnn_in = {k: v for k, v in _L2_gnn_all.items() if k in ('W', 'b')}
    del _L2_gnn_all

    def _L3_gnn_setup():
        import jax, jax.numpy as jnp
        import numpy as np
        N = 4096
        F = 128
        NEG_INF = -9000000000000000.0
        ALPHA = 0.2
        THRESH = 1e-06
        key = jax.random.key(seed)
        k1, k2, k3, k4 = jax.random.split(key, 4)
        x = jax.random.normal(k1, (N, F), jnp.float32)
        h0 = jax.random.normal(k2, (N, F), jnp.float32)
        limit = float(np.sqrt(6.0 / (2 * F + 1)) * 1.414)
        a = jax.random.uniform(k3, (2 * F, 1), jnp.float32, -limit, limit)
        temp = jnp.zeros((5,), jnp.float32)
        adj = jax.random.bernoulli(k4, 0.005, (N, N)).astype(jnp.float32)
        adj = jnp.maximum(adj, jnp.eye(N, dtype=jnp.float32))
        return {'x': x, 'h0': h0, 'a': a, 'temp': temp, 'adj': adj, 'l': 1}
    _L3_gnn_all = _L3_gnn_setup()
    _L3_gnn_in = {k: v for k, v in _L3_gnn_all.items() if k in ('h0', 'a', 'temp')}
    del _L3_gnn_all
    return {'x': x, 'adj': adj, 'L0_gnn_W': _L0_gnn_in['W'], 'L0_gnn_a': _L0_gnn_in['a'], 'L1_gnn_gcn_w': _L1_gnn_in['gcn_w'], 'L1_gnn_gcn_b': _L1_gnn_in['gcn_b'], 'L1_gnn_ln_g': _L1_gnn_in['ln_g'], 'L1_gnn_ln_b': _L1_gnn_in['ln_b'], 'L1_gnn_w_in': _L1_gnn_in['w_in'], 'L1_gnn_conv_w': _L1_gnn_in['conv_w'], 'L1_gnn_conv_b': _L1_gnn_in['conv_b'], 'L1_gnn_w_xp': _L1_gnn_in['w_xp'], 'L1_gnn_w_dt': _L1_gnn_in['w_dt'], 'L1_gnn_b_dt': _L1_gnn_in['b_dt'], 'L1_gnn_A_log': _L1_gnn_in['A_log'], 'L1_gnn_D_skip': _L1_gnn_in['D_skip'], 'L1_gnn_w_out': _L1_gnn_in['w_out'], 'L2_gnn_W': _L2_gnn_in['W'], 'L2_gnn_b': _L2_gnn_in['b'], 'L3_gnn_h0': _L3_gnn_in['h0'], 'L3_gnn_a': _L3_gnn_in['a'], 'L3_gnn_temp': _L3_gnn_in['temp']}

def reference(x, adj, L0_gnn_W, L0_gnn_a, L1_gnn_gcn_w, L1_gnn_gcn_b, L1_gnn_ln_g, L1_gnn_ln_b, L1_gnn_w_in, L1_gnn_conv_w, L1_gnn_conv_b, L1_gnn_w_xp, L1_gnn_w_dt, L1_gnn_b_dt, L1_gnn_A_log, L1_gnn_D_skip, L1_gnn_w_out, L2_gnn_W, L2_gnn_b, L3_gnn_h0, L3_gnn_a, L3_gnn_temp):
    import jax
    import jax.numpy as jnp

    def _L0_gnn_ref(h, adj, W, a):
        import jax, jax.numpy as jnp
        import numpy as np
        NEG_BIG = -9000000000000000.0
        ALPHA = 0.2
        F_out = W.shape[1]
        Wh = h @ W
        a1 = a[:F_out, 0]
        a2 = a[F_out:, 0]
        s1 = Wh @ a1
        s2 = Wh @ a2
        e = jax.nn.leaky_relu(s1[:, None] + s2[None, :], negative_slope=ALPHA)
        e = jnp.where(adj > 0, e, NEG_BIG)
        attention = jax.nn.softmax(e, axis=1)
        h_prime = attention @ Wh
        return jax.nn.elu(h_prime)

    def _L1_gnn_ref(x, adj, gcn_w, gcn_b, ln_g, ln_b, w_in, conv_w, conv_b, w_xp, w_dt, b_dt, A_log, D_skip, w_out):
        import jax, jax.numpy as jnp
        import numpy as np
        from jax import lax
        D_MODEL = 128
        D_STATE = 16
        D_CONV = 4
        EXPAND = 2
        D_INNER = EXPAND * D_MODEL
        DT_RANK = (D_MODEL + 15) // 16
        N = 2048
        EPS = 1e-05

        def _mamba(h, w_in, conv_w, conv_b, w_xp, w_dt, b_dt, A_log, D_skip, w_out):
            L = h.shape[0]
            xz = h @ w_in
            xc, z = (xz[:, :D_INNER], xz[:, D_INNER:])
            xpad = jnp.pad(xc, ((D_CONV - 1, 0), (0, 0)))
            xconv = sum((xpad[k:k + L] * conv_w[:, k] for k in range(D_CONV))) + conv_b
            u = jax.nn.silu(xconv)
            dbc = u @ w_xp
            dt = jax.nn.softplus(dbc[:, :DT_RANK] @ w_dt + b_dt)
            B = dbc[:, DT_RANK:DT_RANK + D_STATE]
            C = dbc[:, DT_RANK + D_STATE:]
            A = -jnp.exp(A_log)
            dA = jnp.exp(dt[:, :, None] * A[None])
            dBu = dt[:, :, None] * B[:, None, :] * u[:, :, None]

            def step(hst, inp):
                dAt, dBut, Ct = inp
                hst = dAt * hst + dBut
                return (hst, hst @ Ct)
            _, ys = lax.scan(step, jnp.zeros((D_INNER, D_STATE), h.dtype), (dA, dBu, C))
            y = ys + u * D_skip
            y = y * jax.nn.silu(z)
            return y @ w_out
        h = jax.nn.relu(adj @ x @ gcn_w + gcn_b)
        mu = h.mean(-1, keepdims=True)
        var = h.var(-1, keepdims=True)
        h = (h - mu) * lax.rsqrt(var + EPS) * ln_g + ln_b
        return _mamba(h, w_in, conv_w, conv_b, w_xp, w_dt, b_dt, A_log, D_skip, w_out)

    def _L2_gnn_ref(input, adj, W, b):
        import jax, jax.numpy as jnp
        import numpy as np
        import math
        N = 4096
        FIN = 128
        FOUT = 128
        A = adj + jnp.eye(adj.shape[0], dtype=adj.dtype)
        D = 1.0 / jnp.sqrt(jnp.sum(A, axis=1))
        A = A * D[:, None] * D[None, :]
        support = input @ W
        out = A @ support
        return jax.nn.relu(out + b)

    def _L3_gnn_ref(x, h0, a, temp, adj, l):
        import jax, jax.numpy as jnp
        import numpy as np
        N = 4096
        F = 128
        NEG_INF = -9000000000000000.0
        ALPHA = 0.2
        THRESH = 1e-06
        Fdim = x.shape[1]
        feat_1 = x @ a[:Fdim]
        feat_2 = x @ a[Fdim:]
        e = jax.nn.leaky_relu(feat_1 + feat_2.T, ALPHA)
        att = jnp.where(adj > 0, e, NEG_INF)
        U = jax.nn.softmax(att, axis=1)
        P = 0.5 * U
        prop_u = U @ x
        rowsum = jnp.sum(U * P, axis=1)
        coe = jax.nn.sigmoid(temp)
        xi = x * rowsum[:, None]
        feat_odd = prop_u - xi
        feat_even = x + prop_u - xi
        feat = coe[2] * feat_odd + (1.0 - coe[2]) * feat_even
        sgn = jnp.sign(feat)
        mod = jnp.abs(feat)
        mod = jnp.where(mod > THRESH, mod - THRESH, 0.0)
        feat = mod * sgn
        pu = U @ feat
        feat_odd2 = feat - coe[3] * pu
        feat_even2 = pu + feat_odd2 * rowsum[:, None]
        feat_odd2 = coe[0] * feat_odd2 + (1.0 - coe[0]) * h0
        out = coe[1] * feat_even2 + (1.0 - coe[1]) * feat_odd2
        return out
    x = _layernorm(x + _L0_gnn_ref(x, adj, L0_gnn_W, L0_gnn_a), axis=-1)
    x = _layernorm(x + _L1_gnn_ref(x, adj, L1_gnn_gcn_w, L1_gnn_gcn_b, L1_gnn_ln_g, L1_gnn_ln_b, L1_gnn_w_in, L1_gnn_conv_w, L1_gnn_conv_b, L1_gnn_w_xp, L1_gnn_w_dt, L1_gnn_b_dt, L1_gnn_A_log, L1_gnn_D_skip, L1_gnn_w_out), axis=-1)
    x = _layernorm(x + _L2_gnn_ref(x, adj, L2_gnn_W, L2_gnn_b), axis=-1)
    x = _layernorm(x + _L3_gnn_ref(x, L3_gnn_h0, L3_gnn_a, L3_gnn_temp, adj, 1), axis=-1)
    return x

_drawn_inputs = setup_inputs


def setup_inputs(seed=0):
    import zlib

    import numpy as np

    out = dict(_drawn_inputs(seed))
    spreads = {'L1_gnn_gcn_b': (0.0, 0.3),
     'L1_gnn_ln_g': (1.0, 0.2),
     'L1_gnn_ln_b': (0.0, 0.1),
     'L1_gnn_conv_b': (0.0, 0.1),
     'L1_gnn_D_skip': (1.0, 0.2),
     'L3_gnn_temp': (0.0, 0.508)}
    factors = {}
    for name, (base, spread) in spreads.items():
        noise = np.random.default_rng([zlib.crc32(name.encode()), seed]).standard_normal(out[name].shape)
        drawn = base * np.exp(spread * noise) if base else spread * noise
        out[name] = jnp.asarray(drawn.astype(out[name].dtype))
    for name, factor in factors.items():
        out[name] = (out[name] * factor).astype(out[name].dtype)
    return out
```

```python
from contextlib import ExitStack

import concourse.bass as bass
from concourse import mybir

P = 128
ALU = mybir.AluOpType
ACT = mybir.ActivationFunctionType
AX_X = mybir.AxisListType.X
F32 = mybir.dt.float32
F16 = mybir.dt.float16
BF16 = mybir.dt.bfloat16
F8 = mybir.dt.float8e4
U8 = mybir.dt.uint8
U32 = mybir.dt.uint32

N = 4096
FEAT = 128
TILES = N // P
CHUNK = 512
BLOCKS = CHUNK // P
STEPS = N // CHUNK
GROUP = 4
GROUPS = TILES // GROUP
RING = 4
PARTS = 3
ONE_F8 = 0x38
SLOPE = 0.2
SHIFT = 30.0
EPS = 1e-5
THRESH = 1e-6


def bcast_cols(col, n):
    return col.unsqueeze(2).broadcast_to([col.shape[0], col.shape[1], n])


class Arena:

    def __init__(self, nc, stage):
        self.nc, self.stage, self.sems, self.ctx = nc, stage, [], ExitStack()

    def __enter__(self):
        return self

    def __exit__(self, *failed):
        self.ctx.close()
        if failed[0] is None and self.sems:
            self.nc.clear_and_free_semaphores(self.sems)
            self.nc.all_engine_barrier()

    def sb(self, name, shape, dt):
        return self.ctx.enter_context(self.nc.sbuf_tensor(f"{self.stage}_{name}", shape, dt))

    def ps(self, name, shape, dt=F32):
        return self.ctx.enter_context(self.nc.psum_tensor(f"{self.stage}_{name}", shape, dt))

    def sem(self, name):
        self.sems.append(self.nc.alloc_semaphore(name=f"{self.stage}_{name}"))
        return self.sems[-1]

    def block(self):
        return self.ctx.enter_context(self.nc.Block())


def norm_blocks(dve, y, out, stats, mv, var_ready, rstd_ready, rstd_wait, rstd):
    for b in range(BLOCKS):
        dve.bn_stats(stats[:, b, :], y[:, b, :])
    dve.drain()
    for b in range(BLOCKS):
        dve.bn_aggr(mv[:, b, :], stats[:, b, :])
    dve.drain()
    dve.tensor_scalar(rstd[:, :, 0], mv[:, :, 1], EPS, None, ALU.add).then_inc(var_ready, 1)
    dve.wait_ge(rstd_ready, rstd_wait)
    for b in range(BLOCKS):
        last = dve.tensor_scalar(out[:, b, :], y[:, b, :], mv[:, b, 0:1], rstd[:, b, 1:2],
                                 ALU.subtract, ALU.mult)
    return last


def attention_pass(nc, kind, kept, dram):
    gat, spread, mix = (kind == k for k in ("gat", "spread", "mix"))
    pw = {"gat": FEAT + 1, "spread": FEAT + 2, "mix": FEAT}[kind]
    width = PARTS * pw + (1 if gat else 0)
    adj = kept["adj"]
    adj_u8 = adj[:, :].rearrange("p (t n) -> p t n", t=TILES)
    adj_u32 = adj[:, :].bitcast(U32).rearrange("p (t n) -> p t n", t=TILES)
    QU = CHUNK // 4
    s1c, s2c, ns2, F1, F2 = kept["s1c"], kept["s2c"], kept["ns2"], kept["F1"], kept["F2"]
    alpha, beta = kept["alpha"], kept["beta"]
    rden, rowsum, coe = kept["rden"], kept["rowsum"], kept["coe"]
    V_d = {"gat": dram["wh"], "spread": dram["x3"], "mix": dram["feat"]}[kind]
    V_g = V_d.rearrange("(g t p) f -> g p t f", p=P, t=GROUP)
    res_d = {"gat": dram["x"], "spread": dram["x3"], "mix": dram["feat"]}[kind]
    out_d = {"gat": dram["x1"], "spread": dram["feat"], "mix": dram["out"]}[kind]
    srow_d = dram["s_row_gat"] if gat else dram["s_row_spread"]

    def rows(ap, i):
        return ap[bass.ds(i * CHUNK, CHUNK), :].rearrange("(b p) f -> p b f", p=P)

    def row_chunk(i):
        return srow_d[:, bass.ds(i * CHUNK, CHUNK)].broadcast_to([P, CHUNK])

    with Arena(nc, kind) as a:
        G = [a.sb(f"G{k}", [P, TILES, width], BF16) for k in (1, 2)]
        m1 = a.sb("m1", [P, RING, GROUP, CHUNK], U8)
        m2 = a.sb("m2", [P, RING, GROUP, CHUNK], U8)
        s_now = a.sb("s_now", [P, CHUNK], F32)
        s_next = a.sb("s_next", [P, CHUNK], F32)
        R = a.sb("R", [P, BLOCKS, width], F32)
        xt = a.sb("xt", [P, BLOCKS, FEAT], F32)
        stats = a.sb("stats", [P, BLOCKS, 6], F32)
        mv = a.sb("mv", [P, BLOCKS, 2], F32)
        rstd = a.sb("rstd", [P, BLOCKS, 2], F32)
        half = a.sb("half", [P, BLOCKS], F32)
        mx = a.sb("mx", [P, 4], F32)
        small = a.sb("small", [P, 6, BLOCKS], F32)
        bank = [a.ps(f"bank{b}", [P, 512]) for b in range(2 * BLOCKS)]

        flat = R[:, :, :].rearrange("p b w -> p (b w)")
        gw = GROUP * pw
        g32 = [flat[:, k * gw:(k + 1) * gw].rearrange("p (t w) -> p t w", t=GROUP) for k in range(2)]
        parts = [G[k][:, :, 0:PARTS * pw].rearrange("p t (c w) -> p t c w", c=PARTS) for k in range(2)]

        vt = [xt[:, :, :], flat[:, 2 * gw:2 * gw + GROUP * FEAT].rearrange("p (t f) -> p t f", t=GROUP)]

        adj_part = [a.sem(f"adj_part{k}") for k in range(2)]
        adj_ready = a.sem("adj_ready")
        v_loaded = [a.sem(f"v_loaded{k}") for k in range(2)]
        v_used = a.sem("v_used")
        s_loaded = a.sem("s_loaded")
        s_first = a.sem("s_first")
        s_taken = a.sem("s_taken")
        mx_own = a.sem("mx_own")
        mx_all = a.sem("mx_all")
        args_ready = a.sem("args_ready")
        cols_ready = a.sem("cols_ready")
        g_scaled = a.sem("g_scaled")
        g_hi = a.sem("g_hi")
        g_rest = a.sem("g_rest")
        g_mid = a.sem("g_mid")
        masks_ready = a.sem("masks_ready")
        masks_used = a.sem("masks_used")
        banks_done = a.sem("banks_done")
        m2_scaled = a.sem("m2_scaled")
        banks_free = a.sem("banks_free")
        res_loaded = a.sem("res_loaded")
        res_used = a.sem("res_used")
        post_done = a.sem("post_done")
        stored = a.sem("stored")
        var_ready = a.sem("var_ready")
        rstd_ready = a.sem("rstd_ready")
        half_ready = a.sem("half_ready")
        elu_arg = a.sem("elu_arg")
        elu_exp = a.sem("elu_exp")
        late_free = a.sem("late_free")
        late_loaded = a.sem("late_loaded")
        pe_passed = a.sem("pe_passed")
        if gat:
            in_loaded = a.sem("in_loaded")
            wa_done = a.sem("wa_done")
            wa_copied = a.sem("wa_copied")
            cols_done = a.sem("cols_done")
            row_done = a.sem("row_done")
            row_copied = a.sem("row_copied")
            row_stored = [a.sem(f"row_stored{k}") for k in range(2)]
            wh_done = a.sem("wh_done")
            wh_copied = a.sem("wh_copied")
            wh_stored = [a.sem(f"wh_stored{k}") for k in range(2)]
            xT = G[0][:, :, :].rearrange("p t w -> p (t w)")[:, 0:2 * N].bitcast(F32)
            m1f = m1[:, :, :, :].rearrange("p r g n -> p (r g n)").bitcast(F32)
            m2f = m2[:, :, :, :].rearrange("p r g n -> p (r g n)").bitcast(F32)
            W0, W0T, a0, wa = m1f[:, 0:128], m1f[:, 128:256], m1f[:, 256:258], m1f[:, 258:260]
            row_sb = [m1f[0:1, 512 + 512 * k:1024 + 512 * k] for k in range(2)]
            wh_sb = [m2f[:, 512 * k:512 + 512 * k].rearrange("p (t f) -> p t f", t=GROUP) for k in range(2)]
            wh_g = dram["wh"].rearrange("(g t p) f -> g p t f", p=P, t=GROUP)
        block = a.block()

        @block.gpsimd
        def _(pool):
            pool.memset(half[:, :], -0.5).then_inc(half_ready, 1)
            pool.wait_ge(half_ready, 1)
            if gat:
                def load_adj(c):
                    src = dram["adjT"][:, c * CHUNK:(c + 1) * CHUNK].rearrange("(t p) n -> p t n", p=P)
                    dst = adj_u8[:, :, c * CHUNK:(c + 1) * CHUNK].bitcast(F8)
                    pool.dma_start(dst, src).then_inc(adj_part[c % 2], 16)

                def adj_arrived(c):
                    pool.wait_ge(adj_part[c % 2], 16 * (c // 2 + 1))
                    pool.sem_inc(adj_ready, 1)

                load_adj(0)
                load_adj(1)
            if not mix:
                pool.wait_ge(mx_own, 1)
                pool.partition_all_reduce(mx[:, 1:2], mx[:, 0:1], P, bass.bass_isa.ReduceOp.max)\
                    .then_inc(mx_all, 1)

            def root(s):
                pool.wait_ge(var_ready, s + 1)
                pool.tensor_tensor(rstd[:, :, 1], rstd[:, :, 0], half[:, :], ALU.pow).then_inc(rstd_ready, 1)

            if gat:
                for c in range(STEPS):
                    adj_arrived(c)
                    if c + 2 < STEPS:
                        load_adj(c + 2)
                    if c >= 2 and c % 2 == 0:
                        root((c - 2) // 2)
                with pool.Fori(3, STEPS) as s:
                    root(s)
            elif mix:
                with pool.Fori(0, STEPS) as s:
                    root(s)

        @block.sync
        def _(sp):
            if gat:
                sp.dma_start(W0T, dram["W0T"]).then_inc(in_loaded, 16)
                sp.dma_start(a0, dram["a0"]).then_inc(in_loaded, 16)
                sp.dma_start(W0, dram["W0"]).then_inc(in_loaded, 16)
                sp.dma_start(xT, dram["xT"]).then_inc(in_loaded, 16)
                for c in range(STEPS):
                    sp.wait_ge(row_copied, c + 1)
                    sp.dma_start(srow_d[:, c * CHUNK:(c + 1) * CHUNK], row_sb[c % 2])\
                        .then_inc(row_stored[c % 2], 16)
                for g in range(GROUPS):
                    sp.wait_ge(wh_copied, g + 1)
                    sp.dma_start(wh_g[g], wh_sb[g % 2]).then_inc(wh_stored[g % 2], 16)
                for k in range(2):
                    sp.wait_ge(row_stored[k], 16 * STEPS // 2)
                    sp.wait_ge(wh_stored[k], 16 * GROUPS // 2)
            sp.dma_start(s_now[:, :], row_chunk(0)).then_inc(s_first, 16)
            sp.dma_start(s_next[:, :], row_chunk(1)).then_inc(s_loaded, 16)
            for g in range(GROUPS):
                if g >= 2:
                    sp.wait_ge(v_used, g - 1)
                sp.dma_start(vt[g % 2], V_g[g]).then_inc(v_loaded[g % 2], 16)
            sp.wait_ge(v_used, GROUPS)

            def step(s, more):
                if more:
                    sp.wait_ge(s_taken, s + 1)
                    sp.dma_start(s_next[:, :], row_chunk(s + 2)).then_inc(s_loaded, 16)
                sp.wait_ge(res_used, s + 1)
                sp.dma_start(xt[:, :, :], rows(res_d, s)).then_inc(res_loaded, 16)
                if mix:
                    sp.wait_ge(late_free, s + 1)
                    sp.dma_start(R[:, :, FEAT:2 * FEAT], rows(dram["x3"], s)).then_inc(late_loaded, 16)
                    sp.dma_start(R[:, :, 2 * FEAT:3 * FEAT], rows(dram["h0"], s)).then_inc(late_loaded, 16)
                sp.wait_ge(post_done, s + 1)
                src = R[:, :, 2 * pw:2 * pw + FEAT]
                sp.dma_start(rows(out_d, s), src).then_inc(stored, 16)

            with sp.Fori(0, STEPS - 2) as s:
                step(s, True)
            with sp.Fori(STEPS - 2, STEPS) as s:
                step(s, False)
            sp.wait_ge(stored, 16 * (STEPS + 1))

        @block.tensor
        def _(pe):
            if gat:
                pe.wait_ge(in_loaded, 64)
                pe.matmul(bank[0][:, 0:2], W0T, a0, start=True, stop=True).then_inc(wa_done, 1)
                pe.wait_ge(wa_copied, 1)
                for t in range(TILES):
                    mm = pe.matmul(bank[1][:, 2 * t:2 * t + 2], xT[:, t * P:(t + 1) * P], wa,
                                   start=True, stop=True)
                mm.then_inc(cols_done, 1)
                for c in range(STEPS):
                    if c >= 2:
                        pe.wait_ge(row_copied, c - 1)
                    pe.matmul(bank[2 + c % 2][0:1, :], wa[:, 0:1], xT[:, c * CHUNK:(c + 1) * CHUNK],
                              start=True, stop=True).then_inc(row_done, 1)
                for g in range(GROUPS):
                    if g >= 2:
                        pe.wait_ge(wh_copied, g - 1)
                    for t in range(GROUP):
                        i = GROUP * g + t
                        mm = pe.matmul(bank[4 + g % 2][:, t * FEAT:(t + 1) * FEAT],
                                       xT[:, i * P:(i + 1) * P], W0, start=True, stop=True)
                    mm.then_inc(wh_done, 1)
                pe.wait_ge(wh_copied, GROUPS)
            with pe.Fori(0, STEPS) as s:
                for g in range(GROUPS):
                    pe.wait_ge(masks_ready, s * GROUPS + (g + 1))
                    pe.sem_inc(pe_passed, 1)
                    for b in range(BLOCKS):
                        if g == 0:
                            pe.wait_ge(banks_free, s * BLOCKS + (b + 1))
                            pe.sem_inc(pe_passed, 1)
                        for t in range(GROUP):
                            for k, m in enumerate((m1, m2)):
                                mask = m[:, g % RING, t, b * P:(b + 1) * P].bitcast(F8)
                                mm = pe.matmul(bank[2 * b + k][:, 0:width], mask,
                                               G[k][:, GROUP * g + t, :],
                                               start=(g == 0 and t == 0),
                                               stop=(g == GROUPS - 1 and t == GROUP - 1))
                        if g == GROUPS - 1:
                            mm.then_inc(banks_done, 1)
                    if g < GROUPS - 1:
                        mm.then_inc(masks_used, 1)

        @block.scalar
        def _(act):
            if gat:
                act.wait_ge(wa_done, 1)
                act.activation(wa, bank[0][:, 0:2], ACT.Copy).then_inc(wa_copied, 1)
                for c in range(STEPS):
                    act.wait_ge(row_done, c + 1)
                    if c >= 2:
                        act.wait_ge(row_stored[c % 2], 16 * (c // 2))
                    act.activation(row_sb[c % 2], bank[2 + c % 2][0:1, :], ACT.Copy).then_inc(row_copied, 1)
                for g in range(GROUPS):
                    act.wait_ge(wh_done, g + 1)
                    if g >= 2:
                        act.wait_ge(wh_stored[g % 2], 16 * (g // 2))
                    act.activation(wh_sb[g % 2], bank[4 + g % 2][:, :].rearrange("p (t f) -> p t f", t=GROUP),
                                   ACT.Copy).then_inc(wh_copied, 1)
            if not mix:
                act.wait_ge(args_ready, 1)
                act.activation(F1[:, :], s2c[:, :], ACT.Exp, bias=mx[:, 2:3])
                act.activation(F2[:, :], s2c[:, :], ACT.Exp, bias=mx[:, 3:4], scale=SLOPE)
                act.activation(alpha[:, :], alpha[:, :], ACT.Exp)
                act.activation(beta[:, :], beta[:, :], ACT.Exp).then_inc(cols_ready, 1)
            for g in range(GROUPS):
                for k in range(2):
                    act.wait_ge(g_scaled, 2 * g + k + 1)
                    act.activation(parts[k][:, GROUP * g:GROUP * (g + 1), 0, :], g32[k], ACT.Copy)\
                       .then_inc(g_hi, 1)
                for k in range(2):
                    act.wait_ge(g_rest, 2 * g + k + 1)
                    act.activation(parts[k][:, GROUP * g:GROUP * (g + 1), 1, :], g32[k], ACT.Copy)\
                       .then_inc(g_mid, 1)
            act.wait_ge(masks_ready, GROUPS)
            act.sem_inc(stored, 16)

            with act.Fori(0, STEPS) as s:
                act.wait_ge(stored, 16 * s + 16)
                for b in range(BLOCKS):
                    act.wait_ge(banks_done, s * BLOCKS + (b + 1))
                    act.activation(R[:, b, :], bank[2 * b + 1][:, 0:width], ACT.Copy,
                                   scale=beta[:, bass.ds(s * BLOCKS + b, 1)]).then_inc(m2_scaled, 1)
                if gat:
                    act.wait_ge(elu_arg, s + 1)
                    act.activation(R[:, :, pw:pw + FEAT], R[:, :, pw:pw + FEAT], ACT.Exp).then_inc(elu_exp, 1)

        @block.vector
        def _(dve):
            if gat:
                dve.wait_ge(cols_done, 1)
                cols = bank[1][:, 0:2 * TILES].rearrange("p (t c) -> p c t", c=2)
                dve.tensor_copy(s1c[:, :], cols[:, 0, :])
                dve.tensor_copy(s2c[:, :], cols[:, 1, :])
                dve.drain()
            if not mix:
                dve.tensor_reduce(mx[:, 0:1], s2c[:, :], AX_X, ALU.max).then_inc(mx_own, 1)
                dve.tensor_scalar(ns2[:, :], s2c[:, :], -1.0, None, ALU.mult)
                dve.wait_ge(mx_all, 1)
                dve.tensor_scalar(mx[:, 2:3], mx[:, 1:2], -1.0, SHIFT, ALU.mult, ALU.add)
                dve.tensor_scalar(mx[:, 3:4], mx[:, 1:2], -SLOPE, None, ALU.mult)
                dve.tensor_scalar(beta[:, :], s1c[:, :], mx[:, 1:2], 1.0 - SLOPE, ALU.add, ALU.mult)
                dve.drain()
                dve.tensor_scalar(alpha[:, :], beta[:, :], 0.0, -SHIFT, ALU.min, ALU.add)
                dve.drain()
                dve.tensor_scalar(beta[:, :], beta[:, :], -1.0, 0.0, ALU.mult, ALU.min)
                dve.drain().then_inc(args_ready, 1)
                dve.wait_ge(cols_ready, 1)
            dve.sem_inc(banks_free, BLOCKS)
            if gat:
                for k in range(2):
                    dve.wait_ge(wh_stored[k], 16 * GROUPS // 2)
                    dve.wait_ge(row_stored[k], 16 * STEPS // 2)
                for k in range(2):
                    dve.memset(G[k][:, :, width - 1:width], 1.0)
            F = (F1, F2)

            def mask(g, t, col):
                i = GROUP * g + t
                dve.scalar_tensor_tensor(m1[:, g % RING, t, :], s_now[:, :], ns2[:, i:i + 1],
                                         adj_u8[:, i, bass.ds(col * CHUNK, CHUNK)], ALU.is_gt, ALU.mult)

            def other_mask(g, col):
                dve.drain()
                dve.tensor_tensor(m2[:, g % RING, :, :].bitcast(U32),
                                  adj_u32[:, GROUP * g:GROUP * (g + 1), bass.ds(col * QU, QU)],
                                  m1[:, g % RING, :, :].bitcast(U32), ALU.bitwise_xor)\
                   .then_inc(masks_ready, 1)

            dve.wait_ge(s_first, 16)
            if gat:
                dve.wait_ge(adj_ready, 1)
            for g in range(GROUPS):
                here = slice(GROUP * g, GROUP * (g + 1))
                dve.wait_ge(v_loaded[g % 2], 16 * (g // 2 + 1))
                for k in range(2):
                    f = F[k][:, here]
                    dve.tensor_tensor(g32[k][:, :, 0:FEAT], vt[g % 2], bcast_cols(f, FEAT), ALU.mult)
                    if pw > FEAT:
                        dve.tensor_copy(g32[k][:, :, FEAT], f)
                    if pw > FEAT + 1:
                        dve.tensor_tensor(g32[k][:, :, FEAT + 1], f, f, ALU.mult)
                    dve.drain().then_inc(g_scaled, 1)
                dve.sem_inc(v_used, 1)
                if g >= RING:
                    dve.wait_ge(masks_used, g - RING + 1)
                for t in range(2):
                    mask(g, t, 0)
                for c, (seen, told) in enumerate(((g_hi, g_rest), (g_mid, None))):
                    for k in range(2):
                        dve.wait_ge(seen, 2 * g + k + 1)
                        if told is not None:
                            dve.tensor_tensor(g32[k], g32[k], parts[k][:, here, c, :], ALU.subtract)\
                               .then_inc(told, 1)
                        else:
                            dve.tensor_tensor(parts[k][:, here, 2, :], g32[k], parts[k][:, here, c, :],
                                              ALU.subtract)
                    if c == 0:
                        for t in range(2, GROUP):
                            mask(g, t, 0)
                other_mask(g, 0)
            dve.sem_inc(res_used, 1)

            def masks(s, g):
                if g < RING:
                    if g + RING < GROUPS - 1:
                        dve.wait_ge(masks_used, s * (GROUPS - 1) + (g + RING + 1))
                    else:
                        dve.wait_ge(banks_done, s * BLOCKS + BLOCKS)
                else:
                    dve.wait_ge(masks_used, s * (GROUPS - 1) + (GROUPS - 1 + g - RING + 1))
                for t in range(GROUP):
                    mask(g, t, s + 1)
                other_mask(g, s + 1)

            def evacuate(s):
                for b in range(BLOCKS):
                    dve.wait_ge(m2_scaled, s * BLOCKS + (b + 1))
                    for k in range(2):
                        if gat:
                            dve.tensor_copy(small[:, k, b:b + 1], bank[2 * b + k][:, width - 1:width])
                        if spread:
                            dve.tensor_reduce(small[:, k, b:b + 1], bank[2 * b + k][:, pw - 1:width:pw],
                                              AX_X, ALU.add)
                    if not mix:
                        dve.drain()
                    dve.scalar_tensor_tensor(R[:, b, :], bank[2 * b][:, 0:width],
                                             alpha[:, bass.ds(s * BLOCKS + b, 1)], R[:, b, :],
                                             ALU.mult, ALU.add).then_inc(banks_free, 1)
                dve.drain()

            def add_parts():
                n = FEAT if mix else FEAT + 1
                dve.tensor_tensor(R[:, :, pw:pw + n], R[:, :, pw:pw + n], R[:, :, 2 * pw:2 * pw + n], ALU.add)
                dve.drain()
                dve.tensor_tensor(R[:, :, 0:n], R[:, :, 0:n], R[:, :, pw:pw + n], ALU.add)
                dve.drain()

            A = R[:, :, 0:FEAT]
            B = R[:, :, pw:pw + FEAT]
            C = R[:, :, 2 * pw:2 * pw + FEAT]

            def finish_gat(s):
                mine = bass.ds(s * BLOCKS, BLOCKS)
                dve.tensor_tensor(kept["deg"][:, mine], small[:, 0, :], small[:, 1, :], ALU.add)
                add_parts()
                dve.reciprocal(small[:, 0, :], R[:, :, FEAT])
                dve.drain()
                dve.tensor_tensor(A, A, bcast_cols(small[:, 0, :], FEAT), ALU.mult)
                dve.drain()
                dve.tensor_scalar(B, A, 0.0, None, ALU.min).then_inc(elu_arg, 1)
                dve.wait_ge(res_loaded, 16 * s + 16)
                dve.scalar_tensor_tensor(C, A, 0.0, xt[:, :, :], ALU.max, ALU.add)
                dve.drain().then_inc(res_used, 1)
                dve.wait_ge(elu_exp, s + 1)
                dve.scalar_tensor_tensor(A, B, 1.0, C, ALU.subtract, ALU.add)
                dve.drain()
                norm_blocks(dve, A, C, stats, mv, var_ready, rstd_ready, s + 1, rstd)\
                    .then_inc(post_done, 1)

            def finish_spread(s):
                mine = bass.ds(s * BLOCKS, BLOCKS)
                q1, q2, u, v, rd, rs = (small[:, j, :] for j in range(6))
                add_parts()
                dve.reciprocal(rd, R[:, :, FEAT])
                dve.drain()
                dve.tensor_copy(rden[:, mine], rd)
                dve.tensor_tensor(u, rd, alpha[:, mine], ALU.mult)
                dve.tensor_tensor(v, rd, beta[:, mine], ALU.mult)
                dve.tensor_tensor(A, A, bcast_cols(rd, FEAT), ALU.mult)
                dve.drain()
                dve.tensor_tensor(q1, q1, u, ALU.mult)
                dve.tensor_tensor(q2, q2, v, ALU.mult)
                dve.drain()
                dve.tensor_tensor(q1, q1, u, ALU.mult)
                dve.tensor_tensor(q2, q2, v, ALU.mult)
                dve.drain()
                dve.tensor_tensor(rs, q1, q2, ALU.add)
                dve.drain()
                dve.tensor_scalar(rowsum[:, mine], rs, 0.5, None, ALU.mult)
                dve.tensor_scalar(u, rs, -0.5, coe[:, 1, 2:3], ALU.mult, ALU.add)
                dve.drain()
                dve.wait_ge(res_loaded, 16 * s + 16)
                dve.tensor_tensor(B, xt[:, :, :], bcast_cols(u, FEAT), ALU.mult)
                dve.drain().then_inc(res_used, 1)
                dve.tensor_tensor(A, A, B, ALU.add)
                dve.drain()
                dve.tensor_scalar(B, A, THRESH, 0.0, ALU.add, ALU.min)
                dve.tensor_scalar(C, A, THRESH, 0.0, ALU.subtract, ALU.max)
                dve.drain()
                dve.tensor_tensor(C, C, B, ALU.add).then_inc(post_done, 1)

            def finish_mix(s):
                mine = bass.ds(s * BLOCKS, BLOCKS)
                add_parts()
                dve.sem_inc(late_free, 1)
                dve.tensor_tensor(A, A, bcast_cols(rden[:, mine], FEAT), ALU.mult)
                dve.drain()
                dve.wait_ge(res_loaded, 16 * s + 16)
                feat = xt[:, :, :]
                dve.scalar_tensor_tensor(feat, A, coe[:, 2, 3:4], feat, ALU.mult, ALU.add)
                dve.wait_ge(late_loaded, 32 * s + 32)
                dve.tensor_scalar(C, C, coe[:, 1, 0:1], None, ALU.mult)
                dve.drain()
                dve.scalar_tensor_tensor(C, feat, coe[:, 0, 0:1], C, ALU.mult, ALU.add)
                dve.drain()
                dve.tensor_tensor(feat, feat, bcast_cols(rowsum[:, mine], FEAT), ALU.mult)
                dve.scalar_tensor_tensor(C, C, coe[:, 1, 1:2], B, ALU.mult, ALU.add)
                dve.drain()
                dve.tensor_tensor(A, A, feat, ALU.add)
                dve.drain().then_inc(res_used, 1)
                dve.scalar_tensor_tensor(A, A, coe[:, 0, 1:2], C, ALU.mult, ALU.add)
                dve.drain()
                norm_blocks(dve, A, C, stats, mv, var_ready, rstd_ready, s + 1, rstd)\
                    .then_inc(post_done, 1)

            finish = {"gat": finish_gat, "spread": finish_spread, "mix": finish_mix}[kind]
            with dve.Fori(0, STEPS - 1) as s:
                dve.drain()
                dve.wait_ge(s_loaded, 16 * s + 16)
                dve.tensor_copy(s_now[:, :], s_next[:, :])
                dve.drain().then_inc(s_taken, 1)
                if gat:
                    dve.wait_ge(adj_ready, s + 2)
                for g in range(RING - 1):
                    masks(s, g)
                evacuate(s)
                masks(s, RING - 1)
                finish(s)
                dve.drain()
                for g in range(RING, GROUPS):
                    masks(s, g)
            evacuate(STEPS - 1)
            finish(STEPS - 1)


def mamba_inputs_stage(nc, kept, dram):
    QU = CHUNK // 4
    SLOTS = 4
    SCALE = 1024.0
    TAPS = 4
    D = 2
    STATE = 16
    RANK = 8
    adj_u32 = kept["adj"][:, :].bitcast(U32).rearrange("p (t n) -> p t n", t=TILES)
    x1_g = dram["x1"].rearrange("(g t p) f -> g p t f", p=P, t=GROUP)

    with Arena(nc, "min") as a:
        Gx = a.sb("Gx", [P, TILES, 2, FEAT], F16)
        stage = a.sb("stage", [P, SLOTS, GROUP, QU], U32)
        stage8 = stage[:, :, :, :].bitcast(F8)
        ident = a.sb("ident", [P, P], F32)
        ones = a.sb("ones", [1, P], F32)
        gcn_w = a.sb("gcn_w", [P, FEAT], F32)
        gcn_b = a.sb("gcn_b", [1, FEAT], F32)
        w_in = a.sb("w_in", [P, 4 * P], F32)
        w_xp = a.sb("w_xp", [P, D, RANK + 2 * STATE], F32)
        w_dt = a.sb("w_dt", [RANK, D * P], F32)
        cvec = a.sb("cvec", [P, 2 + D * (TAPS + 3)], F32)
        ln_g, ln_b = cvec[:, 0:1], cvec[:, 1:2]
        dvec = cvec[:, 2:].rearrange("p (d c) -> p d c", d=D)
        conv_w, conv_b, b_dt, d_half = (dvec[:, :, 0:TAPS], dvec[:, :, TAPS:TAPS + 1],
                                        dvec[:, :, TAPS + 1:TAPS + 2], dvec[:, :, TAPS + 2:TAPS + 3])
        ax = a.sb("ax", [P, CHUNK], F32)
        h = a.sb("h", [P, BLOCKS, FEAT], F32)
        hT = a.sb("hT", [P, CHUNK], F32)
        xc = a.sb("xc", [P, D, TAPS - 1 + CHUNK], F32)
        conv = a.sb("conv", [P, D, CHUNK], F32)
        tanh_c = a.sb("tanh_c", [P, D, CHUNK], F32)
        v = tanh_c
        xin = [conv[:, k, :].rearrange("p (t f) -> p t f", t=GROUP) for k in range(2)]
        u2 = a.sb("u2", [P, D, CHUNK], F32)
        ud = a.sb("ud", [P, D, CHUNK], F32)
        sz = a.sb("sz", [P, D, CHUNK], F32)
        dbc = a.sb("dbc", [RANK + 2 * STATE, CHUNK], F32)
        na = a.sb("na", [P, D, CHUNK], F32)
        dt = a.sb("dt", [P, D, CHUNK], F32)
        du = a.sb("du", [P, D, CHUNK], F32)
        stats = a.sb("stats", [P, BLOCKS, 6], F32)
        mv = a.sb("mv", [P, BLOCKS, 2], F32)
        rstd = a.sb("rstd", [P, BLOCKS, 2], F32)
        half = a.sb("half", [P, BLOCKS], F32)
        ps_ax = a.ps("ax_ps", [P, 512])
        ps_h = a.ps("h_ps", [P, 512])
        ps_hT = a.ps("hT_ps", [P, 512])
        ps_xz = [a.ps(f"xz{m}", [P, 512]) for m in range(4)]
        ps_dbc = a.ps("dbc_ps", [P, 512])

        w_loaded = a.sem("w_loaded")
        x_loaded = [a.sem(f"x_loaded{k}") for k in range(2)]
        x_hi = a.sem("x_hi")
        x_split = a.sem("x_split")
        adj_staged = [a.sem(f"adj_staged{k}") for k in range(SLOTS)]
        adj_used = a.sem("adj_used")
        gcn_done = a.sem("gcn_done")
        ax_ready = a.sem("ax_ready")
        h_done = a.sem("h_done")
        h_relu = a.sem("h_relu")
        var_ready = a.sem("var_ready")
        rstd_ready = a.sem("rstd_ready")
        h_norm = a.sem("h_norm")
        hT_done = a.sem("hT_done")
        hT_ready = a.sem("hT_ready")
        xz_done = a.sem("xz_done")
        xc_ready = a.sem("xc_ready")
        halo_ready = a.sem("halo_ready")
        tz_ready = a.sem("tz_ready")
        sz_ready = a.sem("sz_ready")
        conv_ready = a.sem("conv_ready")
        tanh_ready = a.sem("tanh_ready")
        u_ready = a.sem("u_ready")
        ud_ready = a.sem("ud_ready")
        dbc_done = a.sem("dbc_done")
        dbc_ready = a.sem("dbc_ready")
        dt_done = a.sem("dt_done")
        v_ready = a.sem("v_ready")
        na_ready = a.sem("na_ready")
        log_ready = a.sem("log_ready")
        du_ready = a.sem("du_ready")
        stored = {k: a.sem(f"stored_{k}") for k in ("sz", "ud", "bc", "dt", "du")}
        consts = a.sem("consts")
        ident0 = a.sem("ident0")
        w_scaled = a.sem("w_scaled")
        all_stored = a.sem("all_stored")
        pool_passed = a.sem("pool_passed")
        pe_passed = a.sem("pe_passed")
        block = a.block()

        def store_to(name, c):
            return dram[name][:, :, bass.ds(c * CHUNK, CHUNK)].rearrange("d p n -> p d n")

        @block.sync
        def _(sp):
            for tile, name in ((gcn_w, "gcn_w"), (gcn_b, "gcn_b"), (w_in, "w_in"), (w_dt, "w_dt")):
                sp.dma_start(tile[:, :], dram[name]).then_inc(w_loaded, 16)
            sp.dma_start(w_xp[:, :, :], dram["w_xp"].rearrange("(d p) c -> p d c", p=P)).then_inc(w_loaded, 16)
            sp.dma_start(cvec[:, :], dram["cvec"]).then_inc(w_loaded, 16)
            for g in range(GROUPS):
                if g >= 2:
                    sp.wait_ge(x_split, g - 1)
                sp.dma_start(xin[g % 2], x1_g[g]).then_inc(x_loaded[g % 2], 16)
            with sp.Fori(0, STEPS) as c:
                for g in range(GROUPS):
                    if g == SLOTS - 1:
                        sp.wait_ge(ax_ready, c + 1)
                    else:
                        sp.wait_ge(adj_used, c * (GROUPS - 1) + (g + GROUPS - SLOTS + (g < SLOTS)))
                    sp.dma_start(stage[:, g % SLOTS, :, :],
                                 adj_u32[:, GROUP * g:GROUP * (g + 1), bass.ds(c * QU, QU)])\
                        .then_inc(adj_staged[g % SLOTS], 16)

        @block.gpsimd
        def _(pool):
            pool.memset(half[:, :], -0.5).then_inc(consts, 1)
            pool.memset(ones[:, :], 1.0).then_inc(consts, 1)
            pool.memset(xc[:, :, :], 0.0).then_inc(consts, 1)
            pool.memset(ident[:, :], 0.0).then_inc(ident0, 1)
            pool.wait_ge(ident0, 1)
            pool.affine_select(out=ident[:, :], in_=ident[:, :], compare_op=ALU.not_equal, fill=1.0, base=0,
                               pattern=[[-1, P]], channel_multiplier=1).then_inc(consts, 1)
            pool.wait_ge(consts, 4)
            pool.sem_inc(all_stored, 1)
            with pool.Fori(0, STEPS) as c:
                pool.wait_ge(var_ready, c + 1)
                pool.tensor_tensor(rstd[:, :, 1], rstd[:, :, 0], half[:, :], ALU.pow).then_inc(rstd_ready, 1)
                pool.wait_ge(sz_ready, c + 1)
                pool.sem_inc(pool_passed, 1)
                pool.dma_start(store_to("sz", c), sz[:, :, :]).then_inc(stored["sz"], 16)
                pool.wait_ge(ud_ready, c + 1)
                pool.sem_inc(pool_passed, 1)
                pool.dma_start(store_to("ud", c), ud[:, :, :]).then_inc(stored["ud"], 16)
                pool.wait_ge(dbc_ready, c + 1)
                pool.sem_inc(pool_passed, 1)
                pool.dma_start(dram["bc"][:, bass.ds(c * CHUNK, CHUNK)], dbc[RANK:RANK + 2 * STATE, :])\
                    .then_inc(stored["bc"], 16)
                pool.wait_ge(du_ready, c + 1)
                pool.sem_inc(pool_passed, 1)
                pool.dma_start(store_to("dt", c), dt[:, :, :]).then_inc(stored["dt"], 16)
                pool.dma_start(store_to("du", c), du[:, :, :]).then_inc(stored["du"], 16)
                for s in stored.values():
                    pool.wait_ge(s, 16 * c + 16)
                pool.sem_inc(all_stored, 1)

        @block.tensor
        def _(pe):
            pe.sem_inc(adj_used, GROUPS - 1)

            def gcn(c, g, first):
                pe.wait_ge(adj_staged[g % SLOTS], c * (16 * GROUPS // SLOTS) + 16 * (g // SLOTS + 1))
                if first:
                    pe.wait_ge(x_split, g + 1)
                if g == 0:
                    pe.wait_ge(ax_ready, c + 1)
                pe.sem_inc(pe_passed, 1)
                for t in range(GROUP):
                    i = GROUP * g + t
                    for k in range(2):
                        mm = pe.matmul(ps_ax[:, :], Gx[:, i, k, :], stage8[:, g % SLOTS, t, :],
                                       start=(i == 0 and k == 0), stop=(i == TILES - 1 and k == 1))
                    if t == GROUP - 1:
                        mm.then_inc(adj_used if g < GROUPS - 1 else gcn_done, 1)

            def hidden(c):
                pe.wait_ge(ax_ready, c + 2)
                for b in range(BLOCKS):
                    pe.matmul(ps_h[:, b * P:(b + 1) * P], ax[:, b * P:(b + 1) * P], gcn_w[:, :],
                              start=True, stop=False)
                    mm = pe.matmul(ps_h[:, b * P:(b + 1) * P], ones[:, :], gcn_b[:, :], start=False, stop=True)
                mm.then_inc(h_done, 1)

            def turn(c):
                pe.wait_ge(h_norm, c + 1)
                for b in range(BLOCKS):
                    mm = pe.transpose(ps_hT[:, b * P:(b + 1) * P], h[:, b, :], ident[:, :])
                mm.then_inc(hT_done, 1)

            def project(c):
                pe.wait_ge(hT_ready, c + 1)
                for m in range(4):
                    pe.matmul(ps_xz[m][:, :], w_in[:, m * P:(m + 1) * P], hT[:, :], start=True, stop=True)\
                        .then_inc(xz_done, 1)

            def low_rank(c):
                pe.wait_ge(u_ready, c + 1)
                for d in range(D):
                    mm = pe.matmul(ps_dbc[0:RANK + 2 * STATE, :], w_xp[:, d, :], u2[:, d, :],
                                   start=(d == 0), stop=(d == D - 1))
                mm.then_inc(dbc_done, 1)

            def steps_of_time(c):
                pe.wait_ge(dbc_ready, c + 1)
                for d in range(D):
                    pe.matmul(ps_xz[d][:, :], w_dt[:, d * P:(d + 1) * P], dbc[0:RANK, :],
                              start=True, stop=True).then_inc(dt_done, 1)

            for g in range(GROUPS):
                gcn(0, g, True)
            pe.wait_ge(w_loaded, 16 * 6)
            pe.wait_ge(consts, 4)
            pe.wait_ge(w_scaled, 1)
            with pe.Fori(0, STEPS - 1) as c:
                gcn(c + 1, 0, False)
                hidden(c)
                gcn(c + 1, 1, False)
                gcn(c + 1, 2, False)
                turn(c)
                gcn(c + 1, 3, False)
                project(c)
                gcn(c + 1, 4, False)
                gcn(c + 1, 5, False)
                gcn(c + 1, 6, False)
                low_rank(c)
                gcn(c + 1, 7, False)
                steps_of_time(c)
            for piece in (hidden, turn, project, low_rank, steps_of_time):
                piece(STEPS - 1)

        @block.scalar
        def _(act):
            act.sem_inc(ax_ready, 1)
            for g in range(GROUPS):
                act.wait_ge(x_loaded[g % 2], 16 * (g // 2 + 1))
                act.activation(Gx[:, GROUP * g:GROUP * (g + 1), 0, :], xin[g % 2], ACT.Copy,
                               scale=SCALE).then_inc(x_hi, 1)
            act.wait_ge(consts, 4)
            act.wait_ge(w_loaded, 16 * 6)
            with act.Fori(0, STEPS) as c:
                act.wait_ge(gcn_done, c + 1)
                act.activation(ax[:, :], ps_ax[:, :], ACT.Copy, scale=1.0 / SCALE).then_inc(ax_ready, 1)
                act.wait_ge(h_done, c + 1)
                act.activation(h[:, :, :], ps_h[:, :].rearrange("p (b f) -> p b f", b=BLOCKS), ACT.Relu)\
                    .then_inc(h_relu, 1)
                act.wait_ge(all_stored, c + 1)
                act.wait_ge(halo_ready, c + 1)
                for d in range(D):
                    act.wait_ge(xz_done, 4 * c + d + 1)
                    act.activation(xc[:, d, TAPS - 1:], ps_xz[d][:, :], ACT.Copy).then_inc(xc_ready, 1)
                for d in range(D):
                    act.wait_ge(xz_done, 4 * c + D + d + 1)
                    act.activation(sz[:, d, :], ps_xz[D + d][:, :], ACT.Tanh, scale=0.5).then_inc(tz_ready, 1)
                act.wait_ge(conv_ready, c + 1)
                act.activation(tanh_c[:, :, :], conv[:, :, :], ACT.Tanh, scale=0.5).then_inc(tanh_ready, 1)
                act.wait_ge(dbc_done, c + 1)
                act.activation(dbc[:, :], ps_dbc[0:RANK + 2 * STATE, :], ACT.Copy).then_inc(dbc_ready, 1)
                for d in range(D):
                    act.wait_ge(dt_done, D * c + d + 1)
                    act.activation(v[:, d, :], ps_xz[d][:, :], ACT.Identity, bias=b_dt[:, d, :])\
                        .then_inc(v_ready, 1)
                act.wait_ge(na_ready, c + 1)
                act.activation(na[:, :, :], na[:, :, :], ACT.Exp)
                act.drain()
                act.activation(na[:, :, :], na[:, :, :], ACT.Ln, bias=1.0).then_inc(log_ready, 1)

        @block.vector
        def _(dve):
            for g in range(GROUPS):
                dve.wait_ge(x_hi, g + 1)
                here = slice(GROUP * g, GROUP * (g + 1))
                dve.scalar_tensor_tensor(Gx[:, here, 1, :], xin[g % 2], SCALE, Gx[:, here, 0, :],
                                         ALU.mult, ALU.subtract).then_inc(x_split, 1)
            dve.wait_ge(w_loaded, 16 * 6)
            dve.wait_ge(consts, 4)
            dve.tensor_scalar(w_xp[:, :, :], w_xp[:, :, :], 0.5, None, ALU.mult)
            dve.tensor_scalar(d_half, d_half, 0.5, None, ALU.mult)
            dve.drain().then_inc(w_scaled, 1)
            dve.sem_inc(halo_ready, 1)
            with dve.Fori(0, STEPS) as c:
                dve.wait_ge(h_relu, c + 1)
                norm_blocks(dve, h, h, stats, mv, var_ready, rstd_ready, c + 1, rstd).then_inc(h_norm, 1)
                dve.wait_ge(hT_done, c + 1)
                dve.tensor_scalar(hT[:, :], ps_hT[:, :], ln_g, ln_b, ALU.mult, ALU.add).then_inc(hT_ready, 1)
                for d in range(D):
                    dve.wait_ge(xc_ready, D * c + d + 1)
                    dve.tensor_scalar(conv[:, d, :], xc[:, d, TAPS - 1:], conv_w[:, d, TAPS - 1:TAPS],
                                      conv_b[:, d, :], ALU.mult, ALU.add)
                for k in range(TAPS - 1):
                    dve.drain()
                    for d in range(D):
                        dve.scalar_tensor_tensor(conv[:, d, :], xc[:, d, k:k + CHUNK], conv_w[:, d, k:k + 1],
                                                 conv[:, d, :], ALU.mult, ALU.add)
                dve.drain().then_inc(conv_ready, 1)
                dve.tensor_copy(xc[:, :, 0:TAPS - 1], xc[:, :, CHUNK:CHUNK + TAPS - 1]).then_inc(halo_ready, 1)
                dve.wait_ge(tz_ready, D * (c + 1))
                for d in range(D):
                    last = dve.scalar_tensor_tensor(sz[:, d, :], sz[:, d, :], 1.0, ps_xz[D + d][:, :],
                                                    ALU.add, ALU.mult)
                last.then_inc(sz_ready, 1)
                dve.wait_ge(tanh_ready, c + 1)
                dve.scalar_tensor_tensor(u2[:, :, :], tanh_c[:, :, :], 1.0, conv[:, :, :], ALU.add, ALU.mult)
                dve.drain().then_inc(u_ready, 1)
                for d in range(D):
                    last = dve.tensor_scalar(ud[:, d, :], u2[:, d, :], d_half[:, d, :], None, ALU.mult)
                last.then_inc(ud_ready, 1)
                dve.wait_ge(v_ready, D * (c + 1))
                dve.scalar_tensor_tensor(na[:, :, :], v[:, :, :], -1.0, v[:, :, :], ALU.mult, ALU.min)\
                    .then_inc(na_ready, 1)
                dve.wait_ge(log_ready, c + 1)
                dve.scalar_tensor_tensor(dt[:, :, :], v[:, :, :], 0.0, na[:, :, :], ALU.max, ALU.add)
                dve.drain()
                dve.scalar_tensor_tensor(du[:, :, :], dt[:, :, :], 0.5, u2[:, :, :], ALU.mult, ALU.mult)\
                    .then_inc(du_ready, 1)
                dve.drain()


def mamba_scan_stage(nc, kept, dram):
    D = 2
    STATE = 16
    XRING = 4
    PAIR = 2
    PAIRS = STATE // PAIR

    with Arena(nc, "scan") as a:
        A = a.sb("A", [P, D, STATE], F32)
        w_out = a.sb("w_out", [P, D, FEAT], F32)
        ident = a.sb("ident", [P, P], F32)
        half = a.sb("half", [P, BLOCKS], F32)
        state = a.sb("state", [P, STATE, D], F32)
        dt = [a.sb(f"dt{k}", [P, D, CHUNK], F32) for k in range(2)]
        du = [a.sb(f"du{k}", [P, D, CHUNK], F32) for k in range(2)]
        ud = [a.sb(f"ud{k}", [P, D, CHUNK], F32) for k in range(2)]
        sz = [a.sb(f"sz{k}", [P, D, CHUNK], F32) for k in range(2)]
        B = [a.sb(f"B{k}", [P, PAIR, CHUNK], F32) for k in range(2)]
        C = [a.sb(f"C{k}", [P, PAIR, CHUNK], F32) for k in range(2)]
        X = [a.sb(f"X{k}", [P, D, CHUNK], F32) for k in range(XRING)]
        yv = a.sb("yv", [P, D, CHUNK], F32)
        xt = a.sb("xt", [P, BLOCKS, FEAT], F32)
        stats = a.sb("stats", [P, BLOCKS, 6], F32)
        mv = a.sb("mv", [P, BLOCKS, 2], F32)
        rstd = a.sb("rstd", [P, BLOCKS, 2], F32)
        dA = [a.ps(f"dA{k}", [P, D, CHUNK]) for k in range(2)]
        ps_y = a.ps("y", [P, D, CHUNK])
        ps_o = a.ps("o", [P, 512])

        w_loaded = a.sem("w_loaded")
        w_ready = a.sem("w_ready")
        A_exp = a.sem("A_exp")
        consts = a.sem("consts")
        ident0 = a.sem("ident0")
        in_loaded = [a.sem(f"in_loaded{k}") for k in range(2)]
        B_loaded = [a.sem(f"B_loaded{k}") for k in range(2)]
        C_loaded = [a.sem(f"C_loaded{k}") for k in range(2)]
        dA_ready = a.sem("dA_ready")
        h_ready = a.sem("h_ready")
        hC_ready = a.sem("hC_ready")
        X_used = a.sem("X_used")
        y_sum = a.sem("y_sum")
        y_ready = a.sem("y_ready")
        o_done = a.sem("o_done")
        x_loaded = a.sem("x_loaded")
        var_ready = a.sem("var_ready")
        rstd_ready = a.sem("rstd_ready")
        x2_ready = a.sem("x2_ready")
        x2_stored = a.sem("x2_stored")
        block = a.block()

        def chunk_loop(eng, body):
            body(0, 0, first=True)
            with eng.Fori(0, STEPS // 2 - 1) as i:
                body(i * 2 + 1, 1, first=False)
                body(i * 2 + 2, 0, first=False)
            body(STEPS - 1, 1, first=False)

        def per_tile(row):
            return row.unsqueeze(1).broadcast_to([P, D, CHUNK])

        def chunk_loads(c, parity):
            return 32 * c + (64 if parity == 0 else 32)

        def nodes(c):
            return slice(c * CHUNK, (c + 1) * CHUNK) if isinstance(c, int) else bass.ds(c * CHUNK, CHUNK)

        def rows(name, c):
            return dram[name][nodes(c), :].rearrange("(b p) f -> p b f", p=P)

        @block.sync
        def _(sp):
            sp.dma_start(A[:, :, :], dram["A_log"].rearrange("(d p) s -> p d s", p=P)).then_inc(w_loaded, 16)
            sp.dma_start(w_out[:, :, :], dram["w_out"].rearrange("(d p) f -> p d f", p=P)).then_inc(w_loaded, 16)

            def load_inputs(c, parity):
                for tile, name in ((dt, "dt"), (du, "du"), (ud, "ud"), (sz, "sz")):
                    sp.dma_start(tile[parity][:, :, :], dram[name][:, :, nodes(c)].rearrange("d p n -> p d n"))\
                        .then_inc(in_loaded[parity], 16)

            def body(c, parity, first):
                for j in range(PAIRS):
                    if not (first and j < 2):
                        sp.wait_ge(h_ready, c * STATE + (PAIR * (j - 1)))
                    sp.dma_start(B[j % 2][:, :, :], spread_rows(PAIR * j, c)).then_inc(B_loaded[j % 2], 16)
                    if not (first and j < 2):
                        sp.wait_ge(hC_ready, c * STATE + (PAIR * (j - 1)))
                    sp.dma_start(C[j % 2][:, :, :], spread_rows(STATE + PAIR * j, c))\
                        .then_inc(C_loaded[j % 2], 16)
                    if j == 3:
                        if not first:
                            sp.wait_ge(y_ready, c)
                            if not (isinstance(c, int) and c == STEPS - 1):
                                load_inputs(c + 1, 1 - parity)
                            finish(c - 1)
                        else:
                            load_inputs(1, 1)

            def finish(c):
                sp.wait_ge(x2_stored, 16 * c + 16)
                sp.dma_start(xt[:, :, :], rows("x1", c)).then_inc(x_loaded, 16)
                sp.wait_ge(x2_ready, c + 1)
                sp.dma_start(rows("x2", c), xt[:, :, :]).then_inc(x2_stored, 16)

            def spread_rows(r, c):
                return dram["bc"][r:r + PAIR, nodes(c)].partition_broadcast(P)

            sp.sem_inc(x2_stored, 16)
            load_inputs(0, 0)
            chunk_loop(sp, body)
            finish(STEPS - 1)
            sp.wait_ge(x2_stored, 16 * (STEPS + 1))

        @block.gpsimd
        def _(pool):
            pool.memset(half[:, :], -0.5).then_inc(consts, 1)
            pool.memset(state[:, :, :], 0.0).then_inc(consts, 1)
            pool.memset(ident[:, :], 0.0).then_inc(ident0, 1)
            pool.wait_ge(ident0, 1)
            pool.affine_select(out=ident[:, :], in_=ident[:, :], compare_op=ALU.not_equal, fill=1.0, base=0,
                               pattern=[[-1, P]], channel_multiplier=1).then_inc(consts, 1)
            pool.wait_ge(consts, 3)

            def root(c):
                pool.wait_ge(var_ready, c + 1)
                pool.tensor_tensor(rstd[:, :, 1], rstd[:, :, 0], half[:, :], ALU.pow).then_inc(rstd_ready, 1)

            def body(c, parity, first):
                for n in range(STATE):
                    pool.wait_ge(C_loaded[n // PAIR % 2], c * (16 * PAIRS // 2) + 16 * (n // PAIR // 2 + 1))
                    pool.wait_ge(h_ready, c * STATE + (n + 1))
                    x = X[n % XRING][:, :, :]
                    pool.tensor_tensor(x, x, per_tile(C[n // PAIR % 2][:, n % PAIR, :]), ALU.mult)\
                        .then_inc(hC_ready, 1)
                    if n == 5 and not first:
                        root(c - 1)

            chunk_loop(pool, body)
            root(STEPS - 1)

        @block.scalar
        def _(act):
            act.wait_ge(w_loaded, 32)
            act.activation(A[:, :, :], A[:, :, :], ACT.Exp).then_inc(A_exp, 1)
            act.wait_ge(w_ready, 1)

            def body(c, parity, first):
                act.wait_ge(in_loaded[parity], chunk_loads(c, parity))
                for n in range(STATE):
                    if not (first and n < 2):
                        act.wait_ge(h_ready, c * STATE + (n - 1))
                    for d in range(D):
                        last = act.activation(dA[n % 2][:, d, :], dt[parity][:, d, :], ACT.Exp,
                                              scale=A[:, d, n:n + 1])
                    last.then_inc(dA_ready, 1)

            chunk_loop(act, body)

        @block.tensor
        def _(pe):
            pe.wait_ge(consts, 3)
            pe.wait_ge(w_ready, 1)

            def output(c):
                pe.wait_ge(y_ready, c + 1)
                for b in range(BLOCKS):
                    for d in range(D):
                        mm = pe.matmul(ps_o[:, b * P:(b + 1) * P], y_of(c)[:, d, b * P:(b + 1) * P],
                                       w_out[:, d, :], start=(d == 0), stop=(d == D - 1))
                mm.then_inc(o_done, 1)

            def y_of(c):
                return yv[:, :, :]

            def body(c, parity, first):
                for n in range(STATE):
                    pe.wait_ge(hC_ready, c * STATE + (n + 1))
                    if n == 0 and not first:
                        output(c - 1)
                    for d in range(D):
                        mm = pe.matmul(ps_y[:, d, :], ident[:, :], X[n % XRING][:, d, :],
                                       start=(n == 0), stop=(n == STATE - 1))
                    mm.then_inc(X_used, 1)

            chunk_loop(pe, body)
            output(STEPS - 1)

        @block.vector
        def _(dve):
            dve.wait_ge(A_exp, 1)
            dve.tensor_scalar(A[:, :, :], A[:, :, :], -1.0, None, ALU.mult)
            dve.tensor_scalar(w_out[:, :, :], w_out[:, :, :], 0.5, None, ALU.mult)
            dve.drain().then_inc(w_ready, 1)
            dve.wait_ge(consts, 3)

            def y_readout(c, parity):
                dve.wait_ge(X_used, c * STATE + STATE)
                dve.tensor_tensor(yv[:, :, :], ud[parity][:, :, :], ps_y[:, :, :], ALU.add)
                dve.drain()
                dve.tensor_tensor(yv[:, :, :], yv[:, :, :], sz[parity][:, :, :], ALU.mult)\
                    .then_inc(y_ready, 1)

            def residual(c):
                dve.wait_ge(x_loaded, 16 * c + 16)
                dve.wait_ge(o_done, c + 1)
                dve.tensor_tensor(xt[:, :, :], xt[:, :, :],
                                  ps_o[:, :].rearrange("p (b f) -> p b f", b=BLOCKS), ALU.add)
                dve.drain()
                norm_blocks(dve, xt, xt, stats, mv, var_ready, rstd_ready, c + 1, rstd).then_inc(x2_ready, 1)
                dve.drain()

            def body(c, parity, first):
                dve.wait_ge(in_loaded[parity], chunk_loads(c, parity))
                for n in range(STATE):
                    x = X[n % XRING]
                    dve.wait_ge(B_loaded[n // PAIR % 2], c * (16 * PAIRS // 2) + 16 * (n // PAIR // 2 + 1))
                    if not (first and n < XRING):
                        dve.wait_ge(X_used, c * STATE + (n - XRING + 1))
                    dve.tensor_tensor(x[:, :, :], du[parity][:, :, :], per_tile(B[n // PAIR % 2][:, n % PAIR, :]),
                                      ALU.mult)
                    dve.drain()
                    dve.wait_ge(dA_ready, c * STATE + (n + 1))
                    for d in range(D):
                        dve.tensor_tensor_scan(x[:, d, :], dA[n % 2][:, d, :], x[:, d, :],
                                               state[:, n, d:d + 1], ALU.mult, ALU.add)
                    dve.drain()
                    dve.tensor_copy(state[:, n, :], x[:, :, CHUNK - 1]).then_inc(h_ready, 1)
                    if not first and n == 1:
                        y_readout(c - 1, 1 - parity)
                    if not first and n == 5:
                        residual(c - 1)

            chunk_loop(dve, body)
            y_readout(STEPS - 1, 1)
            residual(STEPS - 1)


def gcn_stage(nc, kept, dram):
    QU = CHUNK // 4
    SLOTS = 4
    SCALE = 1024.0
    adj_u32 = kept["adj"][:, :].bitcast(U32).rearrange("p (t n) -> p t n", t=TILES)
    x2_g = dram["x2"].rearrange("(g t p) f -> g p t f", p=P, t=GROUP)
    s1c, s2c, coe, deg = kept["s1c"], kept["s2c"], kept["coe"], kept["deg"]

    with Arena(nc, "gcn") as a:
        Gx = a.sb("Gx", [P, TILES, 2, FEAT], F16)
        xin = [a.sb(f"xin{k}", [P, GROUP, FEAT], F32) for k in range(2)]
        stage = a.sb("stage", [P, SLOTS, GROUP, QU], U32)
        stage8 = stage[:, :, :, :].bitcast(F8)
        ident = a.sb("ident", [P, P], F32)
        W = a.sb("W", [P, FEAT], F32)
        a3 = a.sb("a3", [P, 2], F32)
        bias = a.sb("bias", [P, FEAT], F32)
        D1 = a.sb("D1", [P, TILES], F32)
        Dc = a.sb("Dc", [P, TILES], F32)
        Ds = a.sb("Ds", [P, TILES], F32)
        halves = a.sb("halves", [P, TILES], F32)
        xn = a.sb("xn", [P, BLOCKS, FEAT], F32)
        xs = a.sb("xs", [P, BLOCKS, FEAT], F32)
        xt = a.sb("xt", [P, BLOCKS, FEAT], F32)
        y = a.sb("y", [P, BLOCKS, FEAT], F32)
        ax = a.sb("ax", [P, CHUNK], F32)
        x3T = a.sb("x3T", [P, CHUNK], F32)
        row = a.sb("row", [1, CHUNK], F32)
        stats = a.sb("stats", [P, BLOCKS, 6], F32)
        mv = a.sb("mv", [P, BLOCKS, 2], F32)
        rstd = a.sb("rstd", [P, BLOCKS, 2], F32)
        ps_ax = a.ps("ax_ps", [P, 512])
        ps_o = a.ps("o_ps", [P, 512])
        ps_T = a.ps("T_ps", [P, 512])
        ps_c = a.ps("c_ps", [P, 512])
        ps_r = a.ps("r_ps", [P, 512])

        w_loaded = a.sem("w_loaded")
        consts = a.sem("consts")
        ident0 = a.sem("ident0")
        deg1 = a.sem("deg1")
        D_ready = a.sem("D_ready")
        x_loaded = [a.sem(f"x_loaded{k}") for k in range(2)]
        x_scaled = a.sem("x_scaled")
        x_hi = a.sem("x_hi")
        x_split = a.sem("x_split")
        adj_staged = [a.sem(f"adj_staged{k}") for k in range(SLOTS)]
        adj_used = a.sem("adj_used")
        next_loaded = a.sem("next_loaded")
        own_ready = a.sem("own_ready")
        gcn_done = a.sem("gcn_done")
        ax_ready = a.sem("ax_ready")
        o_done = a.sem("o_done")
        res_loaded = a.sem("res_loaded")
        res_used = a.sem("res_used")
        var_ready = a.sem("var_ready")
        rstd_ready = a.sem("rstd_ready")
        x3_ready = a.sem("x3_ready")
        x3_stored = a.sem("x3_stored")
        T_done = a.sem("T_done")
        T_ready = a.sem("T_ready")
        scores_done = a.sem("scores_done")
        cols_copied = a.sem("cols_copied")
        row_ready = a.sem("row_ready")
        row_stored = a.sem("row_stored")
        temp_exp = a.sem("temp_exp")
        y_free = a.sem("y_free")
        pool_passed = a.sem("pool_passed")
        pe_passed = a.sem("pe_passed")
        block = a.block()

        def rows(name, c):
            here = slice(c * CHUNK, (c + 1) * CHUNK) if isinstance(c, int) else bass.ds(c * CHUNK, CHUNK)
            return dram[name][here, :].rearrange("(b p) f -> p b f", p=P)

        @block.sync
        def _(sp):
            sp.dma_start(W[:, :], dram["W2"]).then_inc(w_loaded, 16)
            sp.dma_start(a3[:, :], dram["a3"]).then_inc(w_loaded, 16)
            sp.dma_start(bias[:, :], dram["b2"].broadcast_to([P, FEAT])).then_inc(w_loaded, 16)
            sp.dma_start(coe[:, 0, :], dram["temp"].broadcast_to([P, 5])).then_inc(w_loaded, 16)
            for g in range(GROUPS):
                if g >= 2:
                    sp.wait_ge(x_split, g - 1)
                sp.dma_start(xin[g % 2][:, :, :], x2_g[g]).then_inc(x_loaded[g % 2], 16)
            with sp.Fori(0, STEPS) as c:
                for g in range(GROUPS):
                    if g == SLOTS - 1:
                        sp.wait_ge(ax_ready, c + 1)
                    else:
                        sp.wait_ge(adj_used, c * (GROUPS - 1) + (g + GROUPS - SLOTS + (g < SLOTS)))
                    sp.dma_start(stage[:, g % SLOTS, :, :],
                                 adj_u32[:, GROUP * g:GROUP * (g + 1), bass.ds(c * QU, QU)])\
                        .then_inc(adj_staged[g % SLOTS], 16)

        @block.gpsimd
        def _(pool):
            pool.memset(halves[:, :], -0.5).then_inc(consts, 1)
            pool.memset(ident[:, :], 0.0).then_inc(ident0, 1)
            pool.wait_ge(ident0, 1)
            pool.affine_select(out=ident[:, :], in_=ident[:, :], compare_op=ALU.not_equal, fill=1.0, base=0,
                               pattern=[[-1, P]], channel_multiplier=1).then_inc(consts, 1)
            pool.wait_ge(consts, 2)
            pool.wait_ge(deg1, 1)
            pool.tensor_tensor(Dc[:, :], D1[:, :], halves[:, :], ALU.pow).then_inc(D_ready, 1)
            pool.dma_start(xn[:, :, :], rows("x2", 0)).then_inc(next_loaded, 16)

            def chunk(c, more):
                pool.wait_ge(res_used, c + 1)
                pool.sem_inc(pool_passed, 1)
                pool.dma_start(xt[:, :, :], rows("x2", c)).then_inc(res_loaded, 16)
                if more:
                    pool.wait_ge(own_ready, c + 1)
                    pool.sem_inc(pool_passed, 1)
                    pool.dma_start(xn[:, :, :], rows("x2", c + 1)).then_inc(next_loaded, 16)
                pool.wait_ge(var_ready, c + 1)
                pool.tensor_tensor(rstd[:, :, 1], rstd[:, :, 0], halves[:, 0:BLOCKS], ALU.pow)\
                    .then_inc(rstd_ready, 1)
                pool.wait_ge(x3_ready, c + 1)
                pool.sem_inc(pool_passed, 1)
                pool.dma_start(rows("x3", c), y[:, :, :]).then_inc(x3_stored, 16)
                pool.wait_ge(x3_stored, 16 * c + 16)
                pool.sem_inc(y_free, 1)

            with pool.Fori(0, STEPS - 1) as c:
                chunk(c, True)
            chunk(STEPS - 1, False)

        @block.tensor
        def _(pe):
            pe.sem_inc(adj_used, GROUPS - 1)

            def gcn(c, g, first):
                pe.wait_ge(adj_staged[g % SLOTS], c * (16 * GROUPS // SLOTS) + 16 * (g // SLOTS + 1))
                if first:
                    pe.wait_ge(x_split, g + 1)
                if g == 0:
                    pe.wait_ge(ax_ready, c + 1)
                pe.sem_inc(pe_passed, 1)
                for t in range(GROUP):
                    i = GROUP * g + t
                    for k in range(2):
                        mm = pe.matmul(ps_ax[:, :], Gx[:, i, k, :], stage8[:, g % SLOTS, t, :],
                                       start=(i == 0 and k == 0), stop=False)
                if g < GROUPS - 1:
                    mm.then_inc(adj_used, 1)
                else:
                    pe.wait_ge(own_ready, c + 1)
                    for b in range(BLOCKS):
                        mm = pe.matmul(ps_ax[:, b * P:(b + 1) * P], xs[:, b, :], ident[:, :],
                                       start=False, stop=(b == BLOCKS - 1))
                    mm.then_inc(gcn_done, 1)

            def weigh(c):
                pe.wait_ge(ax_ready, c + 2)
                for b in range(BLOCKS):
                    mm = pe.matmul(ps_o[:, b * P:(b + 1) * P], ax[:, b * P:(b + 1) * P], W[:, :],
                                   start=True, stop=True)
                mm.then_inc(o_done, 1)

            def turn(c):
                pe.wait_ge(x3_ready, c + 1)
                for b in range(BLOCKS):
                    mm = pe.transpose(ps_T[:, b * P:(b + 1) * P], y[:, b, :], ident[:, :])
                mm.then_inc(T_done, 1)

            def scores(c):
                pe.wait_ge(T_ready, c + 1)
                for b in range(BLOCKS):
                    pe.matmul(ps_c[:, 2 * b:2 * b + 2], x3T[:, b * P:(b + 1) * P], a3[:, :],
                              start=True, stop=True)
                pe.matmul(ps_r[0:1, :], a3[:, 0:1], x3T[:, :], start=True, stop=True).then_inc(scores_done, 1)

            pe.wait_ge(w_loaded, 64)
            pe.wait_ge(consts, 2)
            for g in range(GROUPS):
                gcn(0, g, True)
            with pe.Fori(0, STEPS - 1) as c:
                gcn(c + 1, 0, False)
                weigh(c)
                for g in range(1, 5):
                    gcn(c + 1, g, False)
                turn(c)
                gcn(c + 1, 5, False)
                scores(c)
                gcn(c + 1, 6, False)
                gcn(c + 1, 7, False)
            for piece in (weigh, turn, scores):
                piece(STEPS - 1)

        @block.scalar
        def _(act):
            act.sem_inc(ax_ready, 1)
            for g in range(GROUPS):
                act.wait_ge(x_scaled, g + 1)
                act.activation(Gx[:, GROUP * g:GROUP * (g + 1), 0, :], xin[g % 2][:, :, :], ACT.Copy,
                               scale=SCALE).then_inc(x_hi, 1)
            act.wait_ge(w_loaded, 64)
            act.activation(coe[:, 0, :], coe[:, 0, :], ACT.Exp, scale=-1.0).then_inc(temp_exp, 1)
            act.wait_ge(consts, 2)
            act.sem_inc(row_stored, 16)
            with act.Fori(0, STEPS) as c:
                act.wait_ge(gcn_done, c + 1)
                act.activation(ax[:, :], ps_ax[:, :], ACT.Copy, scale=1.0 / SCALE).then_inc(ax_ready, 1)
                act.wait_ge(T_done, c + 1)
                act.activation(x3T[:, :], ps_T[:, :], ACT.Copy).then_inc(T_ready, 1)
                act.wait_ge(row_stored, 16 * c + 16)
                act.wait_ge(scores_done, c + 1)
                act.activation(row[:, :], ps_r[0:1, :], ACT.Copy).then_inc(row_ready, 1)
                act.wait_ge(row_ready, c + 1)
                act.dma_start(dram["s_row_spread"][:, bass.ds(c * CHUNK, CHUNK)], row[:, :])\
                    .then_inc(row_stored, 16)
            act.wait_ge(row_stored, 16 * (STEPS + 1))

        @block.vector
        def _(dve):
            dve.tensor_scalar(D1[:, :], deg[:, :], 1.0, None, ALU.add).then_inc(deg1, 1)
            dve.wait_ge(D_ready, 1)
            dve.tensor_scalar(Ds[:, :], Dc[:, :], SCALE, None, ALU.mult)
            for g in range(GROUPS):
                here = slice(GROUP * g, GROUP * (g + 1))
                x = xin[g % 2][:, :, :]
                dve.wait_ge(x_loaded[g % 2], 16 * (g // 2 + 1))
                dve.tensor_tensor(x, x, bcast_cols(Dc[:, here], FEAT), ALU.mult).then_inc(x_scaled, 1)
                dve.wait_ge(x_hi, g + 1)
                dve.scalar_tensor_tensor(Gx[:, here, 1, :], x, SCALE, Gx[:, here, 0, :],
                                         ALU.mult, ALU.subtract).then_inc(x_split, 1)
            dve.wait_ge(temp_exp, 1)
            dve.tensor_scalar(coe[:, 1, :], coe[:, 0, :], 1.0, None, ALU.add)
            dve.drain()
            dve.reciprocal(coe[:, 0, :], coe[:, 1, :])
            dve.drain()
            dve.tensor_scalar(coe[:, 1, :], coe[:, 0, :], -1.0, 1.0, ALU.mult, ALU.add)
            dve.tensor_scalar(coe[:, 2, :], coe[:, 0, :], -1.0, None, ALU.mult)

            def own_rows(c):
                dve.wait_ge(next_loaded, 16 * c + 16)
                dve.tensor_tensor(xs[:, :, :], xn[:, :, :], bcast_cols(Ds[:, blocks_of(c)], FEAT), ALU.mult)\
                    .then_inc(own_ready, 1)

            def blocks_of(c):
                return slice(BLOCKS * c, BLOCKS * (c + 1)) if isinstance(c, int) else bass.ds(c * BLOCKS, BLOCKS)

            def finish(c):
                dve.wait_ge(o_done, c + 1)
                dve.wait_ge(y_free, c + 1)
                for b in range(BLOCKS):
                    at = slice(BLOCKS * c + b, BLOCKS * c + b + 1) if isinstance(c, int) \
                        else bass.ds(c * BLOCKS + b, 1)
                    dve.scalar_tensor_tensor(y[:, b, :], ps_o[:, b * P:(b + 1) * P], Dc[:, at], bias[:, :],
                                             ALU.mult, ALU.add)
                dve.drain()
                dve.wait_ge(res_loaded, 16 * c + 16)
                dve.scalar_tensor_tensor(y[:, :, :], y[:, :, :], 0.0, xt[:, :, :], ALU.max, ALU.add)
                dve.drain().then_inc(res_used, 1)
                norm_blocks(dve, y, y, stats, mv, var_ready, rstd_ready, c + 1, rstd).then_inc(x3_ready, 1)
                dve.wait_ge(scores_done, c + 1)
                cols = ps_c[:, 0:2 * BLOCKS].rearrange("p (b c) -> p c b", c=2)
                dve.tensor_copy(s1c[:, blocks_of(c)], cols[:, 0, :])
                dve.tensor_copy(s2c[:, blocks_of(c)], cols[:, 1, :])
                dve.drain().then_inc(cols_copied, 1)

            dve.sem_inc(y_free, 1)
            dve.sem_inc(res_used, 1)
            own_rows(0)
            with dve.Fori(0, STEPS - 1) as c:
                dve.wait_ge(gcn_done, c + 1)
                own_rows(c + 1)
                finish(c)
            finish(STEPS - 1)


def build_program(nc, dram, stages=("gat", "mamba", "gcn", "spread", "mix")):
    with Arena(nc, "kept") as a:
        kept = {"adj": a.sb("adj", [P, TILES * N], U8)}
        for name in ("s1c", "s2c", "ns2", "F1", "F2", "alpha", "beta", "deg", "rden", "rowsum"):
            kept[name] = a.sb(name, [P, TILES], F32)
        kept["coe"] = a.sb("coe", [P, 3, 5], F32)
        for stage in stages:
            if stage in ("gat", "spread", "mix"):
                attention_pass(nc, stage, kept, dram)
            elif stage == "mamba":
                mamba_inputs_stage(nc, kept, dram)
                mamba_scan_stage(nc, kept, dram)
            else:
                gcn_stage(nc, kept, dram)


def kernel(**inputs):
    import numpy as _np
    import concourse.bacc as _bacc
    from concourse.bass_utils import run_bass_kernel_spmd as _run

    i = {k: _np.asarray(v) for k, v in inputs.items()}
    given = {
        "x": i["x"], "xT": i["x"].T, "adjT": i["adj"].T,
        "W0": i["L0_gnn_W"], "W0T": i["L0_gnn_W"].T, "a0": i["L0_gnn_a"].reshape(2, FEAT).T,
        "h0": i["L3_gnn_h0"],
        "W2": i["L2_gnn_W"], "b2": i["L2_gnn_b"].reshape(1, FEAT),
        "a3": i["L3_gnn_a"].reshape(2, FEAT).T, "temp": i["L3_gnn_temp"].reshape(1, 5),
        "gcn_w": i["L1_gnn_gcn_w"], "gcn_b": i["L1_gnn_gcn_b"].reshape(1, FEAT),
        "w_in": i["L1_gnn_w_in"], "w_xp": i["L1_gnn_w_xp"], "w_dt": i["L1_gnn_w_dt"],
        "A_log": i["L1_gnn_A_log"], "w_out": i["L1_gnn_w_out"],
        "cvec": _np.concatenate([i["L1_gnn_ln_g"][:, None], i["L1_gnn_ln_b"][:, None],
                                 _np.concatenate([i["L1_gnn_conv_w"], i["L1_gnn_conv_b"][:, None],
                                                  i["L1_gnn_b_dt"][:, None], i["L1_gnn_D_skip"][:, None]], 1)
                                 .reshape(2, P, 7).transpose(1, 0, 2).reshape(P, 14)], 1),
    }
    nc = _bacc.Bacc("TRN2", target_bir_lowering=False, num_devices=1)
    arrays, dram = {}, {}
    for name, v in given.items():
        v = _np.ascontiguousarray(v)
        arrays[f"in_{name}"] = v
        dram[name] = nc.dram_tensor(f"in_{name}", v.shape, mybir.dt.from_np(v.dtype), kind="ExternalInput").ap()
    for name, shape in (("wh", [N, FEAT]), ("x1", [N, FEAT]), ("x2", [N, FEAT]), ("x3", [N, FEAT]),
                        ("feat", [N, FEAT]), ("s_row_gat", [1, N]), ("s_row_spread", [1, N])):
        dram[name] = nc.dram_tensor(f"scratch_{name}", shape, F32, kind="Internal").ap()
    for name in ("dt", "du", "ud", "sz"):
        dram[name] = nc.dram_tensor(f"scratch_{name}", [2, P, N], F32, kind="Internal").ap()
    dram["bc"] = nc.dram_tensor("scratch_bc", [32, N], F32, kind="Internal").ap()
    dram["out"] = nc.dram_tensor("out_x", [N, FEAT], F32, kind="ExternalOutput").ap()
    build_program(nc, dram, STAGES)
    r = _run(nc, [arrays], core_ids=[0])
    return r.results[0]["out_x"]


STAGES = ("gat", "mamba", "gcn", "spread", "mix")
```

```python
from contextlib import ExitStack

import concourse.bass as bass
from concourse import mybir

P = 128
ALU = mybir.AluOpType
ACT = mybir.ActivationFunctionType
AX_X = mybir.AxisListType.X
F32 = mybir.dt.float32
F16 = mybir.dt.float16
BF16 = mybir.dt.bfloat16
F8 = mybir.dt.float8e4
U8 = mybir.dt.uint8
I8 = mybir.dt.int8
U32 = mybir.dt.uint32

N = 4096
FEAT = 128
TILES = N // P
CHUNK = 512
BLOCKS = CHUNK // P
STEPS = N // CHUNK
GROUP = 4
GROUPS = TILES // GROUP
RING = 4
FIRST_PARTS = 4
INPUT_LOADS = 5
PARTS = 3
LOW = 2048.0
ONE_F8 = 0x38
SLOPE = 0.2
SHIFT = 30.0
EPS = 1e-5
THRESH = 1e-6


def bcast_cols(col, n):
    return col.unsqueeze(2).broadcast_to([col.shape[0], col.shape[1], n])


class Arena:

    def __init__(self, nc, stage):
        self.nc, self.stage, self.sems, self.ctx = nc, stage, [], ExitStack()

    def __enter__(self):
        return self

    def __exit__(self, *failed):
        self.ctx.close()
        if failed[0] is None and self.sems:
            self.nc.clear_and_free_semaphores(self.sems)
            self.nc.all_engine_barrier()

    def sb(self, name, shape, dt):
        return self.ctx.enter_context(self.nc.sbuf_tensor(f"{self.stage}_{name}", shape, dt))

    def ps(self, name, shape, dt=F32):
        return self.ctx.enter_context(self.nc.psum_tensor(f"{self.stage}_{name}", shape, dt))

    def sem(self, name):
        self.sems.append(self.nc.alloc_semaphore(name=f"{self.stage}_{name}"))
        return self.sems[-1]

    def block(self):
        return self.ctx.enter_context(self.nc.Block())


def norm_moments(dve, y, stats, mv, var_ready, rstd):
    for b in range(BLOCKS):
        dve.bn_stats(stats[:, b, :], y[:, b, :])
    dve.drain()
    for b in range(BLOCKS):
        dve.bn_aggr(mv[:, b, :], stats[:, b, :])
    dve.drain()
    dve.tensor_scalar(rstd[:, :, 0], mv[:, :, 1], EPS, None, ALU.add).then_inc(var_ready, 1)


def norm_apply(dve, y, out, mv, rstd_ready, rstd_wait, rstd):
    dve.wait_ge(rstd_ready, rstd_wait)
    for b in range(BLOCKS):
        last = dve.tensor_scalar(out[:, b, :], y[:, b, :], mv[:, b, 0:1], rstd[:, b, 1:2],
                                 ALU.subtract, ALU.mult)
    return last


def norm_blocks(dve, y, out, stats, mv, var_ready, rstd_ready, rstd_wait, rstd):
    norm_moments(dve, y, stats, mv, var_ready, rstd)
    return norm_apply(dve, y, out, mv, rstd_ready, rstd_wait, rstd)


def attention_pass(nc, kind, kept, dram):
    gat, spread, mix = (kind == k for k in ("gat", "spread", "mix"))
    pw = {"gat": FEAT + 1, "spread": FEAT + 2, "mix": FEAT}[kind]
    width = PARTS * pw + (1 if gat else 0)
    low = not gat
    width2 = 2 * pw if low else width
    adj = kept["adj"]
    adj_u8 = adj[:, :].rearrange("p (t n) -> p t n", t=TILES)
    adj_u32 = adj[:, :].bitcast(U32).rearrange("p (t n) -> p t n", t=TILES)
    QU = CHUNK // 4
    s1c, s2c, F1, F2 = kept["s1c"], kept["s2c"], kept["F1"], kept["F2"]
    alpha, beta, beta_low = kept["alpha"], kept["beta"], kept["beta_low"]
    rden, rowsum, coe = kept["rden"], kept["rowsum"], kept["coe"]
    if not gat:
        V_g = dram["x3" if spread else "feat"].rearrange("(g t p) f -> g p t f", p=P, t=GROUP)
    res_d = {"gat": dram["x"], "spread": dram["x3"], "mix": dram["feat"]}[kind]
    out_d = {"gat": dram["x1"], "spread": dram["feat"], "mix": dram["out"]}[kind]
    srow_d = dram["s_row_gat"] if gat else dram["s_row_spread"]

    def rows(ap, i):
        return ap[bass.ds(i * CHUNK, CHUNK), :].rearrange("(b p) f -> p b f", p=P)

    def row_chunk(i):
        return srow_d[:, bass.ds(i * CHUNK, CHUNK)].broadcast_to([P, CHUNK])

    with Arena(nc, kind) as a:
        G = [a.sb("G1", [P, TILES, width], BF16), a.sb("G2", [P, TILES, width2], F16 if low else BF16)]
        m1 = a.sb("m1", [P, RING, GROUP, CHUNK], U8)
        m2 = a.sb("m2", [P, RING, GROUP, CHUNK], U8)
        s_now = a.sb("s_now", [P, CHUNK], F32)
        s_next = a.sb("s_next", [P, CHUNK], F32)
        R = a.sb("R", [P, BLOCKS, width], F32)
        gw = GROUP * pw
        xt_flat = a.sb("xt", [P, max(BLOCKS * FEAT, gw)], F32)
        xt = xt_flat[:, 0:BLOCKS * FEAT].rearrange("p (b f) -> p b f", b=BLOCKS)
        stats = a.sb("stats", [P, BLOCKS, 6], F32)
        mv = a.sb("mv", [P, BLOCKS, 2], F32)
        rstd = a.sb("rstd", [P, BLOCKS, 2], F32)
        half = a.sb("half", [P, BLOCKS], F32)
        mx = a.sb("mx", [P, 4], F32)
        small = a.sb("small", [P, 6, BLOCKS], F32)
        bank = [a.ps(f"bank{b}", [P, 512]) for b in range(2 * BLOCKS)]

        flat = R[:, :, :].rearrange("p b w -> p (b w)")
        more = xt_flat if gat else a.sb("more", [P, gw], F32)
        g32_sets = [[m.rearrange("p (t w) -> p t w", t=GROUP) for m in pair] for pair in
                    ((flat[:, 0:gw], flat[:, gw:2 * gw]), (flat[:, 2 * gw:3 * gw], more[:, 0:gw]))]
        parts = [G[k][:, :, 0:n * pw].rearrange("p t (c w) -> p t c w", c=n)
                 for k, n in ((0, PARTS), (1, 2 if low else PARTS))]

        if not gat:
            vt = [xt, a.sb("vt1", [P, GROUP, FEAT], F32)[:, :, :]]

        adj_part = [a.sem(f"adj_part{k}") for k in range(2)]
        adj_ready = a.sem("adj_ready")
        v_loaded = [a.sem(f"v_loaded{k}") for k in range(2)]
        v_used = a.sem("v_used")
        s_loaded = a.sem("s_loaded")
        s_first = a.sem("s_first")
        s_taken = a.sem("s_taken")
        mx_own = a.sem("mx_own")
        mx_all = a.sem("mx_all")
        args_ready = a.sem("args_ready")
        cols_ready = a.sem("cols_ready")
        g_scaled = a.sem("g_scaled")
        g_hi = a.sem("g_hi")
        g_rest = a.sem("g_rest")
        g_mid = a.sem("g_mid")
        signs_ready = a.sem("signs_ready")
        masks_ready = a.sem("masks_ready")
        masks_used = a.sem("masks_used")
        banks_done = a.sem("banks_done")
        m2_scaled = a.sem("m2_scaled")
        banks_free = a.sem("banks_free")
        res_loaded = a.sem("res_loaded")
        res_used = a.sem("res_used")
        post_done = a.sem("post_done")
        stored = a.sem("stored")
        var_ready = a.sem("var_ready")
        rstd_ready = a.sem("rstd_ready")
        half_ready = a.sem("half_ready")
        elu_arg = a.sem("elu_arg")
        elu_exp = a.sem("elu_exp")
        late_free = a.sem("late_free")
        late_loaded = a.sem("late_loaded")
        pe_passed = a.sem("pe_passed")
        if gat:
            in_loaded = a.sem("in_loaded")
            wa_done = a.sem("wa_done")
            wa_copied = a.sem("wa_copied")
            cols_done = a.sem("cols_done")
            row_done = a.sem("row_done")
            row_copied = a.sem("row_copied")
            row_stored = a.sem("row_stored")
            wh_done = a.sem("wh_done")
            wh_copied = a.sem("wh_copied")
            cols_copied = a.sem("cols_copied")
            ident0 = a.sem("ident0")
            ident_ready = a.sem("ident_ready")
            adj_first = [a.sem(f"adj_first{k}") for k in range(FIRST_PARTS)]
            adj_f32 = adj[:, :].bitcast(F32).rearrange("p (t n) -> p t n", t=TILES)
            spare = {c: adj_f32[:, :, c * P:(c + 1) * P] for c in range(STEPS)}
            xT, wh = spare[STEPS - 2], spare[STEPS - 1]
            W0, W0T, a0, wa = (spare[STEPS - 4][:, 0, :], spare[STEPS - 4][:, 1, :],
                               spare[STEPS - 4][:, 2, 0:2], spare[STEPS - 4][:, 2, 2:4])
            ident = spare[STEPS - 4][:, 3, :]
            row_sb = spare[STEPS - 3][0:TILES, 0, :]
        block = a.block()

        @block.gpsimd
        def _(pool):
            pool.memset(half[:, :], -0.5).then_inc(half_ready, 1)
            pool.wait_ge(half_ready, 1)
            if gat:
                pool.memset(ident, 0.0).then_inc(ident0, 1)
                pool.wait_ge(ident0, 1)
                pool.affine_select(out=ident, in_=ident, compare_op=ALU.not_equal, fill=1.0, base=0,
                                   pattern=[[-1, P]], channel_multiplier=1).then_inc(ident_ready, 1)

                def load_adj(c, tiles, arrived):
                    src = dram["adjT"][:, c * CHUNK:(c + 1) * CHUNK].rearrange("(t p) n -> p t n", p=P)
                    dst = adj_u8[:, tiles, c * CHUNK:(c + 1) * CHUNK].bitcast(F8)
                    pool.dma_start(dst, src[:, tiles, :]).then_inc(arrived, 16)

                def load_first(k):
                    n = TILES // FIRST_PARTS
                    load_adj(0, slice(k * n, (k + 1) * n), adj_first[k])

                def load_next(c):
                    if c == STEPS - 4:
                        pool.wait_ge(wh_done, GROUPS)
                        pool.wait_ge(row_done, 1)
                    if c == STEPS - 3:
                        pool.wait_ge(row_stored, 16)
                    if c == STEPS - 1:
                        pool.wait_ge(v_used, GROUPS)
                    load_adj(c, slice(0, TILES), adj_part[c % 2])

                def adj_arrived(c):
                    if c == 0:
                        for k in range(FIRST_PARTS):
                            pool.wait_ge(adj_first[k], 16)
                    else:
                        pool.wait_ge(adj_part[c % 2], 16 * ((c + 1) // 2))
                    pool.sem_inc(adj_ready, 1)

                pool.wait_ge(in_loaded, INPUT_LOADS * 16)
                load_first(0)
                load_first(1)
            if not mix:
                pool.wait_ge(mx_own, 1)
                pool.partition_all_reduce(mx[:, 1:2], mx[:, 0:1], P, bass.bass_isa.ReduceOp.max)\
                    .then_inc(mx_all, 1)
            if gat:
                for k in range(2, FIRST_PARTS):
                    load_first(k)
                load_next(1)

            def root(s):
                pool.wait_ge(var_ready, s + 1)
                pool.tensor_tensor(rstd[:, :, 1], rstd[:, :, 0], half[:, :], ALU.pow).then_inc(rstd_ready, 1)

            if gat:
                for c in range(STEPS):
                    adj_arrived(c)
                    if c + 2 < STEPS:
                        load_next(c + 2)
                    if c >= 2 and c % 2 == 0:
                        root((c - 2) // 2)
                with pool.Fori(3, STEPS) as s:
                    root(s)
            elif mix:
                with pool.Fori(0, STEPS) as s:
                    root(s)

        @block.sync
        def _(sp):
            if gat:
                sp.dma_start(W0T, dram["W0T"]).then_inc(in_loaded, 16)
                sp.dma_start(a0, dram["a0"]).then_inc(in_loaded, 16)
                sp.dma_start(W0, dram["W0"]).then_inc(in_loaded, 16)
                half_tiles = TILES // 2
                x_tiles = dram["xT"].rearrange("f (t n) -> f t n", t=TILES)
                for k in range(2):
                    here = slice(k * half_tiles, (k + 1) * half_tiles)
                    sp.dma_start(xT[:, here, :], x_tiles[:, here, :]).then_inc(in_loaded, 16)
                sp.wait_ge(row_copied, 1)
                sp.dma_start(srow_d.rearrange("o (t n) -> (o t) n", t=TILES), row_sb).then_inc(row_stored, 16)
                sp.wait_ge(row_stored, 16)
            sp.dma_start(s_now[:, :], row_chunk(0)).then_inc(s_first, 16)
            sp.dma_start(s_next[:, :], row_chunk(1)).then_inc(s_loaded, 16)
            for g in range(0 if gat else GROUPS):
                if g >= 2:
                    sp.wait_ge(v_used, g - 1)
                sp.dma_start(vt[g % 2], V_g[g]).then_inc(v_loaded[g % 2], 16)
            sp.wait_ge(v_used, GROUPS)

            def step(s, more):
                if more:
                    sp.wait_ge(s_taken, s + 1)
                    sp.dma_start(s_next[:, :], row_chunk(s + 2)).then_inc(s_loaded, 16)
                sp.wait_ge(res_used, s + 1)
                sp.dma_start(xt, rows(res_d, s)).then_inc(res_loaded, 16)
                if mix:
                    sp.wait_ge(late_free, s + 1)
                    sp.dma_start(R[:, :, FEAT:2 * FEAT], rows(dram["x3"], s)).then_inc(late_loaded, 16)
                    sp.dma_start(R[:, :, 2 * FEAT:3 * FEAT], rows(dram["h0"], s)).then_inc(late_loaded, 16)
                sp.wait_ge(post_done, s + 1)
                src = R[:, :, 2 * pw:2 * pw + FEAT]
                sp.dma_start(rows(out_d, s), src).then_inc(stored, 16)

            with sp.Fori(0, STEPS - 2) as s:
                step(s, True)
            with sp.Fori(STEPS - 2, STEPS) as s:
                step(s, False)
            sp.wait_ge(stored, 16 * (STEPS + 1))

        @block.tensor
        def _(pe):
            if gat:
                pe.wait_ge(in_loaded, INPUT_LOADS * 16)
                pe.matmul(bank[0][:, 0:2], W0T, a0, start=True, stop=True).then_inc(wa_done, 1)
                pe.wait_ge(wa_copied, 1)
                for t in range(TILES):
                    mm = pe.matmul(bank[1][:, 2 * t:2 * t + 2], xT[:, t, :], wa, start=True, stop=True)
                mm.then_inc(cols_done, 1)
                for g in range(GROUPS):
                    if g >= 4:
                        pe.wait_ge(wh_copied, g - 3)
                    for t in range(GROUP):
                        mm = pe.matmul(bank[2 + g % 4][:, t * FEAT:(t + 1) * FEAT],
                                       xT[:, GROUP * g + t, :], W0, start=True, stop=True)
                    mm.then_inc(wh_done, 1)
                    if g == 0:
                        pe.wait_ge(ident_ready, 1)
                        pe.wait_ge(cols_copied, 1)
                        pe.transpose(bank[6][0:TILES, 0:P], s1c[:, :], ident).then_inc(row_done, 1)
                pe.wait_ge(row_copied, 1)
                pe.wait_ge(wh_copied, GROUPS)
            with pe.Fori(0, STEPS) as s:
                for g in range(GROUPS):
                    pe.wait_ge(masks_ready, s * GROUPS + (g + 1))
                    pe.sem_inc(pe_passed, 1)
                    for b in range(BLOCKS):
                        if g == 0:
                            pe.wait_ge(banks_free, s * BLOCKS + (b + 1))
                            pe.sem_inc(pe_passed, 1)
                        for t in range(GROUP):
                            for k, m in enumerate((m1, m2)):
                                mask = m[:, g % RING, t, b * P:(b + 1) * P].bitcast(F8)
                                mm = pe.matmul(bank[2 * b + k][:, 0:(width, width2)[k]], mask,
                                               G[k][:, GROUP * g + t, :],
                                               start=(g == 0 and t == 0),
                                               stop=(g == GROUPS - 1 and t == GROUP - 1))
                        if g == GROUPS - 1:
                            mm.then_inc(banks_done, 1)
                    if g < GROUPS - 1:
                        mm.then_inc(masks_used, 1)

        @block.scalar
        def _(act):
            if gat:
                act.wait_ge(wa_done, 1)
                act.activation(wa, bank[0][:, 0:2], ACT.Copy).then_inc(wa_copied, 1)

                def keep_wh(g):
                    act.wait_ge(wh_done, g + 1)
                    act.activation(wh[:, GROUP * g:GROUP * (g + 1), :],
                                   bank[2 + g % 4][:, :].rearrange("p (t f) -> p t f", t=GROUP),
                                   ACT.Copy).then_inc(wh_copied, 1)

                keep_wh(0)
                act.wait_ge(row_done, 1)
                act.activation(row_sb, bank[6][0:TILES, 0:P], ACT.Copy).then_inc(row_copied, 1)
                for g in range(1, 4):
                    keep_wh(g)
            if not mix:
                act.wait_ge(args_ready, 1)
                act.activation(F1[:, :], s2c[:, :], ACT.Exp, bias=mx[:, 2:3])
                act.activation(F2[:, :], s2c[:, :], ACT.Exp, bias=mx[:, 3:4], scale=SLOPE)
                act.activation(alpha[:, :], alpha[:, :], ACT.Exp)
                act.activation(beta[:, :], beta[:, :], ACT.Exp).then_inc(cols_ready, 1)
            def sign(g, t):
                i = GROUP * g + t
                return act.activation(m2[:, g % RING, t, :].bitcast(I8), s_now[:, :], ACT.Sign,
                                      bias=s2c[:, i:i + 1])

            def high_parts(g):
                for k in range(2):
                    act.wait_ge(g_scaled, 2 * g + k + 1)
                    act.activation(parts[k][:, GROUP * g:GROUP * (g + 1), 0, :], g32_sets[g % 2][k], ACT.Copy)\
                       .then_inc(g_hi, 1)

            high_parts(0)
            for g in range(GROUPS):
                for k in range(2):
                    act.wait_ge(g_rest, 2 * g + k + 1)
                    act.activation(parts[k][:, GROUP * g:GROUP * (g + 1), 1, :], g32_sets[g % 2][k], ACT.Copy,
                                   scale=LOW if k == 1 and low else 1.0).then_inc(g_mid, 1)
                if g == 0:
                    act.wait_ge(s_first, 16)
                if g >= RING:
                    act.wait_ge(masks_used, g - RING + 1)
                for t in range(GROUP):
                    last = sign(g, t)
                last.then_inc(signs_ready, 1)
                if gat and g == 0:
                    for later in range(4, GROUPS):
                        keep_wh(later)
                if g < GROUPS - 1:
                    high_parts(g + 1)
            act.wait_ge(masks_ready, GROUPS)
            act.sem_inc(stored, 16)

            def signs(s, g):
                if g < RING:
                    if g + RING < GROUPS - 1:
                        act.wait_ge(masks_used, s * (GROUPS - 1) + (g + RING + 1))
                    else:
                        act.wait_ge(banks_done, s * BLOCKS + BLOCKS)
                else:
                    act.wait_ge(masks_used, s * (GROUPS - 1) + (GROUPS - 1 + g - RING + 1))
                for t in range(GROUP):
                    last = sign(g, t)
                last.then_inc(signs_ready, 1)

            def evacuate(s):
                act.wait_ge(stored, 16 * s + 16)
                for b in range(BLOCKS):
                    act.wait_ge(banks_done, s * BLOCKS + (b + 1))
                    here = slice(s * BLOCKS + b, s * BLOCKS + b + 1) if isinstance(s, int) \
                        else bass.ds(s * BLOCKS + b, 1)
                    if low:
                        act.activation(R[:, b, 0:pw], bank[2 * b + 1][:, 0:pw], ACT.Copy, scale=beta[:, here])
                        act.activation(R[:, b, pw:2 * pw], bank[2 * b + 1][:, pw:2 * pw], ACT.Copy,
                                       scale=beta_low[:, here])
                        act.activation(R[:, b, 2 * pw:3 * pw], bank[2 * b][:, 2 * pw:3 * pw], ACT.Copy,
                                       scale=alpha[:, here]).then_inc(m2_scaled, 1)
                    else:
                        act.activation(R[:, b, :], bank[2 * b + 1][:, 0:width], ACT.Copy,
                                       scale=beta[:, here]).then_inc(m2_scaled, 1)

            def elu(s):
                act.wait_ge(elu_arg, s + 1)
                act.activation(R[:, :, pw:pw + FEAT], R[:, :, pw:pw + FEAT], ACT.Exp).then_inc(elu_exp, 1)

            with act.Fori(0, STEPS - 1) as s:
                act.drain()
                act.wait_ge(s_loaded, 16 * s + 16)
                act.activation(s_now[:, :], s_next[:, :], ACT.Copy)
                act.drain().then_inc(s_taken, 1)
                for g in range(RING - 1):
                    signs(s, g)
                evacuate(s)
                signs(s, RING - 1)
                signs(s, RING)
                if gat:
                    elu(s)
                for g in range(RING + 1, GROUPS):
                    signs(s, g)
            evacuate(STEPS - 1)
            if gat:
                elu(STEPS - 1)

        @block.vector
        def _(dve):
            if gat:
                dve.wait_ge(cols_done, 1)
                cols = bank[1][:, 0:2 * TILES].rearrange("p (t c) -> p c t", c=2)
                dve.tensor_copy(s1c[:, :], cols[:, 0, :])
                dve.tensor_copy(s2c[:, :], cols[:, 1, :])
                dve.drain().then_inc(cols_copied, 1)
            if not mix:
                dve.tensor_reduce(mx[:, 0:1], s2c[:, :], AX_X, ALU.max).then_inc(mx_own, 1)
                dve.wait_ge(mx_all, 1)
                dve.tensor_scalar(mx[:, 2:3], mx[:, 1:2], -1.0, SHIFT, ALU.mult, ALU.add)
                dve.tensor_scalar(mx[:, 3:4], mx[:, 1:2], -SLOPE, None, ALU.mult)
                dve.tensor_scalar(beta[:, :], s1c[:, :], mx[:, 1:2], 1.0 - SLOPE, ALU.add, ALU.mult)
                dve.drain()
                dve.tensor_scalar(alpha[:, :], beta[:, :], 0.0, -SHIFT, ALU.min, ALU.add)
                dve.drain()
                dve.tensor_scalar(beta[:, :], beta[:, :], -1.0, 0.0, ALU.mult, ALU.min)
                dve.drain().then_inc(args_ready, 1)
                dve.wait_ge(cols_ready, 1)
                if low:
                    dve.tensor_scalar(F2[:, :], F2[:, :], LOW, None, ALU.mult)
                    dve.tensor_scalar(beta_low[:, :], beta[:, :], LOW ** -2, None, ALU.mult)
                    dve.drain()
                    dve.tensor_scalar(beta[:, :], beta[:, :], 1.0 / LOW, None, ALU.mult)
                    dve.drain()
            dve.sem_inc(banks_free, BLOCKS)
            if gat:
                for k in range(2):
                    dve.memset(G[k][:, :, width - 1:width], 1.0)
            F = (F1, F2)

            def make_masks(g, col):
                edges = adj_u32[:, GROUP * g:GROUP * (g + 1), bass.ds(col * QU, QU)]
                M1, M2 = (m[:, g % RING, :, :].bitcast(U32) for m in (m1, m2))
                dve.tensor_tensor(M2, M2, edges, ALU.bitwise_and)
                dve.drain()
                dve.tensor_tensor(M1, M2, edges, ALU.bitwise_xor).then_inc(masks_ready, 1)

            def scale_rows(g):
                here = slice(GROUP * g, GROUP * (g + 1))
                if gat:
                    dve.wait_ge(wh_copied, g + 1)
                    V = wh[:, here, :]
                else:
                    dve.wait_ge(v_loaded[g % 2], 16 * (g // 2 + 1))
                    V = vt[g % 2]
                for k in range(2):
                    f = F[k][:, here]
                    g32 = g32_sets[g % 2][k]
                    dve.tensor_tensor(g32[:, :, 0:FEAT], V, bcast_cols(f, FEAT), ALU.mult)
                    if pw > FEAT:
                        dve.tensor_copy(g32[:, :, FEAT], f)
                    if pw > FEAT + 1:
                        dve.scalar_tensor_tensor(g32[:, :, FEAT + 1], f, 1.0 / LOW if k == 1 else 1.0, f,
                                                 ALU.mult, ALU.mult)
                    dve.drain().then_inc(g_scaled, 1)
                dve.sem_inc(v_used, 1)

            scale_rows(0)
            for g in range(GROUPS):
                here = slice(GROUP * g, GROUP * (g + 1))
                g32 = g32_sets[g % 2]
                for k in range(2):
                    dve.wait_ge(g_hi, 2 * g + k + 1)
                    dve.tensor_tensor(g32[k], g32[k], parts[k][:, here, 0, :], ALU.subtract).then_inc(g_rest, 1)
                if g < GROUPS - 1:
                    scale_rows(g + 1)
                for k in range(1 if low else 2):
                    dve.wait_ge(g_mid, 2 * g + k + 1)
                    dve.tensor_tensor(parts[k][:, here, 2, :], g32[k], parts[k][:, here, 1, :], ALU.subtract)
                dve.wait_ge(signs_ready, g + 1)
                if gat:
                    dve.wait_ge(adj_first[g * FIRST_PARTS // GROUPS], 16)
                make_masks(g, 0)
            dve.sem_inc(res_used, 1)

            def masks(s, g):
                dve.wait_ge(signs_ready, s * GROUPS + (GROUPS + g + 1))
                make_masks(g, s + 1)

            def evacuate(s):
                for b in range(BLOCKS):
                    dve.wait_ge(m2_scaled, s * BLOCKS + (b + 1))
                    if gat:
                        for k in range(2):
                            dve.tensor_copy(small[:, k, b:b + 1], bank[2 * b + k][:, width - 1:width])
                    if spread:
                        dve.tensor_reduce(small[:, 0, b:b + 1], bank[2 * b][:, pw - 1:width:pw],
                                          AX_X, ALU.add)
                        dve.tensor_copy(small[:, 2, b:b + 1], bank[2 * b + 1][:, 2 * pw - 1:2 * pw])
                        dve.drain()
                        dve.scalar_tensor_tensor(small[:, 1, b:b + 1], bank[2 * b + 1][:, pw - 1:pw], LOW,
                                                 small[:, 2, b:b + 1], ALU.mult, ALU.add)
                    if not mix:
                        dve.drain()
                    n = width2
                    dve.scalar_tensor_tensor(R[:, b, 0:n], bank[2 * b][:, 0:n],
                                             alpha[:, bass.ds(s * BLOCKS + b, 1)], R[:, b, 0:n],
                                             ALU.mult, ALU.add).then_inc(banks_free, 1)
                dve.drain()

            def add_parts():
                n = FEAT if mix else FEAT + 1
                dve.tensor_tensor(R[:, :, pw:pw + n], R[:, :, pw:pw + n], R[:, :, 2 * pw:2 * pw + n], ALU.add)
                dve.drain()
                dve.tensor_tensor(R[:, :, 0:n], R[:, :, 0:n], R[:, :, pw:pw + n], ALU.add)
                dve.drain()

            A = R[:, :, 0:FEAT]
            B = R[:, :, pw:pw + FEAT]
            C = R[:, :, 2 * pw:2 * pw + FEAT]

            def finish_gat(s):
                mine = bass.ds(s * BLOCKS, BLOCKS)
                dve.tensor_tensor(kept["deg"][:, mine], small[:, 0, :], small[:, 1, :], ALU.add)
                add_parts()
                dve.reciprocal(small[:, 0, :], R[:, :, FEAT])
                dve.drain()
                dve.tensor_tensor(A, A, bcast_cols(small[:, 0, :], FEAT), ALU.mult)
                dve.drain()
                dve.tensor_scalar(B, A, 0.0, None, ALU.min).then_inc(elu_arg, 1)
                dve.wait_ge(res_loaded, 16 * s + 16)
                dve.scalar_tensor_tensor(C, A, 0.0, xt, ALU.max, ALU.add)
                dve.drain().then_inc(res_used, 1)
                dve.wait_ge(elu_exp, s + 1)
                dve.scalar_tensor_tensor(A, B, 1.0, C, ALU.subtract, ALU.add)
                dve.drain()
                norm_blocks(dve, A, C, stats, mv, var_ready, rstd_ready, s + 1, rstd)\
                    .then_inc(post_done, 1)

            def finish_spread(s):
                mine = bass.ds(s * BLOCKS, BLOCKS)
                q1, q2, u, v, rd, rs = (small[:, j, :] for j in range(6))
                add_parts()
                dve.reciprocal(rd, R[:, :, FEAT])
                dve.drain()
                dve.tensor_copy(rden[:, mine], rd)
                dve.tensor_tensor(u, rd, alpha[:, mine], ALU.mult)
                dve.tensor_tensor(v, rd, beta[:, mine], ALU.mult)
                dve.tensor_tensor(A, A, bcast_cols(rd, FEAT), ALU.mult)
                dve.drain()
                dve.tensor_tensor(q1, q1, u, ALU.mult)
                dve.tensor_tensor(q2, q2, v, ALU.mult)
                dve.drain()
                dve.tensor_tensor(q1, q1, u, ALU.mult)
                dve.tensor_tensor(q2, q2, v, ALU.mult)
                dve.drain()
                dve.tensor_tensor(rs, q1, q2, ALU.add)
                dve.drain()
                dve.tensor_scalar(rowsum[:, mine], rs, 0.5, None, ALU.mult)
                dve.tensor_scalar(u, rs, -0.5, coe[:, 1, 2:3], ALU.mult, ALU.add)
                dve.drain()
                dve.wait_ge(res_loaded, 16 * s + 16)
                dve.tensor_tensor(B, xt, bcast_cols(u, FEAT), ALU.mult)
                dve.drain().then_inc(res_used, 1)
                dve.tensor_tensor(A, A, B, ALU.add)
                dve.drain()
                dve.tensor_scalar(B, A, THRESH, 0.0, ALU.add, ALU.min)
                dve.tensor_scalar(C, A, THRESH, 0.0, ALU.subtract, ALU.max)
                dve.drain()
                dve.tensor_tensor(C, C, B, ALU.add).then_inc(post_done, 1)

            def finish_mix(s):
                mine = bass.ds(s * BLOCKS, BLOCKS)
                add_parts()
                dve.sem_inc(late_free, 1)
                dve.tensor_tensor(A, A, bcast_cols(rden[:, mine], FEAT), ALU.mult)
                dve.drain()
                dve.wait_ge(res_loaded, 16 * s + 16)
                feat = xt
                dve.scalar_tensor_tensor(feat, A, coe[:, 2, 3:4], feat, ALU.mult, ALU.add)
                dve.wait_ge(late_loaded, 32 * s + 32)
                dve.tensor_scalar(C, C, coe[:, 1, 0:1], None, ALU.mult)
                dve.drain()
                dve.scalar_tensor_tensor(C, feat, coe[:, 0, 0:1], C, ALU.mult, ALU.add)
                dve.drain()
                dve.tensor_tensor(feat, feat, bcast_cols(rowsum[:, mine], FEAT), ALU.mult)
                dve.scalar_tensor_tensor(C, C, coe[:, 1, 1:2], B, ALU.mult, ALU.add)
                dve.drain()
                dve.tensor_tensor(A, A, feat, ALU.add)
                dve.drain().then_inc(res_used, 1)
                dve.scalar_tensor_tensor(A, A, coe[:, 0, 1:2], C, ALU.mult, ALU.add)
                dve.drain()
                norm_blocks(dve, A, C, stats, mv, var_ready, rstd_ready, s + 1, rstd)\
                    .then_inc(post_done, 1)

            finish = {"gat": finish_gat, "spread": finish_spread, "mix": finish_mix}[kind]
            with dve.Fori(0, STEPS - 1) as s:
                if gat:
                    dve.wait_ge(adj_ready, s + 2)
                for g in range(RING - 1):
                    masks(s, g)
                evacuate(s)
                masks(s, RING - 1)
                finish(s)
                dve.drain()
                for g in range(RING, GROUPS):
                    masks(s, g)
            evacuate(STEPS - 1)
            finish(STEPS - 1)


def mamba_inputs_stage(nc, kept, dram):
    QU = CHUNK // 4
    SLOTS = 4
    SCALE = 1024.0
    TAPS = 4
    D = 2
    STATE = 16
    RANK = 8
    adj_u32 = kept["adj"][:, :].bitcast(U32).rearrange("p (t n) -> p t n", t=TILES)
    x1_g = dram["x1"].rearrange("(g t p) f -> g p t f", p=P, t=GROUP)

    with Arena(nc, "min") as a:
        Gx = a.sb("Gx", [P, TILES, 2, FEAT], F16)
        stage = a.sb("stage", [P, SLOTS, GROUP, QU], U32)
        stage8 = stage[:, :, :, :].bitcast(F8)
        ident = a.sb("ident", [P, P], F32)
        ones = a.sb("ones", [1, P], F32)
        gcn_w = a.sb("gcn_w", [P, FEAT], F32)
        gcn_b = a.sb("gcn_b", [1, FEAT], F32)
        w_in = a.sb("w_in", [P, 4 * P], F32)
        w_xp = a.sb("w_xp", [P, D, RANK + 2 * STATE], F32)
        w_dt = a.sb("w_dt", [2 * STATE + RANK, D * P], F32)
        cvec = a.sb("cvec", [P, 2 + D * (TAPS + 3)], F32)
        ln_g, ln_b = cvec[:, 0:1], cvec[:, 1:2]
        dvec = cvec[:, 2:].rearrange("p (d c) -> p d c", d=D)
        conv_w, conv_b, b_dt, d_half = (dvec[:, :, 0:TAPS], dvec[:, :, TAPS:TAPS + 1],
                                        dvec[:, :, TAPS + 1:TAPS + 2], dvec[:, :, TAPS + 2:TAPS + 3])
        ax = a.sb("ax", [P, CHUNK], F32)
        h = a.sb("h", [P, BLOCKS, FEAT], F32)
        hT = a.sb("hT", [P, CHUNK], F32)
        xc = a.sb("xc", [P, D, TAPS - 1 + CHUNK], F32)
        conv = a.sb("conv", [P, D, CHUNK], F32)
        tanh_c = a.sb("tanh_c", [P, D, CHUNK], F32)
        v = tanh_c
        u2 = a.sb("u2", [P, D, CHUNK], F32)
        ud = a.sb("ud", [P, D, CHUNK], F32)
        sz = a.sb("sz", [P, D, CHUNK], F32)
        xin = [room[:, k, :].rearrange("p (t f) -> p t f", t=GROUP)
               for room in (conv, u2, ud, sz) for k in range(D)]
        halves = a.sb("halves", [P, TILES], F32)
        D1 = a.sb("D1", [P, TILES], F32)
        dbc = a.sb("dbc", [2 * STATE + RANK, CHUNK], F32)
        bc_parts = a.sb("bc_parts", [2 * STATE, PARTS, CHUNK], BF16)
        na = a.sb("na", [P, D, CHUNK], F32)
        dt = a.sb("dt", [P, D, CHUNK], F32)
        du = a.sb("du", [P, D, CHUNK], F32)
        stats = a.sb("stats", [P, BLOCKS, 6], F32)
        mv = a.sb("mv", [P, BLOCKS, 2], F32)
        rstd = a.sb("rstd", [P, BLOCKS, 2], F32)
        half = a.sb("half", [P, BLOCKS], F32)
        ps_ax = a.ps("ax_ps", [P, 512])
        ps_h = a.ps("h_ps", [P, 512])
        ps_hT = a.ps("hT_ps", [P, 512])
        ps_xz = [a.ps(f"xz{m}", [P, 512]) for m in range(4)]
        ps_dbc = a.ps("dbc_ps", [P, 512])

        w_loaded = a.sem("w_loaded")
        x_loaded = [a.sem(f"x_loaded{k}") for k in range(GROUPS)]
        deg1 = a.sem("deg1")
        D_ready = a.sem("D_ready")
        x_hi = a.sem("x_hi")
        x_split = a.sem("x_split")
        adj_staged = [a.sem(f"adj_staged{k}") for k in range(SLOTS)]
        adj_used = a.sem("adj_used")
        gcn_done = a.sem("gcn_done")
        ax_ready = a.sem("ax_ready")
        h_done = a.sem("h_done")
        h_relu = a.sem("h_relu")
        var_ready = a.sem("var_ready")
        rstd_ready = a.sem("rstd_ready")
        h_norm = a.sem("h_norm")
        hT_done = a.sem("hT_done")
        hT_ready = a.sem("hT_ready")
        xz_done = a.sem("xz_done")
        xc_ready = a.sem("xc_ready")
        halo_ready = a.sem("halo_ready")
        tz_ready = a.sem("tz_ready")
        sz_ready = a.sem("sz_ready")
        conv_ready = a.sem("conv_ready")
        tanh_ready = a.sem("tanh_ready")
        u_ready = a.sem("u_ready")
        ud_ready = a.sem("ud_ready")
        dbc_done = a.sem("dbc_done")
        dbc_ready = a.sem("dbc_ready")
        bc_hi = a.sem("bc_hi")
        bc_rest = a.sem("bc_rest")
        bc_mid = a.sem("bc_mid")
        bc_split = a.sem("bc_split")
        dt_done = a.sem("dt_done")
        v_ready = a.sem("v_ready")
        na_ready = a.sem("na_ready")
        log_ready = a.sem("log_ready")
        du_ready = a.sem("du_ready")
        stored = {k: a.sem(f"stored_{k}") for k in ("sz", "ud", "bc", "dt", "du")}
        consts = a.sem("consts")
        ident0 = a.sem("ident0")
        w_scaled = a.sem("w_scaled")
        front_stored = a.sem("front_stored")
        tail_stored = a.sem("tail_stored")
        pool_passed = a.sem("pool_passed")
        pe_passed = a.sem("pe_passed")
        block = a.block()

        def store_to(name, c):
            return dram[name][:, :, bass.ds(c * CHUNK, CHUNK)].rearrange("d p n -> p d n")

        @block.sync
        def _(sp):
            for g in range(GROUPS):
                sp.dma_start(xin[g], x1_g[g]).then_inc(x_loaded[g], 16)
            for tile, name in ((gcn_w, "gcn_w"), (gcn_b, "gcn_b"), (w_in, "w_in"),
                               (w_dt[2 * STATE:, :], "w_dt")):
                sp.dma_start(tile[:, :], dram[name]).then_inc(w_loaded, 16)
            sp.dma_start(w_xp[:, :, :], dram["w_xp"].rearrange("(d p) c -> p d c", p=P)).then_inc(w_loaded, 16)
            sp.dma_start(cvec[:, :], dram["cvec"]).then_inc(w_loaded, 16)
            with sp.Fori(0, STEPS) as c:
                for g in range(GROUPS):
                    if g == SLOTS - 1:
                        sp.wait_ge(ax_ready, c + 1)
                    else:
                        sp.wait_ge(adj_used, c * (GROUPS - 1) + (g + GROUPS - SLOTS + (g < SLOTS)))
                    sp.dma_start(stage[:, g % SLOTS, :, :],
                                 adj_u32[:, GROUP * g:GROUP * (g + 1), bass.ds(c * QU, QU)])\
                        .then_inc(adj_staged[g % SLOTS], 16)

        @block.gpsimd
        def _(pool):
            pool.memset(half[:, :], -0.5).then_inc(consts, 1)
            pool.memset(ones[:, :], 1.0).then_inc(consts, 1)
            pool.memset(xc[:, :, :], 0.0).then_inc(consts, 1)
            pool.memset(ident[:, :], 0.0).then_inc(ident0, 1)
            pool.wait_ge(ident0, 1)
            pool.affine_select(out=ident[:, :], in_=ident[:, :], compare_op=ALU.not_equal, fill=1.0, base=0,
                               pattern=[[-1, P]], channel_multiplier=1).then_inc(consts, 1)
            pool.wait_ge(consts, 4)
            pool.memset(halves[:, :], -0.5).then_inc(ident0, 1)
            pool.wait_ge(ident0, 2)
            pool.wait_ge(deg1, 1)
            pool.tensor_tensor(kept["Dc"][:, :], D1[:, :], halves[:, :], ALU.pow).then_inc(D_ready, 1)
            pool.sem_inc(front_stored, 1)
            pool.sem_inc(tail_stored, 1)
            def chunk(c, first):
                pool.wait_ge(var_ready, c + 1)
                pool.tensor_tensor(rstd[:, :, 1], rstd[:, :, 0], half[:, :], ALU.pow).then_inc(rstd_ready, 1)
                if not first:
                    tail_out(c - 1)
                pool.wait_ge(sz_ready, c + 1)
                pool.sem_inc(pool_passed, 1)
                pool.dma_start(store_to("sz", c), sz[:, :, :]).then_inc(stored["sz"], 16)
                pool.wait_ge(ud_ready, c + 1)
                pool.sem_inc(pool_passed, 1)
                pool.dma_start(store_to("ud", c), ud[:, :, :]).then_inc(stored["ud"], 16)
                if not first:
                    tail_left(c - 1)
                for name in ("sz", "ud"):
                    pool.wait_ge(stored[name], 16 * c + 16)
                pool.sem_inc(front_stored, 1)

            def tail_out(c):
                pool.wait_ge(bc_split, c + 1)
                pool.sem_inc(pool_passed, 1)
                pool.dma_start(dram["bc_parts"][:, :, bass.ds(c * CHUNK, CHUNK)].rearrange("k r n -> r k n"),
                               bc_parts[:, :, :]).then_inc(stored["bc"], 16)
                pool.wait_ge(du_ready, c + 1)
                pool.sem_inc(pool_passed, 1)
                pool.dma_start(store_to("dt", c), dt[:, :, :]).then_inc(stored["dt"], 16)
                pool.dma_start(store_to("du", c), du[:, :, :]).then_inc(stored["du"], 16)

            def tail_left(c):
                for name in ("bc", "dt", "du"):
                    pool.wait_ge(stored[name], 16 * c + 16)
                pool.sem_inc(tail_stored, 1)

            chunk(0, True)
            with pool.Fori(0, STEPS - 1) as i:
                chunk(i + 1, False)
            tail_out(STEPS - 1)
            tail_left(STEPS - 1)

        @block.tensor
        def _(pe):
            pe.sem_inc(adj_used, GROUPS - 1)

            def gcn(c, g, first):
                pe.wait_ge(adj_staged[g % SLOTS], c * (16 * GROUPS // SLOTS) + 16 * (g // SLOTS + 1))
                if first:
                    pe.wait_ge(x_split, g + 1)
                if g == 0:
                    pe.wait_ge(ax_ready, c + 1)
                pe.sem_inc(pe_passed, 1)
                for t in range(GROUP):
                    i = GROUP * g + t
                    for k in range(2):
                        mm = pe.matmul(ps_ax[:, :], Gx[:, i, k, :], stage8[:, g % SLOTS, t, :],
                                       start=(i == 0 and k == 0), stop=(i == TILES - 1 and k == 1))
                    if t == GROUP - 1:
                        mm.then_inc(adj_used if g < GROUPS - 1 else gcn_done, 1)

            def hidden(c):
                pe.wait_ge(ax_ready, c + 2)
                for b in range(BLOCKS):
                    pe.matmul(ps_h[:, b * P:(b + 1) * P], ax[:, b * P:(b + 1) * P], gcn_w[:, :],
                              start=True, stop=False)
                    mm = pe.matmul(ps_h[:, b * P:(b + 1) * P], ones[:, :], gcn_b[:, :], start=False, stop=True)
                mm.then_inc(h_done, 1)

            def turn(c):
                pe.wait_ge(h_norm, c + 1)
                for b in range(BLOCKS):
                    mm = pe.transpose(ps_hT[:, b * P:(b + 1) * P], h[:, b, :], ident[:, :])
                mm.then_inc(hT_done, 1)

            def project(c):
                pe.wait_ge(hT_ready, c + 1)
                pe.wait_ge(v_ready, D * (c + 1))
                for m in range(4):
                    pe.matmul(ps_xz[m][:, :], w_in[:, m * P:(m + 1) * P], hT[:, :], start=True, stop=True)\
                        .then_inc(xz_done, 1)

            def low_rank(c):
                pe.wait_ge(u_ready, c + 1)
                for d in range(D):
                    mm = pe.matmul(ps_dbc[0:RANK + 2 * STATE, :], w_xp[:, d, :], u2[:, d, :],
                                   start=(d == 0), stop=(d == D - 1))
                mm.then_inc(dbc_done, 1)

            def steps_of_time(c):
                pe.wait_ge(dbc_ready, c + 1)
                for d in range(D):
                    pe.matmul(ps_xz[d][:, :], w_dt[2 * STATE:, d * P:(d + 1) * P], dbc[2 * STATE:, :],
                              start=True, stop=True).then_inc(dt_done, 1)

            for g in range(GROUPS):
                gcn(0, g, True)
            pe.wait_ge(w_loaded, 16 * 6)
            pe.wait_ge(consts, 4)
            pe.wait_ge(w_scaled, 1)
            with pe.Fori(0, STEPS - 1) as c:
                gcn(c + 1, 0, False)
                hidden(c)
                gcn(c + 1, 1, False)
                gcn(c + 1, 2, False)
                turn(c)
                gcn(c + 1, 3, False)
                project(c)
                gcn(c + 1, 4, False)
                gcn(c + 1, 5, False)
                gcn(c + 1, 6, False)
                low_rank(c)
                gcn(c + 1, 7, False)
                steps_of_time(c)
            for piece in (hidden, turn, project, low_rank, steps_of_time):
                piece(STEPS - 1)

        @block.scalar
        def _(act):
            act.sem_inc(ax_ready, 1)
            for g in range(GROUPS):
                act.wait_ge(x_loaded[g], 16)
                act.activation(Gx[:, GROUP * g:GROUP * (g + 1), 0, :], xin[g], ACT.Copy,
                               scale=SCALE).then_inc(x_hi, 1)
            act.sem_inc(v_ready, D)
            act.wait_ge(consts, 4)
            act.wait_ge(w_loaded, 16 * 6)

            def arguments(c):
                for d in range(D):
                    act.wait_ge(dt_done, D * c + d + 1)
                    act.activation(v[:, d, :], ps_xz[d][:, :], ACT.Identity, bias=b_dt[:, d, :])\
                        .then_inc(v_ready, 1)
                act.wait_ge(tail_stored, c + 1)
                act.activation(bc_parts[:, 0, :], dbc[0:2 * STATE, :], ACT.Copy).then_inc(bc_hi, 1)

            def softplus(c):
                act.wait_ge(bc_rest, c + 1)
                act.activation(bc_parts[:, 1, :], dbc[0:2 * STATE, :], ACT.Copy).then_inc(bc_mid, 1)
                act.wait_ge(na_ready, c + 1)
                act.activation(na[:, :, :], na[:, :, :], ACT.Exp)
                act.drain()
                act.activation(na[:, :, :], na[:, :, :], ACT.Ln, bias=1.0).then_inc(log_ready, 1)

            def chunk(c, first):
                act.wait_ge(gcn_done, c + 1)
                act.activation(ax[:, :], ps_ax[:, :], ACT.Copy, scale=1.0 / SCALE).then_inc(ax_ready, 1)
                if not first:
                    arguments(c - 1)
                act.wait_ge(h_done, c + 1)
                act.activation(h[:, :, :], ps_h[:, :].rearrange("p (b f) -> p b f", b=BLOCKS), ACT.Relu)\
                    .then_inc(h_relu, 1)
                if not first:
                    softplus(c - 1)
                act.wait_ge(halo_ready, c + 1)
                for d in range(D):
                    act.wait_ge(xz_done, 4 * c + d + 1)
                    act.activation(xc[:, d, TAPS - 1:], ps_xz[d][:, :], ACT.Copy).then_inc(xc_ready, 1)
                act.wait_ge(front_stored, c + 1)
                for d in range(D):
                    act.wait_ge(xz_done, 4 * c + D + d + 1)
                    act.activation(sz[:, d, :], ps_xz[D + d][:, :], ACT.Tanh, scale=0.5).then_inc(tz_ready, 1)
                act.wait_ge(conv_ready, c + 1)
                act.activation(tanh_c[:, :, :], conv[:, :, :], ACT.Tanh, scale=0.5).then_inc(tanh_ready, 1)
                act.wait_ge(dbc_done, c + 1)
                act.activation(dbc[:, :], ps_dbc[0:RANK + 2 * STATE, :], ACT.Copy).then_inc(dbc_ready, 1)

            chunk(0, True)
            with act.Fori(0, STEPS - 1) as i:
                chunk(i + 1, False)
            arguments(STEPS - 1)
            softplus(STEPS - 1)

        @block.vector
        def _(dve):
            dve.tensor_scalar(D1[:, :], kept["deg"][:, :], 1.0, None, ALU.add).then_inc(deg1, 1)
            for g in range(GROUPS):
                dve.wait_ge(x_hi, g + 1)
                here = slice(GROUP * g, GROUP * (g + 1))
                dve.scalar_tensor_tensor(Gx[:, here, 1, :], xin[g], SCALE, Gx[:, here, 0, :],
                                         ALU.mult, ALU.subtract).then_inc(x_split, 1)
            dve.wait_ge(w_loaded, 16 * 6)
            dve.wait_ge(consts, 4)
            dve.tensor_scalar(w_xp[:, :, :], w_xp[:, :, :], 0.5, None, ALU.mult)
            dve.tensor_scalar(d_half, d_half, 0.5, None, ALU.mult)
            dve.drain().then_inc(w_scaled, 1)
            dve.sem_inc(halo_ready, 1)

            def arguments(c):
                dve.wait_ge(bc_hi, c + 1)
                dve.tensor_tensor(dbc[0:2 * STATE, :], dbc[0:2 * STATE, :], bc_parts[:, 0, :], ALU.subtract)\
                    .then_inc(bc_rest, 1)
                dve.wait_ge(v_ready, D * (c + 2))
                dve.scalar_tensor_tensor(na[:, :, :], v[:, :, :], -1.0, v[:, :, :], ALU.mult, ALU.min)\
                    .then_inc(na_ready, 1)

            def low_parts(c):
                dve.wait_ge(bc_mid, c + 1)
                dve.tensor_tensor(bc_parts[:, 2, :], dbc[0:2 * STATE, :], bc_parts[:, 1, :], ALU.subtract)\
                    .then_inc(bc_split, 1)

            def softplus(c):
                dve.wait_ge(log_ready, c + 1)
                dve.wait_ge(tail_stored, c + 1)
                dve.scalar_tensor_tensor(dt[:, :, :], v[:, :, :], 0.0, na[:, :, :], ALU.max, ALU.add)
                dve.drain()
                dve.scalar_tensor_tensor(du[:, :, :], dt[:, :, :], 0.5, u2[:, :, :], ALU.mult, ALU.mult)\
                    .then_inc(du_ready, 1)

            def chunk(c, first):
                if not first:
                    arguments(c - 1)
                dve.wait_ge(h_relu, c + 1)
                norm_blocks(dve, h, h, stats, mv, var_ready, rstd_ready, c + 1, rstd).then_inc(h_norm, 1)
                if not first:
                    low_parts(c - 1)
                dve.wait_ge(hT_done, c + 1)
                dve.tensor_scalar(hT[:, :], ps_hT[:, :], ln_g, ln_b, ALU.mult, ALU.add).then_inc(hT_ready, 1)
                if not first:
                    softplus(c - 1)
                for d in range(D):
                    dve.wait_ge(xc_ready, D * c + d + 1)
                    dve.tensor_scalar(conv[:, d, :], xc[:, d, TAPS - 1:], conv_w[:, d, TAPS - 1:TAPS],
                                      conv_b[:, d, :], ALU.mult, ALU.add)
                for k in range(TAPS - 1):
                    dve.drain()
                    for d in range(D):
                        dve.scalar_tensor_tensor(conv[:, d, :], xc[:, d, k:k + CHUNK], conv_w[:, d, k:k + 1],
                                                 conv[:, d, :], ALU.mult, ALU.add)
                dve.drain().then_inc(conv_ready, 1)
                dve.tensor_copy(xc[:, :, 0:TAPS - 1], xc[:, :, CHUNK:CHUNK + TAPS - 1]).then_inc(halo_ready, 1)
                dve.wait_ge(tz_ready, D * (c + 1))
                for d in range(D):
                    last = dve.scalar_tensor_tensor(sz[:, d, :], sz[:, d, :], 1.0, ps_xz[D + d][:, :],
                                                    ALU.add, ALU.mult)
                last.then_inc(sz_ready, 1)
                dve.wait_ge(tanh_ready, c + 1)
                dve.scalar_tensor_tensor(u2[:, :, :], tanh_c[:, :, :], 1.0, conv[:, :, :], ALU.add, ALU.mult)
                dve.drain().then_inc(u_ready, 1)
                for d in range(D):
                    last = dve.tensor_scalar(ud[:, d, :], u2[:, d, :], d_half[:, d, :], None, ALU.mult)
                last.then_inc(ud_ready, 1)

            chunk(0, True)
            with dve.Fori(0, STEPS - 1) as i:
                chunk(i + 1, False)
            arguments(STEPS - 1)
            low_parts(STEPS - 1)
            softplus(STEPS - 1)


def mamba_scan_stage(nc, kept, dram):
    D = 2
    STATE = 16
    ROWS = 2 * STATE
    XRING = 4
    CRING = 4
    LAG = 2

    with Arena(nc, "scan") as a:
        A = a.sb("A", [P, D, STATE], F32)
        w_out = a.sb("w_out", [P, D, FEAT], F32)
        ident = a.sb("ident", [P, P], F32)
        pick = a.sb("pick", [PARTS * ROWS, ROWS], BF16)
        half = a.sb("half", [P, BLOCKS], F32)
        state = a.sb("state", [P, STATE, D], F32)
        dt = [a.sb(f"dt{k}", [P, D, CHUNK], F32) for k in range(2)]
        du = [a.sb(f"du{k}", [P, D, CHUNK], F32) for k in range(2)]
        ud = [a.sb(f"ud{k}", [P, D, CHUNK], F32) for k in range(2)]
        sz = [a.sb(f"sz{k}", [P, D, CHUNK], F32) for k in range(2)]
        bc = [a.sb(f"bc{k}", [PARTS * ROWS, CHUNK], BF16) for k in range(2)]
        dA = [a.sb(f"dA{k}", [P, D, CHUNK], F32) for k in range(2)]
        C_sb = [a.sb(f"C_sb{k}", [P, CHUNK], F32) for k in range(CRING)]
        X = [a.sb(f"X{k}", [P, D, CHUNK], F32) for k in range(XRING)]
        yv = a.sb("yv", [P, D, CHUNK], F32)
        xt = a.sb("xt", [P, BLOCKS, FEAT], F32)
        stats = a.sb("stats", [P, BLOCKS, 6], F32)
        mv = a.sb("mv", [P, BLOCKS, 2], F32)
        rstd = a.sb("rstd", [P, BLOCKS, 2], F32)
        B = [a.ps(f"B{k}", [P, CHUNK]) for k in range(2)]
        C = [a.ps(f"C{k}", [P, CHUNK]) for k in range(2)]
        ps_y = a.ps("y", [P, D, CHUNK])
        ps_o = a.ps("o", [P, 512])

        w_loaded = a.sem("w_loaded")
        w_ready = a.sem("w_ready")
        A_exp = a.sem("A_exp")
        consts = a.sem("consts")
        zeros = a.sem("zeros")
        in_loaded = [a.sem(f"in_loaded{k}") for k in range(2)]
        bc_spread = a.sem("bc_spread")
        B_used = a.sem("B_used")
        dA_ready = a.sem("dA_ready")
        C_ready = a.sem("C_ready")
        h_ready = a.sem("h_ready")
        hC_ready = a.sem("hC_ready")
        X_used = a.sem("X_used")
        y_ready = a.sem("y_ready")
        o_done = a.sem("o_done")
        x_loaded = a.sem("x_loaded")
        var_ready = a.sem("var_ready")
        rstd_ready = a.sem("rstd_ready")
        x2_ready = a.sem("x2_ready")
        x2_stored = a.sem("x2_stored")
        block = a.block()

        INPUTS = 5

        def chunk_loop(eng, body):
            body(0, 0, first=True)
            with eng.Fori(0, STEPS // 2 - 1) as i:
                body(i * 2 + 1, 1, first=False)
                body(i * 2 + 2, 0, first=False)
            body(STEPS - 1, 1, first=False)

        def chunk_loads(c, parity):
            return 8 * INPUTS * c + 8 * INPUTS * (2 - parity)

        def is_last(c):
            return isinstance(c, int) and c == STEPS - 1

        def nodes(c):
            return slice(c * CHUNK, (c + 1) * CHUNK) if isinstance(c, int) else bass.ds(c * CHUNK, CHUNK)

        def rows(name, c):
            return dram[name][nodes(c), :].rearrange("(b p) f -> p b f", p=P)

        def per_tile(row):
            return row.unsqueeze(1).broadcast_to([P, D, CHUNK])

        @block.sync
        def _(sp):
            sp.dma_start(A[:, :, :], dram["A_log"].rearrange("(d p) s -> p d s", p=P)).then_inc(w_loaded, 16)
            sp.dma_start(w_out[:, :, :], dram["w_out"].rearrange("(d p) f -> p d f", p=P)).then_inc(w_loaded, 16)

            def load_inputs(c, parity):
                sp.dma_start(bc[parity][:, :], dram["bc_parts"][:, :, nodes(c)].rearrange("k r n -> (k r) n"))\
                    .then_inc(in_loaded[parity], 16)
                for tile, name in ((du, "du"), (dt, "dt"), (ud, "ud"), (sz, "sz")):
                    sp.dma_start(tile[parity][:, :, :], dram[name][:, :, nodes(c)].rearrange("d p n -> p d n"))\
                        .then_inc(in_loaded[parity], 16)

            def finish(c):
                sp.wait_ge(x2_stored, 16 * c + 16)
                sp.dma_start(xt[:, :, :], rows("x1", c)).then_inc(x_loaded, 16)
                sp.wait_ge(x2_ready, c + 1)
                sp.dma_start(rows("x2", c), xt[:, :, :]).then_inc(x2_stored, 16)

            def body(c, parity, first):
                if first:
                    load_inputs(1, 1)
                    return
                sp.wait_ge(y_ready, c)
                if not is_last(c):
                    load_inputs(c + 1, 1 - parity)
                finish(c - 1)

            sp.sem_inc(x2_stored, 16)
            load_inputs(0, 0)
            chunk_loop(sp, body)
            finish(STEPS - 1)
            sp.wait_ge(x2_stored, 16 * (STEPS + 1))

        @block.gpsimd
        def _(pool):
            pool.memset(pick[:, :], 0.0).then_inc(zeros, 1)
            pool.memset(ident[:, :], 0.0).then_inc(zeros, 1)
            pool.wait_ge(zeros, 2)
            for k in range(PARTS):
                pool.affine_select(out=pick[:, :], in_=pick[:, :], compare_op=ALU.not_equal, fill=1.0,
                                   base=-ROWS * k, pattern=[[-1, ROWS]], channel_multiplier=1)\
                    .then_inc(zeros, 1)
                pool.wait_ge(zeros, 3 + k)
            pool.affine_select(out=ident[:, :], in_=ident[:, :], compare_op=ALU.not_equal, fill=1.0, base=0,
                               pattern=[[-1, P]], channel_multiplier=1).then_inc(consts, 1)
            pool.memset(half[:, :], -0.5).then_inc(consts, 1)
            pool.wait_ge(consts, 2)

            def root(c):
                pool.wait_ge(var_ready, c + 1)
                pool.tensor_tensor(rstd[:, :, 1], rstd[:, :, 0], half[:, :], ALU.pow).then_inc(rstd_ready, 1)

            def body(c, parity, first):
                for n in range(STATE):
                    pool.wait_ge(C_ready, c * STATE + (n + 1))
                    pool.wait_ge(h_ready, c * STATE + (n + 1))
                    x = X[n % XRING][:, :, :]
                    pool.tensor_tensor(x, x, per_tile(C_sb[n % CRING][:, :]), ALU.mult).then_inc(hC_ready, 1)
                    if n == 6 and not first:
                        root(c - 1)

            chunk_loop(pool, body)
            root(STEPS - 1)

        @block.scalar
        def _(act):
            act.wait_ge(w_loaded, 32)
            act.activation(A[:, :, :], A[:, :, :], ACT.Exp).then_inc(A_exp, 1)
            act.wait_ge(w_ready, 1)

            def body(c, parity, first):
                act.wait_ge(in_loaded[parity], chunk_loads(c, parity))
                for n in range(STATE):
                    if not (first and n < 2):
                        act.wait_ge(h_ready, c * STATE + (n - 1))
                    for d in range(D):
                        last = act.activation(dA[n % 2][:, d, :], dt[parity][:, d, :], ACT.Exp,
                                              scale=A[:, d, n:n + 1])
                    last.then_inc(dA_ready, 1)
                    act.wait_ge(bc_spread, c * STATE + (n + 1))
                    if not (first and n < CRING):
                        act.wait_ge(hC_ready, c * STATE + (n - CRING + 1))
                    act.activation(C_sb[n % CRING][:, :], C[n % 2][:, :], ACT.Copy).then_inc(C_ready, 1)

            chunk_loop(act, body)

        @block.tensor
        def _(pe):
            pe.wait_ge(consts, 2)
            pe.wait_ge(w_ready, 1)

            def picked(r):
                return pick[:, r:r + 1].broadcast_to([PARTS * ROWS, P])

            def spread(c, parity, n):
                if not (isinstance(c, int) and c == 0 and n < 2):
                    pe.wait_ge(B_used, c * STATE + (n - 1))
                    pe.wait_ge(C_ready, c * STATE + (n - 1))
                if n == 0:
                    pe.wait_ge(in_loaded[parity], chunk_loads(c, parity))
                pe.matmul(B[n % 2][:, :], picked(n), bc[parity][:, :], start=True, stop=True)
                pe.matmul(C[n % 2][:, :], picked(STATE + n), bc[parity][:, :], start=True, stop=True)\
                    .then_inc(bc_spread, 1)

            def add(c, n):
                pe.wait_ge(hC_ready, c * STATE + (n + 1))
                for d in range(D):
                    mm = pe.matmul(ps_y[:, d, :], ident[:, :], X[n % XRING][:, d, :],
                                   start=(n == 0), stop=(n == STATE - 1))
                mm.then_inc(X_used, 1)

            def output(c):
                pe.wait_ge(y_ready, c + 1)
                for b in range(BLOCKS):
                    for d in range(D):
                        mm = pe.matmul(ps_o[:, b * P:(b + 1) * P], yv[:, d, b * P:(b + 1) * P],
                                       w_out[:, d, :], start=(d == 0), stop=(d == D - 1))
                mm.then_inc(o_done, 1)

            def body(c, parity, first):
                for n in range(STATE):
                    if n < STATE - 1:
                        spread(c, parity, n + 1)
                    elif not is_last(c):
                        spread(c + 1, 1 - parity, 0)
                    if n == LAG and not first:
                        pe.wait_ge(y_ready, c)
                    if n >= LAG:
                        add(c, n - LAG)
                    elif not first:
                        add(c - 1, STATE + n - LAG)
                    if n == LAG + 1 and not first:
                        output(c - 1)

            spread(0, 0, 0)
            chunk_loop(pe, body)
            for n in range(STATE - LAG, STATE):
                add(STEPS - 1, n)
            output(STEPS - 1)

        @block.vector
        def _(dve):
            dve.wait_ge(A_exp, 1)
            dve.tensor_scalar(A[:, :, :], A[:, :, :], -1.0, None, ALU.mult)
            dve.tensor_scalar(w_out[:, :, :], w_out[:, :, :], 0.5, None, ALU.mult)
            dve.memset(state[:, :, :], 0.0)
            dve.drain().then_inc(w_ready, 1)
            dve.wait_ge(consts, 2)

            def drive(c, parity, n):
                if n == 0:
                    dve.wait_ge(in_loaded[parity], chunk_loads(c, parity))
                if not (isinstance(c, int) and c == 0 and n < XRING):
                    dve.wait_ge(X_used, c * STATE + (n - XRING + 1))
                dve.wait_ge(bc_spread, c * STATE + (n + 1))
                dve.tensor_tensor(X[n % XRING][:, :, :], du[parity][:, :, :], per_tile(B[n % 2][:, :]),
                                  ALU.mult).then_inc(B_used, 1)

            def y_readout(c, parity):
                dve.wait_ge(X_used, c * STATE + STATE)
                dve.tensor_tensor(yv[:, :, :], ud[parity][:, :, :], ps_y[:, :, :], ALU.add)
                dve.drain()
                dve.tensor_tensor(yv[:, :, :], yv[:, :, :], sz[parity][:, :, :], ALU.mult)\
                    .then_inc(y_ready, 1)

            def residual(c):
                dve.wait_ge(x_loaded, 16 * c + 16)
                dve.wait_ge(o_done, c + 1)
                dve.tensor_tensor(xt[:, :, :], xt[:, :, :],
                                  ps_o[:, :].rearrange("p (b f) -> p b f", b=BLOCKS), ALU.add)
                dve.drain()
                norm_moments(dve, xt, stats, mv, var_ready, rstd)

            def normalize(c):
                norm_apply(dve, xt, xt, mv, rstd_ready, c + 1, rstd).then_inc(x2_ready, 1)

            def body(c, parity, first):
                for n in range(STATE):
                    x = X[n % XRING]
                    dve.wait_ge(dA_ready, c * STATE + (n + 1))
                    for d in range(D):
                        dve.tensor_tensor_scan(x[:, d, :], dA[n % 2][:, d, :], x[:, d, :],
                                               state[:, n, d:d + 1], ALU.mult, ALU.add)
                    if not first and n == 2:
                        y_readout(c - 1, 1 - parity)
                    if n < STATE - 1:
                        drive(c, parity, n + 1)
                    elif not is_last(c):
                        drive(c + 1, 1 - parity, 0)
                    dve.drain()
                    dve.tensor_copy(state[:, n, :], x[:, :, CHUNK - 1]).then_inc(h_ready, 1)
                    if not first and n == 6:
                        residual(c - 1)
                    if not first and n == 9:
                        normalize(c - 1)

            drive(0, 0, 0)
            dve.drain()
            chunk_loop(dve, body)
            dve.drain()
            y_readout(STEPS - 1, 1)
            residual(STEPS - 1)
            normalize(STEPS - 1)


def gcn_stage(nc, kept, dram):
    QU = CHUNK // 4
    SLOTS = 4
    SCALE = 1024.0
    adj_u32 = kept["adj"][:, :].bitcast(U32).rearrange("p (t n) -> p t n", t=TILES)
    x2_g = dram["x2"].rearrange("(g t p) f -> g p t f", p=P, t=GROUP)
    s1c, s2c, coe, Dc = kept["s1c"], kept["s2c"], kept["coe"], kept["Dc"]

    with Arena(nc, "gcn") as a:
        Gx = a.sb("Gx", [P, TILES, 2, FEAT], F16)
        xin = [a.sb(f"xin{k}", [P, GROUP, FEAT], F32) for k in range(GROUPS)]
        stage = a.sb("stage", [P, SLOTS, GROUP, QU], U32)
        stage8 = stage[:, :, :, :].bitcast(F8)
        ident = a.sb("ident", [P, P], F32)
        W = a.sb("W", [P, FEAT], F32)
        a3 = a.sb("a3", [P, 2], F32)
        bias = a.sb("bias", [P, FEAT], F32)
        Ds = a.sb("Ds", [P, TILES], F32)
        halves = a.sb("halves", [P, TILES], F32)
        xn = a.sb("xn", [P, BLOCKS, FEAT], F32)
        xs = a.sb("xs", [P, BLOCKS, FEAT], F32)
        xt = a.sb("xt", [P, BLOCKS, FEAT], F32)
        y = a.sb("y", [P, BLOCKS, FEAT], F32)
        ax = a.sb("ax", [P, CHUNK], F32)
        x3T = a.sb("x3T", [P, CHUNK], F32)
        row = a.sb("row", [TILES, P], F32)
        stats = a.sb("stats", [P, BLOCKS, 6], F32)
        mv = a.sb("mv", [P, BLOCKS, 2], F32)
        rstd = a.sb("rstd", [P, BLOCKS, 2], F32)
        ps_ax = a.ps("ax_ps", [P, 512])
        ps_o = a.ps("o_ps", [P, 512])
        ps_T = a.ps("T_ps", [P, 512])
        ps_c = a.ps("c_ps", [P, 512])
        ps_r = a.ps("r_ps", [P, 512])

        w_loaded = a.sem("w_loaded")
        consts = a.sem("consts")
        ident0 = a.sem("ident0")
        x_loaded = [a.sem(f"x_loaded{k}") for k in range(GROUPS)]
        x_scaled = a.sem("x_scaled")
        x_hi = a.sem("x_hi")
        x_split = a.sem("x_split")
        adj_staged = [a.sem(f"adj_staged{k}") for k in range(SLOTS)]
        adj_used = a.sem("adj_used")
        next_loaded = a.sem("next_loaded")
        own_ready = a.sem("own_ready")
        gcn_done = a.sem("gcn_done")
        ax_ready = a.sem("ax_ready")
        o_done = a.sem("o_done")
        res_loaded = a.sem("res_loaded")
        res_used = a.sem("res_used")
        var_ready = a.sem("var_ready")
        rstd_ready = a.sem("rstd_ready")
        x3_ready = a.sem("x3_ready")
        x3_stored = a.sem("x3_stored")
        T_done = a.sem("T_done")
        T_ready = a.sem("T_ready")
        scores_done = a.sem("scores_done")
        cols_copied = a.sem("cols_copied")
        row_done = a.sem("row_done")
        row_ready = a.sem("row_ready")
        row_stored = a.sem("row_stored")
        temp_exp = a.sem("temp_exp")
        y_free = a.sem("y_free")
        pool_passed = a.sem("pool_passed")
        pe_passed = a.sem("pe_passed")
        block = a.block()

        def rows(name, c):
            here = slice(c * CHUNK, (c + 1) * CHUNK) if isinstance(c, int) else bass.ds(c * CHUNK, CHUNK)
            return dram[name][here, :].rearrange("(b p) f -> p b f", p=P)

        @block.sync
        def _(sp):
            for g in range(GROUPS):
                sp.dma_start(xin[g][:, :, :], x2_g[g]).then_inc(x_loaded[g], 16)
            sp.dma_start(W[:, :], dram["W2"]).then_inc(w_loaded, 16)
            sp.dma_start(a3[:, :], dram["a3"]).then_inc(w_loaded, 16)
            sp.dma_start(bias[:, :], dram["b2"].broadcast_to([P, FEAT])).then_inc(w_loaded, 16)
            sp.dma_start(coe[:, 0, :], dram["temp"].broadcast_to([P, 5])).then_inc(w_loaded, 16)
            with sp.Fori(0, STEPS) as c:
                for g in range(GROUPS):
                    if g == SLOTS - 1:
                        sp.wait_ge(ax_ready, c + 1)
                    else:
                        sp.wait_ge(adj_used, c * (GROUPS - 1) + (g + GROUPS - SLOTS + (g < SLOTS)))
                    sp.dma_start(stage[:, g % SLOTS, :, :],
                                 adj_u32[:, GROUP * g:GROUP * (g + 1), bass.ds(c * QU, QU)])\
                        .then_inc(adj_staged[g % SLOTS], 16)

        @block.gpsimd
        def _(pool):
            pool.memset(halves[:, :], -0.5).then_inc(consts, 1)
            pool.memset(ident[:, :], 0.0).then_inc(ident0, 1)
            pool.wait_ge(ident0, 1)
            pool.affine_select(out=ident[:, :], in_=ident[:, :], compare_op=ALU.not_equal, fill=1.0, base=0,
                               pattern=[[-1, P]], channel_multiplier=1).then_inc(consts, 1)
            pool.wait_ge(consts, 2)
            pool.dma_start(xn[:, :, :], rows("x2", 0)).then_inc(next_loaded, 16)

            def chunk(c, more):
                pool.wait_ge(res_used, c + 1)
                pool.sem_inc(pool_passed, 1)
                pool.dma_start(xt[:, :, :], rows("x2", c)).then_inc(res_loaded, 16)
                if more:
                    pool.wait_ge(own_ready, c + 1)
                    pool.sem_inc(pool_passed, 1)
                    pool.dma_start(xn[:, :, :], rows("x2", c + 1)).then_inc(next_loaded, 16)
                pool.wait_ge(var_ready, c + 1)
                pool.tensor_tensor(rstd[:, :, 1], rstd[:, :, 0], halves[:, 0:BLOCKS], ALU.pow)\
                    .then_inc(rstd_ready, 1)
                pool.wait_ge(x3_ready, c + 1)
                pool.sem_inc(pool_passed, 1)
                pool.dma_start(rows("x3", c), y[:, :, :]).then_inc(x3_stored, 16)
                pool.wait_ge(x3_stored, 16 * c + 16)
                pool.sem_inc(y_free, 1)

            with pool.Fori(0, STEPS - 1) as c:
                chunk(c, True)
            chunk(STEPS - 1, False)

        @block.tensor
        def _(pe):
            pe.sem_inc(adj_used, GROUPS - 1)

            def gcn(c, g, first):
                pe.wait_ge(adj_staged[g % SLOTS], c * (16 * GROUPS // SLOTS) + 16 * (g // SLOTS + 1))
                if first:
                    pe.wait_ge(x_split, g + 1)
                if g == 0:
                    pe.wait_ge(ax_ready, c + 1)
                pe.sem_inc(pe_passed, 1)
                for t in range(GROUP):
                    i = GROUP * g + t
                    for k in range(2):
                        mm = pe.matmul(ps_ax[:, :], Gx[:, i, k, :], stage8[:, g % SLOTS, t, :],
                                       start=(i == 0 and k == 0), stop=False)
                if g < GROUPS - 1:
                    mm.then_inc(adj_used, 1)
                else:
                    pe.wait_ge(own_ready, c + 1)
                    for b in range(BLOCKS):
                        mm = pe.matmul(ps_ax[:, b * P:(b + 1) * P], xs[:, b, :], ident[:, :],
                                       start=False, stop=(b == BLOCKS - 1))
                    mm.then_inc(gcn_done, 1)

            def weigh(c):
                pe.wait_ge(ax_ready, c + 2)
                for b in range(BLOCKS):
                    mm = pe.matmul(ps_o[:, b * P:(b + 1) * P], ax[:, b * P:(b + 1) * P], W[:, :],
                                   start=True, stop=True)
                mm.then_inc(o_done, 1)

            def turn(c):
                pe.wait_ge(x3_ready, c + 1)
                for b in range(BLOCKS):
                    mm = pe.transpose(ps_T[:, b * P:(b + 1) * P], y[:, b, :], ident[:, :])
                mm.then_inc(T_done, 1)

            def scores(c):
                pe.wait_ge(T_ready, c + 1)
                for b in range(BLOCKS):
                    mm = pe.matmul(ps_c[:, 2 * b:2 * b + 2], x3T[:, b * P:(b + 1) * P], a3[:, :],
                                   start=True, stop=True)
                mm.then_inc(scores_done, 1)

            pe.wait_ge(w_loaded, 64)
            pe.wait_ge(consts, 2)
            for g in range(GROUPS):
                gcn(0, g, True)
            with pe.Fori(0, STEPS - 1) as c:
                gcn(c + 1, 0, False)
                weigh(c)
                for g in range(1, 5):
                    gcn(c + 1, g, False)
                turn(c)
                gcn(c + 1, 5, False)
                scores(c)
                gcn(c + 1, 6, False)
                gcn(c + 1, 7, False)
            for piece in (weigh, turn, scores):
                piece(STEPS - 1)
            pe.wait_ge(cols_copied, STEPS)
            pe.transpose(ps_r[0:TILES, 0:P], s1c[:, :], ident[:, :]).then_inc(row_done, 1)

        @block.scalar
        def _(act):
            act.sem_inc(ax_ready, 1)
            for g in range(GROUPS):
                act.wait_ge(x_scaled, g + 1)
                act.activation(Gx[:, GROUP * g:GROUP * (g + 1), 0, :], xin[g][:, :, :], ACT.Copy,
                               scale=SCALE).then_inc(x_hi, 1)
            act.wait_ge(w_loaded, 64)
            act.activation(coe[:, 0, :], coe[:, 0, :], ACT.Exp, scale=-1.0).then_inc(temp_exp, 1)
            act.wait_ge(consts, 2)
            with act.Fori(0, STEPS) as c:
                act.wait_ge(gcn_done, c + 1)
                act.activation(ax[:, :], ps_ax[:, :], ACT.Copy, scale=1.0 / SCALE).then_inc(ax_ready, 1)
                act.wait_ge(T_done, c + 1)
                act.activation(x3T[:, :], ps_T[:, :], ACT.Copy).then_inc(T_ready, 1)
            act.wait_ge(row_done, 1)
            act.activation(row[:, :], ps_r[0:TILES, 0:P], ACT.Copy).then_inc(row_ready, 1)
            act.wait_ge(row_ready, 1)
            act.dma_start(dram["s_row_spread"].rearrange("o (t n) -> (o t) n", t=TILES), row[:, :])\
                .then_inc(row_stored, 16)
            act.wait_ge(row_stored, 16)

        @block.vector
        def _(dve):
            dve.tensor_scalar(Ds[:, :], Dc[:, :], SCALE, None, ALU.mult)
            for g in range(GROUPS):
                here = slice(GROUP * g, GROUP * (g + 1))
                x = xin[g][:, :, :]
                dve.wait_ge(x_loaded[g], 16)
                dve.tensor_tensor(x, x, bcast_cols(Dc[:, here], FEAT), ALU.mult).then_inc(x_scaled, 1)
                dve.wait_ge(x_hi, g + 1)
                dve.scalar_tensor_tensor(Gx[:, here, 1, :], x, SCALE, Gx[:, here, 0, :],
                                         ALU.mult, ALU.subtract).then_inc(x_split, 1)
            dve.wait_ge(temp_exp, 1)
            dve.tensor_scalar(coe[:, 1, :], coe[:, 0, :], 1.0, None, ALU.add)
            dve.drain()
            dve.reciprocal(coe[:, 0, :], coe[:, 1, :])
            dve.drain()
            dve.tensor_scalar(coe[:, 1, :], coe[:, 0, :], -1.0, 1.0, ALU.mult, ALU.add)
            dve.tensor_scalar(coe[:, 2, :], coe[:, 0, :], -1.0, None, ALU.mult)

            def own_rows(c):
                dve.wait_ge(next_loaded, 16 * c + 16)
                dve.tensor_tensor(xs[:, :, :], xn[:, :, :], bcast_cols(Ds[:, blocks_of(c)], FEAT), ALU.mult)\
                    .then_inc(own_ready, 1)

            def blocks_of(c):
                return slice(BLOCKS * c, BLOCKS * (c + 1)) if isinstance(c, int) else bass.ds(c * BLOCKS, BLOCKS)

            def finish(c):
                dve.wait_ge(o_done, c + 1)
                dve.wait_ge(y_free, c + 1)
                for b in range(BLOCKS):
                    at = slice(BLOCKS * c + b, BLOCKS * c + b + 1) if isinstance(c, int) \
                        else bass.ds(c * BLOCKS + b, 1)
                    dve.scalar_tensor_tensor(y[:, b, :], ps_o[:, b * P:(b + 1) * P], Dc[:, at], bias[:, :],
                                             ALU.mult, ALU.add)
                dve.drain()
                dve.wait_ge(res_loaded, 16 * c + 16)
                dve.scalar_tensor_tensor(y[:, :, :], y[:, :, :], 0.0, xt[:, :, :], ALU.max, ALU.add)
                dve.drain().then_inc(res_used, 1)
                norm_blocks(dve, y, y, stats, mv, var_ready, rstd_ready, c + 1, rstd).then_inc(x3_ready, 1)
                dve.wait_ge(scores_done, c + 1)
                cols = ps_c[:, 0:2 * BLOCKS].rearrange("p (b c) -> p c b", c=2)
                dve.tensor_copy(s1c[:, blocks_of(c)], cols[:, 0, :])
                dve.tensor_copy(s2c[:, blocks_of(c)], cols[:, 1, :])
                dve.drain().then_inc(cols_copied, 1)

            dve.sem_inc(y_free, 1)
            dve.sem_inc(res_used, 1)
            own_rows(0)
            with dve.Fori(0, STEPS - 1) as c:
                dve.wait_ge(gcn_done, c + 1)
                own_rows(c + 1)
                finish(c)
            finish(STEPS - 1)


def build_program(nc, dram, stages=("gat", "mamba", "gcn", "spread", "mix")):
    with Arena(nc, "kept") as a:
        kept = {"adj": a.sb("adj", [P, TILES * N], U8)}
        for name in ("s1c", "s2c", "F1", "F2", "alpha", "beta", "beta_low", "deg", "Dc", "rden", "rowsum"):
            kept[name] = a.sb(name, [P, TILES], F32)
        kept["coe"] = a.sb("coe", [P, 3, 5], F32)
        for stage in stages:
            if stage in ("gat", "spread", "mix"):
                attention_pass(nc, stage, kept, dram)
            elif stage == "mamba":
                mamba_inputs_stage(nc, kept, dram)
                mamba_scan_stage(nc, kept, dram)
            else:
                gcn_stage(nc, kept, dram)


def kernel(**inputs):
    import numpy as _np
    import concourse.bacc as _bacc
    from concourse.bass_utils import run_bass_kernel_spmd as _run

    i = {k: _np.asarray(v) for k, v in inputs.items()}
    given = {
        "x": i["x"], "xT": i["x"].T, "adjT": i["adj"].T,
        "W0": i["L0_gnn_W"], "W0T": i["L0_gnn_W"].T, "a0": i["L0_gnn_a"].reshape(2, FEAT).T,
        "h0": i["L3_gnn_h0"],
        "W2": i["L2_gnn_W"], "b2": i["L2_gnn_b"].reshape(1, FEAT),
        "a3": i["L3_gnn_a"].reshape(2, FEAT).T, "temp": i["L3_gnn_temp"].reshape(1, 5),
        "gcn_w": i["L1_gnn_gcn_w"], "gcn_b": i["L1_gnn_gcn_b"].reshape(1, FEAT),
        "w_in": i["L1_gnn_w_in"],
        "w_xp": _np.concatenate([i["L1_gnn_w_xp"][:, 8:], i["L1_gnn_w_xp"][:, :8]], 1), "w_dt": i["L1_gnn_w_dt"],
        "A_log": i["L1_gnn_A_log"], "w_out": i["L1_gnn_w_out"],
        "cvec": _np.concatenate([i["L1_gnn_ln_g"][:, None], i["L1_gnn_ln_b"][:, None],
                                 _np.concatenate([i["L1_gnn_conv_w"], i["L1_gnn_conv_b"][:, None],
                                                  i["L1_gnn_b_dt"][:, None], i["L1_gnn_D_skip"][:, None]], 1)
                                 .reshape(2, P, 7).transpose(1, 0, 2).reshape(P, 14)], 1),
    }
    nc = _bacc.Bacc("TRN2", target_bir_lowering=False, num_devices=1)
    arrays, dram = {}, {}
    for name, v in given.items():
        v = _np.ascontiguousarray(v)
        arrays[f"in_{name}"] = v
        dram[name] = nc.dram_tensor(f"in_{name}", v.shape, mybir.dt.from_np(v.dtype), kind="ExternalInput").ap()
    for name, shape in (("x1", [N, FEAT]), ("x2", [N, FEAT]), ("x3", [N, FEAT]),
                        ("feat", [N, FEAT]), ("s_row_gat", [1, N]), ("s_row_spread", [1, N])):
        dram[name] = nc.dram_tensor(f"scratch_{name}", shape, F32, kind="Internal").ap()
    for name in ("dt", "du", "ud", "sz"):
        dram[name] = nc.dram_tensor(f"scratch_{name}", [2, P, N], F32, kind="Internal").ap()
    dram["bc_parts"] = nc.dram_tensor("scratch_bc_parts", [PARTS, 32, N], BF16, kind="Internal").ap()
    dram["out"] = nc.dram_tensor("out_x", [N, FEAT], F32, kind="ExternalOutput").ap()
    build_program(nc, dram, STAGES)
    r = _run(nc, [arrays], core_ids=[0])
    return r.results[0]["out_x"]


STAGES = ("gat", "mamba", "gcn", "spread", "mix")
```

```python
from contextlib import ExitStack

import concourse.bass as bass
from concourse import mybir

P = 128
ALU = mybir.AluOpType
ACT = mybir.ActivationFunctionType
AX_X = mybir.AxisListType.X
AX_XY = mybir.AxisListType.XY
F32 = mybir.dt.float32
F16 = mybir.dt.float16
BF16 = mybir.dt.bfloat16
F8 = mybir.dt.float8e4
U8 = mybir.dt.uint8
I8 = mybir.dt.int8
U32 = mybir.dt.uint32

N = 4096
FEAT = 128
TILES = N // P
CHUNK = 512
BLOCKS = CHUNK // P
STEPS = N // CHUNK
GROUP = 4
GROUPS = TILES // GROUP
RING = 4
FIRST_PARTS = 4
INPUT_LOADS = 5
AHEAD = 2
PARTS = 3
LOW = 2048.0
TOP = 32768.0
ONE_F8 = 0x38
SLOPE = 0.2
NEAR = 15.0
SHIFT = 30.0
EPS = 1e-5
THRESH = 1e-6


def bcast_cols(col, n):
    return col.unsqueeze(2).broadcast_to([col.shape[0], col.shape[1], n])


class Arena:

    def __init__(self, nc, stage):
        self.nc, self.stage, self.sems, self.ctx = nc, stage, [], ExitStack()

    def __enter__(self):
        return self

    def __exit__(self, *failed):
        self.ctx.close()
        if failed[0] is None and self.sems:
            self.nc.clear_and_free_semaphores(self.sems)
            self.nc.all_engine_barrier()

    def sb(self, name, shape, dt):
        return self.ctx.enter_context(self.nc.sbuf_tensor(f"{self.stage}_{name}", shape, dt))

    def ps(self, name, shape, dt=F32):
        return self.ctx.enter_context(self.nc.psum_tensor(f"{self.stage}_{name}", shape, dt))

    def sem(self, name):
        self.sems.append(self.nc.alloc_semaphore(name=f"{self.stage}_{name}"))
        return self.sems[-1]

    def block(self):
        return self.ctx.enter_context(self.nc.Block())


def norm_moments(dve, y, stats, mv, var_ready, rstd):
    for b in range(BLOCKS):
        dve.bn_stats(stats[:, b, :], y[:, b, :])
    dve.drain()
    for b in range(BLOCKS):
        dve.bn_aggr(mv[:, b, :], stats[:, b, :])
    dve.drain()
    dve.tensor_scalar(rstd[:, :, 0], mv[:, :, 1], EPS, None, ALU.add).then_inc(var_ready, 1)


def norm_apply(dve, y, out, mv, rstd_ready, rstd_wait, rstd):
    dve.wait_ge(rstd_ready, rstd_wait)
    for b in range(BLOCKS):
        last = dve.tensor_scalar(out[:, b, :], y[:, b, :], mv[:, b, 0:1], rstd[:, b, 1:2],
                                 ALU.subtract, ALU.mult)
    return last


def norm_blocks(dve, y, out, stats, mv, var_ready, rstd_ready, rstd_wait, rstd):
    norm_moments(dve, y, stats, mv, var_ready, rstd)
    return norm_apply(dve, y, out, mv, rstd_ready, rstd_wait, rstd)


def attention_pass(nc, kind, kept, dram):
    gat, spread, mix = (kind == k for k in ("gat", "spread", "mix"))
    pw = {"gat": FEAT + 1, "spread": FEAT + 2, "mix": FEAT}[kind]
    width = PARTS * pw + (1 if gat else 0)
    def part_width(k, wide):
        return (PARTS if wide and k == 0 else 2) * pw + (1 if gat else 0)

    width = part_width(0, True)
    adj = kept["adj"]
    adj_u8 = adj[:, :].rearrange("p (t n) -> p t n", t=TILES)
    adj_u32 = adj[:, :].bitcast(U32).rearrange("p (t n) -> p t n", t=TILES)
    QU = CHUNK // 4
    s1c, s2c, F1, F2 = kept["s1c"], kept["s2c"], kept["F1"], kept["F2"]
    alpha, beta = kept["alpha"], kept["beta"]
    alpha_low, beta_low = kept["alpha_low"], kept["beta_low"]
    wide_flag = kept["wide_flag"]
    rden, rowsum, coe = kept["rden"], kept["rowsum"], kept["coe"]
    if not gat:
        V_g = dram["x3" if spread else "feat"].rearrange("(g t p) f -> g p t f", p=P, t=GROUP)
    res_d = {"gat": dram["x"], "spread": dram["x3"], "mix": dram["feat"]}[kind]
    out_d = {"gat": dram["x1"], "spread": dram["feat"], "mix": dram["out"]}[kind]
    srow_d = dram["s_row_gat"] if gat else dram["s_row_spread"]

    def rows(ap, i):
        return ap[bass.ds(i * CHUNK, CHUNK), :].rearrange("(b p) f -> p b f", p=P)

    def row_chunk(i):
        return srow_d[:, bass.ds(i * CHUNK, CHUNK)].broadcast_to([P, CHUNK])

    with Arena(nc, kind) as a:
        G1_room = a.sb("G1", [P, TILES * width], BF16)
        G2_room = a.sb("G2", [P, TILES * part_width(1, True)], F16)

        def G(k, wide):
            n = part_width(k, wide)
            room = G2_room[:, :] if k == 1 else G1_room[:, :] if wide else G1_room[:, :].bitcast(F16)
            return room[:, 0:TILES * n].rearrange("p (t w) -> p t w", t=TILES)

        def split_parts(k, wide):
            n = PARTS if wide and k == 0 else 2
            return G(k, wide)[:, :, 0:n * pw].rearrange("p t (c w) -> p t c w", c=n)
        m1 = a.sb("m1", [P, RING, GROUP, CHUNK], U8)
        m2 = a.sb("m2", [P, RING, GROUP, CHUNK], U8)
        s_now = a.sb("s_now", [P, CHUNK], F32)
        s_next = a.sb("s_next", [P, CHUNK], F32)
        R = a.sb("R", [P, BLOCKS, width], F32)
        gw = GROUP * pw
        xt_flat = a.sb("xt", [P, max(BLOCKS * FEAT, gw)], F32)
        xt = xt_flat[:, 0:BLOCKS * FEAT].rearrange("p (b f) -> p b f", b=BLOCKS)
        stats = a.sb("stats", [P, BLOCKS, 6], F32)
        mv = a.sb("mv", [P, BLOCKS, 2], F32)
        rstd = a.sb("rstd", [P, BLOCKS, 2], F32)
        half = a.sb("half", [P, BLOCKS], F32)
        mx = a.sb("mx", [P, 4], F32)
        mx_g = a.sb("mx_g", [P, 4], F32)
        shifts = a.sb("shifts", [P, 2], F32)
        wide_f = a.sb("wide_f", [P, 2], F32)
        bound = a.sb("bound", [P, 2], F32)
        small = a.sb("small", [P, 6, BLOCKS], F32)
        pairs = a.sb("pairs", [P, 2, 2, BLOCKS], F32)
        bank = [a.ps(f"bank{b}", [P, 512]) for b in range(2 * BLOCKS)]

        flat = R[:, :, :].rearrange("p b w -> p (b w)")
        more = xt_flat if gat else a.sb("more", [P, gw], F32)
        g32_sets = [[m.rearrange("p (t w) -> p t w", t=GROUP) for m in pair] for pair in
                    ((flat[:, 0:gw], flat[:, gw:2 * gw]), (flat[:, 2 * gw:3 * gw], more[:, 0:gw]))]
        if not gat:
            vt = [xt, a.sb("vt1", [P, GROUP, FEAT], F32)[:, :, :]]
        if mix:
            x3_rows, h0_rows = vt[1], more[:, 0:gw].rearrange("p (b f) -> p b f", b=BLOCKS)

        adj_part = [a.sem(f"adj_part{k}") for k in range(2)]
        adj_ready = a.sem("adj_ready")
        v_loaded = [a.sem(f"v_loaded{k}") for k in range(2)]
        v_used = a.sem("v_used")
        s_loaded = a.sem("s_loaded")
        s_first = a.sem("s_first")
        s_taken = a.sem("s_taken")
        mx_own = a.sem("mx_own")
        mx_all = a.sem("mx_all")
        args_ready = a.sem("args_ready")
        flag_ready = a.sem("flag_ready")
        cols_ready = a.sem("cols_ready")
        g_scaled = a.sem("g_scaled")
        g_hi = a.sem("g_hi")
        g_rest = a.sem("g_rest")
        g_mid = a.sem("g_mid")
        signs_ready = a.sem("signs_ready")
        masks_ready = a.sem("masks_ready")
        masks_used = a.sem("masks_used")
        banks_done = a.sem("banks_done")
        m2_scaled = a.sem("m2_scaled")
        banks_free = a.sem("banks_free")
        res_loaded = a.sem("res_loaded")
        res_used = a.sem("res_used")
        post_done = a.sem("post_done")
        stored = a.sem("stored")
        var_ready = a.sem("var_ready")
        rstd_ready = a.sem("rstd_ready")
        half_ready = a.sem("half_ready")
        elu_arg = a.sem("elu_arg")
        elu_exp = a.sem("elu_exp")
        late_free = a.sem("late_free")
        late_loaded = a.sem("late_loaded")
        pe_passed = a.sem("pe_passed")
        if gat:
            in_loaded = a.sem("in_loaded")
            wa_done = a.sem("wa_done")
            wa_copied = a.sem("wa_copied")
            cols_done = a.sem("cols_done")
            row_done = a.sem("row_done")
            row_copied = a.sem("row_copied")
            row_stored = a.sem("row_stored")
            wh_done = a.sem("wh_done")
            wh_copied = a.sem("wh_copied")
            cols_copied = a.sem("cols_copied")
            ident0 = a.sem("ident0")
            ident_ready = a.sem("ident_ready")
            adj_first = [a.sem(f"adj_first{k}") for k in range(FIRST_PARTS)]
            adj_f32 = adj[:, :].bitcast(F32).rearrange("p (t n) -> p t n", t=TILES)
            spare = {c: adj_f32[:, :, c * P:(c + 1) * P] for c in range(STEPS)}
            xT, wh = spare[STEPS - 2], spare[STEPS - 1]
            W0, W0T, a0, wa = (spare[STEPS - 4][:, 0, :], spare[STEPS - 4][:, 1, :],
                               spare[STEPS - 4][:, 2, 0:2], spare[STEPS - 4][:, 2, 2:4])
            ident = kept["ident"][:, :]
            row_sb = spare[STEPS - 3][0:TILES, 0, :]

        def by_range(eng, main):
            if not mix:
                eng.wait_ge(flag_ready, 1)
            flag = eng.value_load(wide_flag[0:1, 0:1], min_val=0, max_val=1)
            with eng.If(flag < 1):
                main(False)
            with eng.If(flag >= 1):
                main(True)

        block = a.block()

        @block.gpsimd
        def _(pool):
            pool.memset(half[:, :], -0.5).then_inc(half_ready, 1)
            pool.wait_ge(half_ready, 1)
            if gat:
                pool.memset(ident, 0.0).then_inc(ident0, 1)
                pool.wait_ge(ident0, 1)
                pool.affine_select(out=ident, in_=ident, compare_op=ALU.not_equal, fill=1.0, base=0,
                                   pattern=[[-1, P]], channel_multiplier=1).then_inc(ident_ready, 1)

                def load_adj(c, tiles, arrived):
                    src = dram["adjT"][:, c * CHUNK:(c + 1) * CHUNK].rearrange("(t p) n -> p t n", p=P)
                    dst = adj_u8[:, tiles, c * CHUNK:(c + 1) * CHUNK].bitcast(F8)
                    pool.dma_start(dst, src[:, tiles, :]).then_inc(arrived, 16)

                def load_first(k):
                    n = TILES // FIRST_PARTS
                    load_adj(0, slice(k * n, (k + 1) * n), adj_first[k])

                def load_next(c):
                    if c == STEPS - 4:
                        pool.wait_ge(wh_done, GROUPS)
                        pool.wait_ge(row_done, 1)
                    if c == STEPS - 3:
                        pool.wait_ge(row_stored, 16)
                    if c == STEPS - 1:
                        pool.wait_ge(v_used, GROUPS)
                    load_adj(c, slice(0, TILES), adj_part[c % 2])

                def adj_arrived(c):
                    if c == 0:
                        for k in range(FIRST_PARTS):
                            pool.wait_ge(adj_first[k], 16)
                    else:
                        pool.wait_ge(adj_part[c % 2], 16 * ((c + 1) // 2))
                    pool.sem_inc(adj_ready, 1)

                pool.wait_ge(in_loaded, INPUT_LOADS * 16)
                load_first(0)
                load_first(1)
            if not mix:
                pool.wait_ge(mx_own, 1)
                pool.partition_all_reduce(mx_g[:, :], mx[:, :], P, bass.bass_isa.ReduceOp.max)\
                    .then_inc(mx_all, 1)
            if gat:
                for k in range(2, FIRST_PARTS):
                    load_first(k)
                load_next(1)

            def root(s):
                pool.wait_ge(var_ready, s + 1)
                pool.tensor_tensor(rstd[:, :, 1], rstd[:, :, 0], half[:, :], ALU.pow).then_inc(rstd_ready, 1)

            if gat:
                for c in range(STEPS):
                    adj_arrived(c)
                    if c + 2 < STEPS:
                        load_next(c + 2)
                    if c >= 2 and c % 2 == 0:
                        root((c - 2) // 2)
                with pool.Fori(3, STEPS) as s:
                    root(s)
            elif mix:
                with pool.Fori(0, STEPS) as s:
                    root(s)

        @block.sync
        def _(sp):
            if gat:
                sp.dma_start(W0T, dram["W0T"]).then_inc(in_loaded, 16)
                sp.dma_start(a0, dram["a0"]).then_inc(in_loaded, 16)
                sp.dma_start(W0, dram["W0"]).then_inc(in_loaded, 16)
                half_tiles = TILES // 2
                x_tiles = dram["xT"].rearrange("f (t n) -> f t n", t=TILES)
                for k in range(2):
                    here = slice(k * half_tiles, (k + 1) * half_tiles)
                    sp.dma_start(xT[:, here, :], x_tiles[:, here, :]).then_inc(in_loaded, 16)
                sp.wait_ge(row_copied, 1)
                sp.dma_start(srow_d.rearrange("o (t n) -> (o t) n", t=TILES), row_sb).then_inc(row_stored, 16)
                sp.wait_ge(row_stored, 16)
            sp.dma_start(s_now[:, :], row_chunk(0)).then_inc(s_first, 16)
            sp.dma_start(s_next[:, :], row_chunk(1)).then_inc(s_loaded, 16)
            for g in range(0 if gat else GROUPS):
                if g >= 2:
                    sp.wait_ge(v_used, g - 1)
                sp.dma_start(vt[g % 2], V_g[g]).then_inc(v_loaded[g % 2], 16)
            sp.wait_ge(v_used, GROUPS)

            def step(s, more):
                if more:
                    sp.wait_ge(s_taken, s + 1)
                    sp.dma_start(s_next[:, :], row_chunk(s + 2)).then_inc(s_loaded, 16)
                sp.wait_ge(res_used, s + 1)
                sp.dma_start(xt, rows(res_d, s)).then_inc(res_loaded, 16)
                if mix:
                    sp.wait_ge(late_free, s + 1)
                    sp.dma_start(x3_rows, rows(dram["x3"], s)).then_inc(late_loaded, 16)
                    sp.dma_start(h0_rows, rows(dram["h0"], s)).then_inc(late_loaded, 16)
                sp.wait_ge(post_done, s + 1)
                src = R[:, :, 2 * pw:2 * pw + FEAT]
                sp.dma_start(rows(out_d, s), src).then_inc(stored, 16)

            with sp.Fori(0, STEPS - 2) as s:
                step(s, True)
            with sp.Fori(STEPS - 2, STEPS) as s:
                step(s, False)
            sp.wait_ge(stored, 16 * (STEPS + 1))

        @block.tensor
        def _(pe):
            if gat:
                pe.wait_ge(in_loaded, INPUT_LOADS * 16)
                pe.matmul(bank[0][:, 0:2], W0T, a0, start=True, stop=True).then_inc(wa_done, 1)
                pe.wait_ge(wa_copied, 1)
                for t in range(TILES):
                    mm = pe.matmul(bank[1][:, 2 * t:2 * t + 2], xT[:, t, :], wa, start=True, stop=True)
                mm.then_inc(cols_done, 1)
                for g in range(GROUPS):
                    if g >= 4:
                        pe.wait_ge(wh_copied, g - 3)
                    for t in range(GROUP):
                        mm = pe.matmul(bank[2 + g % 4][:, t * FEAT:(t + 1) * FEAT],
                                       xT[:, GROUP * g + t, :], W0, start=True, stop=True)
                    mm.then_inc(wh_done, 1)
                    if g == 0:
                        pe.wait_ge(ident_ready, 1)
                        pe.wait_ge(cols_copied, 1)
                        pe.transpose(bank[6][0:TILES, 0:P], s1c[:, :], ident).then_inc(row_done, 1)
                pe.wait_ge(row_copied, 1)
                pe.wait_ge(wh_copied, GROUPS)
            def main(wide):
                Gw = [G(k, wide) for k in range(2)]
                with pe.Fori(0, STEPS) as s:
                    for g in range(GROUPS):
                        pe.wait_ge(masks_ready, s * GROUPS + (g + 1))
                        pe.sem_inc(pe_passed, 1)
                        for b in range(BLOCKS):
                            if g == 0:
                                pe.wait_ge(banks_free, s * BLOCKS + (b + 1))
                                pe.sem_inc(pe_passed, 1)
                            for t in range(GROUP):
                                for k, m in enumerate((m1, m2)):
                                    mask = m[:, g % RING, t, b * P:(b + 1) * P].bitcast(F8)
                                    mm = pe.matmul(bank[2 * b + k][:, 0:part_width(k, wide)], mask,
                                                   Gw[k][:, GROUP * g + t, :],
                                                   start=(g == 0 and t == 0),
                                                   stop=(g == GROUPS - 1 and t == GROUP - 1))
                            if g == GROUPS - 1:
                                mm.then_inc(banks_done, 1)
                        if g < GROUPS - 1:
                            mm.then_inc(masks_used, 1)

            by_range(pe, main)

        @block.scalar
        def _(act):
            if gat:
                act.wait_ge(wa_done, 1)
                act.activation(wa, bank[0][:, 0:2], ACT.Copy).then_inc(wa_copied, 1)

                def keep_wh(g):
                    act.wait_ge(wh_done, g + 1)
                    act.activation(wh[:, GROUP * g:GROUP * (g + 1), :],
                                   bank[2 + g % 4][:, :].rearrange("p (t f) -> p t f", t=GROUP),
                                   ACT.Copy).then_inc(wh_copied, 1)

                keep_wh(0)
                act.wait_ge(row_done, 1)
                act.activation(row_sb, bank[6][0:TILES, 0:P], ACT.Copy).then_inc(row_copied, 1)
                for g in range(1, 4):
                    keep_wh(g)
            if not mix:
                act.wait_ge(args_ready, 1)
                act.activation(F1[:, :], s2c[:, :], ACT.Exp, bias=shifts[:, 0:1])
                act.activation(F2[:, :], s2c[:, :], ACT.Exp, bias=shifts[:, 1:2], scale=SLOPE)
                act.activation(alpha[:, :], alpha[:, :], ACT.Exp)
                act.activation(beta[:, :], beta[:, :], ACT.Exp).then_inc(cols_ready, 1)

            def sign(g, t):
                i = GROUP * g + t
                return act.activation(m2[:, g % RING, t, :].bitcast(I8), s_now[:, :], ACT.Sign,
                                      bias=s2c[:, i:i + 1])

            def main(wide):
                parts = [split_parts(k, wide) for k in range(2)]

                def high_parts(g):
                    here = slice(GROUP * g, GROUP * (g + 1))
                    for k in range(2):
                        act.wait_ge(g_scaled, 2 * g + k + 1)
                        act.activation(parts[k][:, here, 0, :], g32_sets[g % 2][k], ACT.Copy,
                                       scale=1.0 if wide and k == 0 else 1.0 / LOW).then_inc(g_hi, 1)

                high_parts(0)
                for g in range(GROUPS):
                    if wide:
                        act.wait_ge(g_rest, g + 1)
                        act.activation(parts[0][:, GROUP * g:GROUP * (g + 1), 1, :], g32_sets[g % 2][0],
                                       ACT.Copy).then_inc(g_mid, 1)
                    if g == 0:
                        act.wait_ge(s_first, 16)
                    if g >= RING:
                        act.wait_ge(masks_used, g - RING + 1)
                    for t in range(GROUP):
                        last = sign(g, t)
                    last.then_inc(signs_ready, 1)
                    if gat and g == 0:
                        for later in range(4, GROUPS):
                            keep_wh(later)
                    if g < GROUPS - 1:
                        high_parts(g + 1)
                act.wait_ge(masks_ready, GROUPS)
                act.sem_inc(stored, 16)

                def signs(s, g):
                    if g < RING:
                        if g + RING < GROUPS - 1:
                            act.wait_ge(masks_used, s * (GROUPS - 1) + (g + RING + 1))
                        else:
                            act.wait_ge(banks_done, s * BLOCKS + BLOCKS)
                    else:
                        act.wait_ge(masks_used, s * (GROUPS - 1) + (GROUPS - 1 + g - RING + 1))
                    for t in range(GROUP):
                        last = sign(g, t)
                    last.then_inc(signs_ready, 1)

                def evacuate(s):
                    act.wait_ge(stored, 16 * s + 16)
                    for b in range(BLOCKS):
                        act.wait_ge(banks_done, s * BLOCKS + (b + 1))
                        here = slice(s * BLOCKS + b, s * BLOCKS + b + 1) if isinstance(s, int) \
                            else bass.ds(s * BLOCKS + b, 1)
                        act.activation(R[:, b, 0:pw], bank[2 * b + 1][:, 0:pw], ACT.Copy, scale=beta[:, here])
                        last = act.activation(R[:, b, pw:2 * pw], bank[2 * b + 1][:, pw:2 * pw], ACT.Copy,
                                       scale=beta_low[:, here])
                        if wide:
                            last = act.activation(R[:, b, 2 * pw:3 * pw], bank[2 * b][:, 2 * pw:3 * pw],
                                                  ACT.Copy, scale=alpha[:, here])
                        last.then_inc(m2_scaled, 1)

                def elu(s):
                    act.wait_ge(elu_arg, s + 1)
                    act.activation(R[:, :, pw:pw + FEAT], R[:, :, pw:pw + FEAT], ACT.Exp).then_inc(elu_exp, 1)

                with act.Fori(0, STEPS - 1) as s:
                    act.drain()
                    act.wait_ge(s_loaded, 16 * s + 16)
                    act.activation(s_now[:, :], s_next[:, :], ACT.Copy)
                    act.drain().then_inc(s_taken, 1)
                    for g in range(AHEAD):
                        signs(s, g)
                    evacuate(s)
                    for g in range(AHEAD, RING + 1):
                        signs(s, g)
                    if gat:
                        elu(s)
                    for g in range(RING + 1, GROUPS):
                        signs(s, g)
                evacuate(STEPS - 1)
                if gat:
                    elu(STEPS - 1)

            by_range(act, main)

        @block.vector
        def _(dve):
            if spread:
                dve.memset(mx[:, 1:3], 0.0)
            if gat:
                dve.wait_ge(in_loaded, INPUT_LOADS * 16)
                dve.tensor_reduce(mx[:, 1:2], xT, AX_XY, ALU.max, apply_absolute_value=True)
                dve.tensor_reduce(mx[:, 2:3], W0T, AX_X, ALU.add, apply_absolute_value=True)
                dve.wait_ge(cols_done, 1)
                cols = bank[1][:, 0:2 * TILES].rearrange("p (t c) -> p c t", c=2)
                dve.tensor_copy(s1c[:, :], cols[:, 0, :])
                dve.tensor_copy(s2c[:, :], cols[:, 1, :])
                dve.drain().then_inc(cols_copied, 1)
            if not mix:
                dve.tensor_reduce(mx[:, 3:4], s1c[:, :], AX_X, ALU.max)
                dve.tensor_reduce(mx[:, 0:1], s2c[:, :], AX_X, ALU.max)
                dve.drain().then_inc(mx_own, 1)
                dve.wait_ge(mx_all, 1)
                dve.tensor_scalar(wide_f[:, 0:1], mx_g[:, 0:1], mx_g[:, 3:4], NEAR, ALU.add, ALU.is_gt)
                dve.tensor_scalar(shifts[:, 1:2], mx_g[:, 0:1], -SLOPE, None, ALU.mult)
                dve.drain()
                dve.tensor_scalar(wide_f[:, 1:2], wide_f[:, 0:1], SHIFT, None, ALU.mult)
                dve.tensor_copy(wide_flag[:, :], wide_f[:, 0:1])
                dve.drain().then_inc(flag_ready, 1)
                dve.tensor_scalar(shifts[:, 0:1], mx_g[:, 0:1], -1.0, wide_f[:, 1:2], ALU.mult, ALU.add)
                dve.tensor_scalar(beta[:, :], s1c[:, :], mx_g[:, 0:1], 1.0 - SLOPE, ALU.add, ALU.mult)
                dve.drain()
                dve.tensor_scalar(alpha[:, :], beta[:, :], 0.0, wide_f[:, 1:2], ALU.min, ALU.subtract)
                dve.drain()
                dve.tensor_scalar(beta[:, :], beta[:, :], -1.0, 0.0, ALU.mult, ALU.min)
                dve.drain().then_inc(args_ready, 1)
                if gat:
                    up, down = bound[:, 1:2], bound[:, 0:1]
                    dve.tensor_scalar(bound[:, 0:1], mx_g[:, 1:2], mx_g[:, 2:3], 1.0, ALU.mult, ALU.max)
                    dve.drain()
                    dve.reciprocal(bound[:, 1:2], bound[:, 0:1])
                    dve.drain()
                    dve.tensor_scalar(bound[:, 0:1], bound[:, 0:1], 1.0 / TOP, None, ALU.mult)
                    dve.tensor_scalar(bound[:, 1:2], bound[:, 1:2], TOP, None, ALU.mult)
                    dve.drain()
                    dve.wait_ge(cols_ready, 1)
                else:
                    up, down = LOW, 1.0 / LOW
                    dve.wait_ge(cols_ready, 1)
                dve.tensor_scalar(F2[:, :], F2[:, :], up, LOW, ALU.mult, ALU.mult)
                dve.tensor_scalar(beta_low[:, :], beta[:, :], down, 1.0 / LOW, ALU.mult, ALU.mult)
                dve.drain()
                dve.tensor_scalar(beta[:, :], beta[:, :], down, None, ALU.mult)
                dve.drain()
            dve.sem_inc(banks_free, BLOCKS)
            def main(wide):
                if not mix and not wide:
                    dve.tensor_scalar(F1[:, :], F1[:, :], up, LOW, ALU.mult, ALU.mult)
                    dve.tensor_scalar(alpha_low[:, :], alpha[:, :], down, 1.0 / LOW, ALU.mult, ALU.mult)
                    dve.drain()
                    dve.tensor_scalar(alpha[:, :], alpha[:, :], down, None, ALU.mult)
                    dve.drain()
                parts = [split_parts(k, wide) for k in range(2)]
                if gat:
                    for k in range(2):
                        n = part_width(k, wide)
                        dve.memset(G(k, wide)[:, :, n - 1:n], 1.0)
                F = (F1, F2)

                def make_masks(g, col):
                    edges = adj_u32[:, GROUP * g:GROUP * (g + 1), bass.ds(col * QU, QU)]
                    M1, M2 = (m[:, g % RING, :, :].bitcast(U32) for m in (m1, m2))
                    dve.tensor_tensor(M2, M2, edges, ALU.bitwise_and)
                    dve.drain()
                    dve.tensor_tensor(M1, M2, edges, ALU.bitwise_xor).then_inc(masks_ready, 1)

                def scale_rows(g):
                    here = slice(GROUP * g, GROUP * (g + 1))
                    if gat:
                        dve.wait_ge(wh_copied, g + 1)
                        V = wh[:, here, :]
                    else:
                        dve.wait_ge(v_loaded[g % 2], 16 * (g // 2 + 1))
                        V = vt[g % 2]
                    for k in range(2):
                        f = F[k][:, here]
                        g32 = g32_sets[g % 2][k]
                        dve.tensor_tensor(g32[:, :, 0:FEAT], V, bcast_cols(f, FEAT), ALU.mult)
                        if pw > FEAT:
                            dve.tensor_copy(g32[:, :, FEAT], f)
                        if pw > FEAT + 1:
                            dve.scalar_tensor_tensor(g32[:, :, FEAT + 1], f, 1.0 if wide and k == 0 else LOW ** -2, f,
                                                     ALU.mult, ALU.mult)
                        dve.drain().then_inc(g_scaled, 1)
                    dve.sem_inc(v_used, 1)

                scale_rows(0)
                for g in range(GROUPS):
                    here = slice(GROUP * g, GROUP * (g + 1))
                    g32 = g32_sets[g % 2]
                    if g < GROUPS - 1:
                        scale_rows(g + 1)
                    for k in range(2):
                        dve.wait_ge(g_hi, 2 * g + k + 1)
                        if wide and k == 0:
                            dve.tensor_tensor(g32[0], g32[0], parts[0][:, here, 0, :], ALU.subtract)\
                                .then_inc(g_rest, 1)
                        else:
                            dve.scalar_tensor_tensor(parts[k][:, here, 1, :], parts[k][:, here, 0, :], -LOW,
                                                     g32[k], ALU.mult, ALU.add)
                    if wide:
                        dve.wait_ge(g_mid, g + 1)
                        dve.tensor_tensor(parts[0][:, here, 2, :], g32[0], parts[0][:, here, 1, :],
                                          ALU.subtract)
                    dve.wait_ge(signs_ready, g + 1)
                    if gat:
                        dve.wait_ge(adj_first[g * FIRST_PARTS // GROUPS], 16)
                    make_masks(g, 0)
                dve.sem_inc(res_used, 1)
                dve.sem_inc(late_free, 1)

                def masks(s, g):
                    dve.wait_ge(signs_ready, s * GROUPS + (GROUPS + g + 1))
                    make_masks(g, s + 1)

                def evacuate(s):
                    for b in range(BLOCKS):
                        dve.wait_ge(m2_scaled, s * BLOCKS + (b + 1))
                        for k in range(2):
                            if gat:
                                n = part_width(k, wide)
                                dve.tensor_copy(small[:, k, b:b + 1], bank[2 * b + k][:, n - 1:n])
                            if spread and wide and k == 0:
                                dve.tensor_reduce(small[:, 0, b:b + 1], bank[2 * b][:, pw - 1:width:pw],
                                                  AX_X, ALU.add)
                            elif spread:
                                dve.tensor_copy(pairs[:, k, :, b], bank[2 * b + k][:, pw - 1:2 * pw:pw])
                        here = bass.ds(s * BLOCKS + b, 1)
                        for n, factor in ((slice(0, 2 * pw), alpha),) if wide else \
                                ((slice(0, pw), alpha), (slice(pw, 2 * pw), alpha_low)):
                            last = dve.scalar_tensor_tensor(R[:, b, n], bank[2 * b][:, n], factor[:, here],
                                                            R[:, b, n], ALU.mult, ALU.add)
                        last.then_inc(banks_free, 1)
                    dve.drain()
                    if spread:
                        for k in range(1 if wide else 0, 2):
                            dve.scalar_tensor_tensor(small[:, k, :], pairs[:, k, 0, :], LOW, pairs[:, k, 1, :],
                                                     ALU.mult, ALU.add)
                        dve.drain()

                def add_parts():
                    n = FEAT if mix else FEAT + 1
                    if wide:
                        dve.tensor_tensor(R[:, :, pw:pw + n], R[:, :, pw:pw + n], R[:, :, 2 * pw:2 * pw + n],
                                          ALU.add)
                        dve.drain()
                    dve.tensor_tensor(R[:, :, 0:n], R[:, :, 0:n], R[:, :, pw:pw + n], ALU.add)
                    dve.drain()

                A = R[:, :, 0:FEAT]
                B = R[:, :, pw:pw + FEAT]
                C = R[:, :, 2 * pw:2 * pw + FEAT]

                def finish_gat(s, between):
                    mine = bass.ds(s * BLOCKS, BLOCKS)
                    dve.tensor_tensor(kept["deg"][:, mine], small[:, 0, :], small[:, 1, :], ALU.add)
                    add_parts()
                    dve.reciprocal(small[:, 0, :], R[:, :, FEAT])
                    dve.drain()
                    dve.tensor_tensor(A, A, bcast_cols(small[:, 0, :], FEAT), ALU.mult)
                    dve.drain()
                    dve.tensor_scalar(B, A, 0.0, None, ALU.min).then_inc(elu_arg, 1)
                    dve.wait_ge(res_loaded, 16 * s + 16)
                    dve.scalar_tensor_tensor(C, A, 0.0, xt, ALU.max, ALU.add)
                    dve.drain().then_inc(res_used, 1)
                    between(0)
                    dve.wait_ge(elu_exp, s + 1)
                    dve.scalar_tensor_tensor(A, B, 1.0, C, ALU.subtract, ALU.add)
                    dve.drain()
                    between(1)
                    norm_moments(dve, A, stats, mv, var_ready, rstd)
                    between(2)
                    norm_apply(dve, A, C, mv, rstd_ready, s + 1, rstd).then_inc(post_done, 1)

                def finish_spread(s, between):
                    mine = bass.ds(s * BLOCKS, BLOCKS)
                    q1, q2, u, v, rd, rs = (small[:, j, :] for j in range(6))
                    add_parts()
                    dve.reciprocal(rd, R[:, :, FEAT])
                    dve.drain()
                    dve.tensor_copy(rden[:, mine], rd)
                    dve.tensor_tensor(u, rd, alpha[:, mine], ALU.mult)
                    dve.tensor_tensor(v, rd, beta[:, mine], ALU.mult)
                    dve.tensor_tensor(A, A, bcast_cols(rd, FEAT), ALU.mult)
                    dve.drain()
                    dve.tensor_tensor(q1, q1, u, ALU.mult)
                    dve.tensor_tensor(q2, q2, v, ALU.mult)
                    dve.drain()
                    dve.tensor_tensor(q1, q1, u, ALU.mult)
                    dve.tensor_tensor(q2, q2, v, ALU.mult)
                    dve.drain()
                    dve.tensor_tensor(rs, q1, q2, ALU.add)
                    dve.drain()
                    dve.tensor_scalar(rowsum[:, mine], rs, 0.5, None, ALU.mult)
                    between(0)
                    dve.tensor_scalar(u, rs, -0.5, coe[:, 1, 2:3], ALU.mult, ALU.add)
                    dve.drain()
                    dve.wait_ge(res_loaded, 16 * s + 16)
                    dve.tensor_tensor(B, xt, bcast_cols(u, FEAT), ALU.mult)
                    dve.drain().then_inc(res_used, 1)
                    dve.tensor_tensor(A, A, B, ALU.add)
                    dve.drain()
                    between(1)
                    dve.tensor_scalar(B, A, THRESH, 0.0, ALU.add, ALU.min)
                    dve.tensor_scalar(C, A, THRESH, 0.0, ALU.subtract, ALU.max)
                    dve.drain()
                    dve.tensor_tensor(C, C, B, ALU.add).then_inc(post_done, 1)

                def finish_mix(s, between):
                    mine = bass.ds(s * BLOCKS, BLOCKS)
                    add_parts()
                    dve.tensor_tensor(A, A, bcast_cols(rden[:, mine], FEAT), ALU.mult)
                    dve.drain()
                    dve.wait_ge(res_loaded, 16 * s + 16)
                    feat = xt
                    dve.scalar_tensor_tensor(feat, A, coe[:, 2, 3:4], feat, ALU.mult, ALU.add)
                    dve.wait_ge(late_loaded, 32 * s + 32)
                    between(0)
                    dve.tensor_scalar(C, h0_rows, coe[:, 1, 0:1], None, ALU.mult)
                    dve.drain()
                    dve.scalar_tensor_tensor(C, feat, coe[:, 0, 0:1], C, ALU.mult, ALU.add)
                    dve.drain()
                    dve.tensor_tensor(feat, feat, bcast_cols(rowsum[:, mine], FEAT), ALU.mult)
                    dve.scalar_tensor_tensor(C, C, coe[:, 1, 1:2], x3_rows, ALU.mult, ALU.add)
                    dve.drain().then_inc(late_free, 1)
                    dve.tensor_tensor(A, A, feat, ALU.add)
                    dve.drain().then_inc(res_used, 1)
                    dve.scalar_tensor_tensor(A, A, coe[:, 0, 1:2], C, ALU.mult, ALU.add)
                    dve.drain()
                    between(1)
                    norm_moments(dve, A, stats, mv, var_ready, rstd)
                    between(2)
                    norm_apply(dve, A, C, mv, rstd_ready, s + 1, rstd).then_inc(post_done, 1)

                finish = {"gat": finish_gat, "spread": finish_spread, "mix": finish_mix}[kind]
                with dve.Fori(0, STEPS - 1) as s:
                    if gat:
                        dve.wait_ge(adj_ready, s + 2)
                    for g in range(AHEAD):
                        masks(s, g)
                    evacuate(s)
                    for g in range(AHEAD, RING):
                        masks(s, g)
                    n = 2 if spread else 3
                    finish(s, lambda part: masks(s, RING + part))
                    dve.drain()
                    for g in range(RING + n, GROUPS):
                        masks(s, g)
                evacuate(STEPS - 1)
                finish(STEPS - 1, lambda part: None)

            by_range(dve, main)


def mamba_inputs_stage(nc, kept, dram):
    QU = CHUNK // 4
    SLOTS = 4
    SCALE = 1024.0
    TAPS = 4
    D = 2
    STATE = 16
    RANK = 8
    adj_u32 = kept["adj"][:, :].bitcast(U32).rearrange("p (t n) -> p t n", t=TILES)
    x1_g = dram["x1"].rearrange("(g t p) f -> g p t f", p=P, t=GROUP)

    with Arena(nc, "min") as a:
        Gx = a.sb("Gx", [P, TILES, 2, FEAT], F16)
        stage = a.sb("stage", [P, SLOTS, GROUP, QU], U32)
        stage8 = stage[:, :, :, :].bitcast(F8)
        ident, A, w_out = kept["ident"], kept["A"], kept["w_out"]
        ones = a.sb("ones", [1, P], F32)
        gcn_w = a.sb("gcn_w", [P, FEAT], F32)
        gcn_b = a.sb("gcn_b", [1, FEAT], F32)
        w_in = a.sb("w_in", [P, 4 * P], F32)
        w_xp = a.sb("w_xp", [P, D, RANK + 2 * STATE], F32)
        w_dt = a.sb("w_dt", [2 * STATE + RANK, D * P], F32)
        cvec = a.sb("cvec", [P, 2 + D * (TAPS + 3)], F32)
        ln_g, ln_b = cvec[:, 0:1], cvec[:, 1:2]
        dvec = cvec[:, 2:].rearrange("p (d c) -> p d c", d=D)
        conv_w, conv_b, b_dt, d_half = (dvec[:, :, 0:TAPS], dvec[:, :, TAPS:TAPS + 1],
                                        dvec[:, :, TAPS + 1:TAPS + 2], dvec[:, :, TAPS + 2:TAPS + 3])
        ax = a.sb("ax", [P, CHUNK], F32)
        h = a.sb("h", [P, BLOCKS, FEAT], F32)
        hT = a.sb("hT", [P, CHUNK], F32)
        xc = a.sb("xc", [P, D, TAPS - 1 + CHUNK], F32)
        conv = a.sb("conv", [P, D, CHUNK], F32)
        tanh_c = a.sb("tanh_c", [P, D, CHUNK], F32)
        v = tanh_c
        u2 = a.sb("u2", [P, D, CHUNK], F32)
        ud = a.sb("ud", [P, D, CHUNK], F32)
        sz = a.sb("sz", [P, D, CHUNK], F32)
        xin = [room[:, k, :].rearrange("p (t f) -> p t f", t=GROUP)
               for room in (conv, u2, ud, sz) for k in range(D)]
        halves = a.sb("halves", [P, TILES], F32)
        D1 = a.sb("D1", [P, TILES], F32)
        dbc = a.sb("dbc", [2 * STATE + RANK, CHUNK], F32)
        bc_parts = a.sb("bc_parts", [2 * STATE, PARTS, CHUNK], BF16)
        na = a.sb("na", [P, D, CHUNK], F32)
        dt = a.sb("dt", [P, D, CHUNK], F32)
        du = a.sb("du", [P, D, CHUNK], F32)
        stats = a.sb("stats", [P, BLOCKS, 6], F32)
        mv = a.sb("mv", [P, BLOCKS, 2], F32)
        rstd = a.sb("rstd", [P, BLOCKS, 2], F32)
        half = a.sb("half", [P, BLOCKS], F32)
        ps_ax = a.ps("ax_ps", [P, 512])
        ps_h = a.ps("h_ps", [P, 512])
        ps_hT = a.ps("hT_ps", [P, 512])
        ps_xz = [a.ps(f"xz{m}", [P, 512]) for m in range(4)]
        ps_dbc = a.ps("dbc_ps", [P, 512])

        w_loaded = a.sem("w_loaded")
        x_loaded = [a.sem(f"x_loaded{k}") for k in range(GROUPS)]
        deg1 = a.sem("deg1")
        D_ready = a.sem("D_ready")
        x_hi = a.sem("x_hi")
        x_split = a.sem("x_split")
        adj_staged = [a.sem(f"adj_staged{k}") for k in range(SLOTS)]
        adj_used = a.sem("adj_used")
        gcn_done = a.sem("gcn_done")
        ax_ready = a.sem("ax_ready")
        h_done = a.sem("h_done")
        h_relu = a.sem("h_relu")
        var_ready = a.sem("var_ready")
        rstd_ready = a.sem("rstd_ready")
        h_norm = a.sem("h_norm")
        hT_done = a.sem("hT_done")
        hT_ready = a.sem("hT_ready")
        xz_done = a.sem("xz_done")
        xc_ready = a.sem("xc_ready")
        halo_ready = a.sem("halo_ready")
        tz_ready = a.sem("tz_ready")
        sz_ready = a.sem("sz_ready")
        conv_ready = a.sem("conv_ready")
        tanh_ready = a.sem("tanh_ready")
        u_ready = a.sem("u_ready")
        ud_ready = a.sem("ud_ready")
        dbc_done = a.sem("dbc_done")
        dbc_ready = a.sem("dbc_ready")
        bc_hi = a.sem("bc_hi")
        bc_rest = a.sem("bc_rest")
        bc_mid = a.sem("bc_mid")
        bc_split = a.sem("bc_split")
        dt_done = a.sem("dt_done")
        v_ready = a.sem("v_ready")
        na_ready = a.sem("na_ready")
        log_ready = a.sem("log_ready")
        du_ready = a.sem("du_ready")
        stored = {k: a.sem(f"stored_{k}") for k in ("sz", "ud", "bc", "dt", "du")}
        consts = a.sem("consts")
        picking = a.sem("picking")
        scan_w_loaded = a.sem("scan_w_loaded")
        A_exp = a.sem("A_exp")
        w_scaled = a.sem("w_scaled")
        front_stored = a.sem("front_stored")
        tail_stored = a.sem("tail_stored")
        pool_passed = a.sem("pool_passed")
        pe_passed = a.sem("pe_passed")
        block = a.block()

        def store_to(name, c):
            return dram[name][:, :, bass.ds(c * CHUNK, CHUNK)].rearrange("d p n -> p d n")

        @block.sync
        def _(sp):
            for g in range(GROUPS):
                sp.dma_start(xin[g], x1_g[g]).then_inc(x_loaded[g], 16)
            for tile, name in ((gcn_w, "gcn_w"), (gcn_b, "gcn_b"), (w_in, "w_in"),
                               (w_dt[2 * STATE:, :], "w_dt")):
                sp.dma_start(tile[:, :], dram[name]).then_inc(w_loaded, 16)
            sp.dma_start(w_xp[:, :, :], dram["w_xp"].rearrange("(d p) c -> p d c", p=P)).then_inc(w_loaded, 16)
            sp.dma_start(cvec[:, :], dram["cvec"]).then_inc(w_loaded, 16)
            sp.dma_start(A[:, :, :], dram["A_log"].rearrange("(d p) s -> p d s", p=P)).then_inc(scan_w_loaded, 16)
            sp.dma_start(w_out[:, :, :], dram["w_out"].rearrange("(d p) f -> p d f", p=P))\
                .then_inc(scan_w_loaded, 16)
            with sp.Fori(0, STEPS) as c:
                for g in range(GROUPS):
                    if g == SLOTS - 1:
                        sp.wait_ge(ax_ready, c + 1)
                    else:
                        sp.wait_ge(adj_used, c * (GROUPS - 1) + (g + GROUPS - SLOTS + (g < SLOTS)))
                    sp.dma_start(stage[:, g % SLOTS, :, :],
                                 adj_u32[:, GROUP * g:GROUP * (g + 1), bass.ds(c * QU, QU)])\
                        .then_inc(adj_staged[g % SLOTS], 16)

        @block.gpsimd
        def _(pool):
            pool.memset(half[:, :], -0.5).then_inc(consts, 1)
            pool.memset(ones[:, :], 1.0).then_inc(consts, 1)
            pool.memset(xc[:, :, :], 0.0).then_inc(consts, 1)
            pool.memset(halves[:, :], -0.5).then_inc(consts, 1)
            pool.wait_ge(consts, 4)
            pool.wait_ge(deg1, 1)
            pool.tensor_tensor(kept["Dc"][:, :], D1[:, :], halves[:, :], ALU.pow).then_inc(D_ready, 1)
            pick = kept["pick"]
            pool.memset(pick[:, :], 0.0).then_inc(picking, 1)
            pool.wait_ge(picking, 1)
            for k in range(PARTS):
                pool.affine_select(out=pick[:, :], in_=pick[:, :], compare_op=ALU.not_equal, fill=1.0,
                                   base=-2 * STATE * k, pattern=[[-1, 2 * STATE]], channel_multiplier=1)\
                    .then_inc(picking, 1)
                pool.wait_ge(picking, 2 + k)
            pool.sem_inc(front_stored, 1)
            pool.sem_inc(tail_stored, 1)
            def chunk(c, first):
                pool.wait_ge(var_ready, c + 1)
                pool.tensor_tensor(rstd[:, :, 1], rstd[:, :, 0], half[:, :], ALU.pow).then_inc(rstd_ready, 1)
                if not first:
                    tail_out(c - 1)
                pool.wait_ge(sz_ready, c + 1)
                pool.sem_inc(pool_passed, 1)
                pool.dma_start(store_to("sz", c), sz[:, :, :]).then_inc(stored["sz"], 16)
                pool.wait_ge(ud_ready, c + 1)
                pool.sem_inc(pool_passed, 1)
                pool.dma_start(store_to("ud", c), ud[:, :, :]).then_inc(stored["ud"], 16)
                if not first:
                    tail_left(c - 1)
                for name in ("sz", "ud"):
                    pool.wait_ge(stored[name], 16 * c + 16)
                pool.sem_inc(front_stored, 1)

            def tail_out(c):
                pool.wait_ge(bc_split, c + 1)
                pool.sem_inc(pool_passed, 1)
                pool.dma_start(dram["bc_parts"][:, :, bass.ds(c * CHUNK, CHUNK)].rearrange("k r n -> r k n"),
                               bc_parts[:, :, :]).then_inc(stored["bc"], 16)
                pool.wait_ge(du_ready, c + 1)
                pool.sem_inc(pool_passed, 1)
                pool.dma_start(store_to("dt", c), dt[:, :, :]).then_inc(stored["dt"], 16)
                pool.dma_start(store_to("du", c), du[:, :, :]).then_inc(stored["du"], 16)

            def tail_left(c):
                for name in ("bc", "dt", "du"):
                    pool.wait_ge(stored[name], 16 * c + 16)
                pool.sem_inc(tail_stored, 1)

            chunk(0, True)
            with pool.Fori(0, STEPS - 1) as i:
                chunk(i + 1, False)
            tail_out(STEPS - 1)
            tail_left(STEPS - 1)

        @block.tensor
        def _(pe):
            pe.sem_inc(adj_used, GROUPS - 1)

            def gcn(c, g, first):
                pe.wait_ge(adj_staged[g % SLOTS], c * (16 * GROUPS // SLOTS) + 16 * (g // SLOTS + 1))
                if first:
                    pe.wait_ge(x_split, g + 1)
                if g == 0:
                    pe.wait_ge(ax_ready, c + 1)
                pe.sem_inc(pe_passed, 1)
                for t in range(GROUP):
                    i = GROUP * g + t
                    for k in range(2):
                        mm = pe.matmul(ps_ax[:, :], Gx[:, i, k, :], stage8[:, g % SLOTS, t, :],
                                       start=(i == 0 and k == 0), stop=(i == TILES - 1 and k == 1))
                    if t == GROUP - 1:
                        mm.then_inc(adj_used if g < GROUPS - 1 else gcn_done, 1)

            def hidden(c):
                pe.wait_ge(ax_ready, c + 2)
                for b in range(BLOCKS):
                    pe.matmul(ps_h[:, b * P:(b + 1) * P], ax[:, b * P:(b + 1) * P], gcn_w[:, :],
                              start=True, stop=False)
                    mm = pe.matmul(ps_h[:, b * P:(b + 1) * P], ones[:, :], gcn_b[:, :], start=False, stop=True)
                mm.then_inc(h_done, 1)

            def turn(c):
                pe.wait_ge(h_norm, c + 1)
                for b in range(BLOCKS):
                    mm = pe.transpose(ps_hT[:, b * P:(b + 1) * P], h[:, b, :], ident[:, :])
                mm.then_inc(hT_done, 1)

            def project(c):
                pe.wait_ge(hT_ready, c + 1)
                pe.wait_ge(v_ready, D * (c + 1))
                for m in range(4):
                    pe.matmul(ps_xz[m][:, :], w_in[:, m * P:(m + 1) * P], hT[:, :], start=True, stop=True)\
                        .then_inc(xz_done, 1)

            def low_rank(c):
                pe.wait_ge(u_ready, c + 1)
                for d in range(D):
                    mm = pe.matmul(ps_dbc[0:RANK + 2 * STATE, :], w_xp[:, d, :], u2[:, d, :],
                                   start=(d == 0), stop=(d == D - 1))
                mm.then_inc(dbc_done, 1)

            def steps_of_time(c):
                pe.wait_ge(dbc_ready, c + 1)
                for d in range(D):
                    pe.matmul(ps_xz[d][:, :], w_dt[2 * STATE:, d * P:(d + 1) * P], dbc[2 * STATE:, :],
                              start=True, stop=True).then_inc(dt_done, 1)

            for g in range(GROUPS):
                gcn(0, g, True)
            pe.wait_ge(w_loaded, 16 * 6)
            pe.wait_ge(consts, 4)
            pe.wait_ge(w_scaled, 1)

            def chunk(c, first):
                gcn(c + 1, 0, False)
                if not first:
                    low_rank(c - 1)
                hidden(c)
                gcn(c + 1, 1, False)
                if not first:
                    steps_of_time(c - 1)
                gcn(c + 1, 2, False)
                gcn(c + 1, 3, False)
                turn(c)
                gcn(c + 1, 4, False)
                project(c)
                for g in range(5, GROUPS):
                    gcn(c + 1, g, False)

            chunk(0, True)
            with pe.Fori(0, STEPS - 2) as i:
                chunk(i + 1, False)
            last = STEPS - 1
            low_rank(last - 1)
            hidden(last)
            steps_of_time(last - 1)
            for piece in (turn, project, low_rank, steps_of_time):
                piece(last)

        @block.scalar
        def _(act):
            act.sem_inc(ax_ready, 1)
            for g in range(GROUPS):
                act.wait_ge(x_loaded[g], 16)
                act.activation(Gx[:, GROUP * g:GROUP * (g + 1), 0, :], xin[g], ACT.Copy,
                               scale=SCALE).then_inc(x_hi, 1)
            act.wait_ge(scan_w_loaded, 32)
            act.activation(A[:, :, :], A[:, :, :], ACT.Exp).then_inc(A_exp, 1)
            act.sem_inc(v_ready, D)
            act.wait_ge(consts, 4)
            act.wait_ge(w_loaded, 16 * 6)

            def arguments(c):
                for d in range(D):
                    act.wait_ge(dt_done, D * c + d + 1)
                    act.activation(v[:, d, :], ps_xz[d][:, :], ACT.Identity, bias=b_dt[:, d, :])\
                        .then_inc(v_ready, 1)
                act.wait_ge(tail_stored, c + 1)
                act.activation(bc_parts[:, 0, :], dbc[0:2 * STATE, :], ACT.Copy).then_inc(bc_hi, 1)

            def softplus(c):
                act.wait_ge(bc_rest, c + 1)
                act.activation(bc_parts[:, 1, :], dbc[0:2 * STATE, :], ACT.Copy).then_inc(bc_mid, 1)
                act.wait_ge(na_ready, c + 1)
                act.activation(na[:, :, :], na[:, :, :], ACT.Exp)
                act.drain()
                act.activation(na[:, :, :], na[:, :, :], ACT.Ln, bias=1.0).then_inc(log_ready, 1)

            def chunk(c, first):
                act.wait_ge(gcn_done, c + 1)
                act.activation(ax[:, :], ps_ax[:, :], ACT.Copy, scale=1.0 / SCALE).then_inc(ax_ready, 1)
                if not first:
                    low_rank_rows(c - 1)
                act.wait_ge(h_done, c + 1)
                act.activation(h[:, :, :], ps_h[:, :].rearrange("p (b f) -> p b f", b=BLOCKS), ACT.Relu)\
                    .then_inc(h_relu, 1)
                if not first:
                    arguments(c - 1)
                    softplus(c - 1)
                act.wait_ge(halo_ready, c + 1)
                for d in range(D):
                    act.wait_ge(xz_done, 4 * c + d + 1)
                    act.activation(xc[:, d, TAPS - 1:], ps_xz[d][:, :], ACT.Copy).then_inc(xc_ready, 1)
                act.wait_ge(front_stored, c + 1)
                for d in range(D):
                    act.wait_ge(xz_done, 4 * c + D + d + 1)
                    act.activation(sz[:, d, :], ps_xz[D + d][:, :], ACT.Tanh, scale=0.5).then_inc(tz_ready, 1)
                act.wait_ge(conv_ready, c + 1)
                act.activation(tanh_c[:, :, :], conv[:, :, :], ACT.Tanh, scale=0.5).then_inc(tanh_ready, 1)

            def low_rank_rows(c):
                act.wait_ge(dbc_done, c + 1)
                act.activation(dbc[:, :], ps_dbc[0:RANK + 2 * STATE, :], ACT.Copy).then_inc(dbc_ready, 1)

            chunk(0, True)
            with act.Fori(0, STEPS - 1) as i:
                chunk(i + 1, False)
            low_rank_rows(STEPS - 1)
            arguments(STEPS - 1)
            softplus(STEPS - 1)

        @block.vector
        def _(dve):
            dve.tensor_scalar(D1[:, :], kept["deg"][:, :], 1.0, None, ALU.add).then_inc(deg1, 1)
            for g in range(GROUPS):
                dve.wait_ge(x_hi, g + 1)
                here = slice(GROUP * g, GROUP * (g + 1))
                dve.scalar_tensor_tensor(Gx[:, here, 1, :], xin[g], SCALE, Gx[:, here, 0, :],
                                         ALU.mult, ALU.subtract).then_inc(x_split, 1)
            dve.wait_ge(w_loaded, 16 * 6)
            dve.wait_ge(consts, 4)
            dve.tensor_scalar(w_xp[:, :, :], w_xp[:, :, :], 0.5, None, ALU.mult)
            dve.tensor_scalar(d_half, d_half, 0.5, None, ALU.mult)
            dve.wait_ge(A_exp, 1)
            dve.tensor_scalar(A[:, :, :], A[:, :, :], -1.0, None, ALU.mult)
            dve.tensor_scalar(w_out[:, :, :], w_out[:, :, :], 0.5, None, ALU.mult)
            dve.drain().then_inc(w_scaled, 1)
            dve.sem_inc(halo_ready, 1)

            def arguments(c):
                dve.wait_ge(bc_hi, c + 1)
                dve.tensor_tensor(dbc[0:2 * STATE, :], dbc[0:2 * STATE, :], bc_parts[:, 0, :], ALU.subtract)\
                    .then_inc(bc_rest, 1)
                dve.wait_ge(v_ready, D * (c + 2))
                dve.scalar_tensor_tensor(na[:, :, :], v[:, :, :], -1.0, v[:, :, :], ALU.mult, ALU.min)\
                    .then_inc(na_ready, 1)

            def low_parts(c):
                dve.wait_ge(bc_mid, c + 1)
                dve.tensor_tensor(bc_parts[:, 2, :], dbc[0:2 * STATE, :], bc_parts[:, 1, :], ALU.subtract)\
                    .then_inc(bc_split, 1)

            def softplus(c):
                dve.wait_ge(log_ready, c + 1)
                dve.wait_ge(tail_stored, c + 1)
                dve.scalar_tensor_tensor(dt[:, :, :], v[:, :, :], 0.0, na[:, :, :], ALU.max, ALU.add)
                dve.drain()
                dve.scalar_tensor_tensor(du[:, :, :], dt[:, :, :], 0.5, u2[:, :, :], ALU.mult, ALU.mult)\
                    .then_inc(du_ready, 1)

            def chunk(c, first):
                dve.wait_ge(h_relu, c + 1)
                norm_blocks(dve, h, h, stats, mv, var_ready, rstd_ready, c + 1, rstd).then_inc(h_norm, 1)
                if not first:
                    arguments(c - 1)
                    low_parts(c - 1)
                dve.wait_ge(hT_done, c + 1)
                dve.tensor_scalar(hT[:, :], ps_hT[:, :], ln_g, ln_b, ALU.mult, ALU.add).then_inc(hT_ready, 1)
                if not first:
                    softplus(c - 1)
                for d in range(D):
                    dve.wait_ge(xc_ready, D * c + d + 1)
                    dve.tensor_scalar(conv[:, d, :], xc[:, d, TAPS - 1:], conv_w[:, d, TAPS - 1:TAPS],
                                      conv_b[:, d, :], ALU.mult, ALU.add)
                for k in range(TAPS - 1):
                    dve.drain()
                    for d in range(D):
                        dve.scalar_tensor_tensor(conv[:, d, :], xc[:, d, k:k + CHUNK], conv_w[:, d, k:k + 1],
                                                 conv[:, d, :], ALU.mult, ALU.add)
                dve.drain().then_inc(conv_ready, 1)
                dve.tensor_copy(xc[:, :, 0:TAPS - 1], xc[:, :, CHUNK:CHUNK + TAPS - 1]).then_inc(halo_ready, 1)
                dve.wait_ge(tanh_ready, c + 1)
                dve.scalar_tensor_tensor(u2[:, :, :], tanh_c[:, :, :], 1.0, conv[:, :, :], ALU.add, ALU.mult)
                dve.drain().then_inc(u_ready, 1)
                dve.wait_ge(tz_ready, D * (c + 1))
                for d in range(D):
                    last = dve.scalar_tensor_tensor(sz[:, d, :], sz[:, d, :], 1.0, ps_xz[D + d][:, :],
                                                    ALU.add, ALU.mult)
                last.then_inc(sz_ready, 1)
                for d in range(D):
                    last = dve.tensor_scalar(ud[:, d, :], u2[:, d, :], d_half[:, d, :], None, ALU.mult)
                last.then_inc(ud_ready, 1)

            chunk(0, True)
            with dve.Fori(0, STEPS - 1) as i:
                chunk(i + 1, False)
            arguments(STEPS - 1)
            low_parts(STEPS - 1)
            softplus(STEPS - 1)


def mamba_scan_stage(nc, kept, dram):
    D = 2
    STATE = 16
    ROWS = 2 * STATE
    XRING = 4
    CRING = 4
    LAG = 2

    with Arena(nc, "scan") as a:
        ident, pick, A, w_out = kept["ident"], kept["pick"], kept["A"], kept["w_out"]
        half = a.sb("half", [P, BLOCKS], F32)
        state = a.sb("state", [P, STATE, D], F32)
        dt = [a.sb(f"dt{k}", [P, D, CHUNK], F32) for k in range(2)]
        du = [a.sb(f"du{k}", [P, D, CHUNK], F32) for k in range(2)]
        ud = [a.sb(f"ud{k}", [P, D, CHUNK], F32) for k in range(2)]
        sz = [a.sb(f"sz{k}", [P, D, CHUNK], F32) for k in range(2)]
        bc = [a.sb(f"bc{k}", [PARTS * ROWS, CHUNK], BF16) for k in range(2)]
        dA = [a.sb(f"dA{k}", [P, D, CHUNK], F32) for k in range(2)]
        C_sb = [a.sb(f"C_sb{k}", [P, CHUNK], F32) for k in range(CRING)]
        X = [a.sb(f"X{k}", [P, D, CHUNK], F32) for k in range(XRING)]
        yv = a.sb("yv", [P, D, CHUNK], F32)
        xt = a.sb("xt", [P, BLOCKS, FEAT], F32)
        stats = a.sb("stats", [P, BLOCKS, 6], F32)
        mv = a.sb("mv", [P, BLOCKS, 2], F32)
        rstd = a.sb("rstd", [P, BLOCKS, 2], F32)
        B = [a.ps(f"B{k}", [P, CHUNK]) for k in range(2)]
        C = [a.ps(f"C{k}", [P, CHUNK]) for k in range(2)]
        ps_y = a.ps("y", [P, D, CHUNK])
        ps_o = a.ps("o", [P, 512])

        consts = a.sem("consts")
        in_loaded = [a.sem(f"in_loaded{k}") for k in range(2)]
        bc_spread = a.sem("bc_spread")
        B_used = a.sem("B_used")
        dA_ready = a.sem("dA_ready")
        C_ready = a.sem("C_ready")
        scanned = a.sem("scanned")
        h_ready = a.sem("h_ready")
        hC_ready = a.sem("hC_ready")
        X_used = a.sem("X_used")
        y_ready = a.sem("y_ready")
        o_done = a.sem("o_done")
        x_loaded = a.sem("x_loaded")
        var_ready = a.sem("var_ready")
        rstd_ready = a.sem("rstd_ready")
        x2_ready = a.sem("x2_ready")
        x2_stored = a.sem("x2_stored")
        block = a.block()

        INPUTS = 5

        def chunk_loop(eng, body):
            body(0, 0, first=True)
            with eng.Fori(0, STEPS // 2 - 1) as i:
                body(i * 2 + 1, 1, first=False)
                body(i * 2 + 2, 0, first=False)
            body(STEPS - 1, 1, first=False)

        def chunk_loads(c, parity):
            return 8 * INPUTS * c + 8 * INPUTS * (2 - parity)

        def is_last(c):
            return isinstance(c, int) and c == STEPS - 1

        def nodes(c):
            return slice(c * CHUNK, (c + 1) * CHUNK) if isinstance(c, int) else bass.ds(c * CHUNK, CHUNK)

        def rows(name, c):
            return dram[name][nodes(c), :].rearrange("(b p) f -> p b f", p=P)

        def per_tile(row):
            return row.unsqueeze(1).broadcast_to([P, D, CHUNK])

        @block.sync
        def _(sp):
            def load_inputs(c, parity):
                sp.dma_start(bc[parity][:, :], dram["bc_parts"][:, :, nodes(c)].rearrange("k r n -> (k r) n"))\
                    .then_inc(in_loaded[parity], 16)
                for tile, name in ((du, "du"), (dt, "dt"), (ud, "ud"), (sz, "sz")):
                    sp.dma_start(tile[parity][:, :, :], dram[name][:, :, nodes(c)].rearrange("d p n -> p d n"))\
                        .then_inc(in_loaded[parity], 16)

            def finish(c):
                sp.wait_ge(x2_stored, 16 * c + 16)
                sp.dma_start(xt[:, :, :], rows("x1", c)).then_inc(x_loaded, 16)
                sp.wait_ge(x2_ready, c + 1)
                sp.dma_start(rows("x2", c), xt[:, :, :]).then_inc(x2_stored, 16)

            def body(c, parity, first):
                if first:
                    load_inputs(1, 1)
                    return
                sp.wait_ge(y_ready, c)
                if not is_last(c):
                    load_inputs(c + 1, 1 - parity)
                finish(c - 1)

            sp.sem_inc(x2_stored, 16)
            load_inputs(0, 0)
            chunk_loop(sp, body)
            finish(STEPS - 1)
            sp.wait_ge(x2_stored, 16 * (STEPS + 1))

        @block.gpsimd
        def _(pool):
            pool.memset(half[:, :], -0.5).then_inc(consts, 1)
            pool.wait_ge(consts, 1)

            def root(c):
                pool.wait_ge(var_ready, c + 1)
                pool.tensor_tensor(rstd[:, :, 1], rstd[:, :, 0], half[:, :], ALU.pow).then_inc(rstd_ready, 1)

            def body(c, parity, first):
                for n in range(STATE):
                    pool.wait_ge(C_ready, c * STATE + (n + 1))
                    pool.wait_ge(h_ready, c * STATE + (n + 1))
                    x = X[n % XRING][:, :, :]
                    pool.tensor_tensor(x, x, per_tile(C_sb[n % CRING][:, :]), ALU.mult).then_inc(hC_ready, 1)
                    if n == 6 and not first:
                        root(c - 1)

            chunk_loop(pool, body)
            root(STEPS - 1)

        @block.scalar
        def _(act):
            def body(c, parity, first):
                act.wait_ge(in_loaded[parity], chunk_loads(c, parity))
                for n in range(STATE):
                    if not (first and n < 2):
                        act.wait_ge(h_ready, c * STATE + (n - 1))
                    for d in range(D):
                        last = act.activation(dA[n % 2][:, d, :], dt[parity][:, d, :], ACT.Exp,
                                              scale=A[:, d, n:n + 1])
                    last.then_inc(dA_ready, 1)
                    act.wait_ge(bc_spread, c * STATE + (n + 1))
                    if not (first and n < CRING):
                        act.wait_ge(hC_ready, c * STATE + (n - CRING + 1))
                    act.activation(C_sb[n % CRING][:, :], C[n % 2][:, :], ACT.Copy).then_inc(C_ready, 1)

            chunk_loop(act, body)

        @block.tensor
        def _(pe):
            def picked(r):
                return pick[:, r:r + 1].broadcast_to([PARTS * ROWS, P])

            def spread(c, parity, n):
                if not (isinstance(c, int) and c == 0 and n < 2):
                    pe.wait_ge(B_used, c * STATE + (n - 1))
                    pe.wait_ge(C_ready, c * STATE + (n - 1))
                if n == 0:
                    pe.wait_ge(in_loaded[parity], chunk_loads(c, parity))
                pe.matmul(B[n % 2][:, :], picked(n), bc[parity][:, :], start=True, stop=True)
                pe.matmul(C[n % 2][:, :], picked(STATE + n), bc[parity][:, :], start=True, stop=True)\
                    .then_inc(bc_spread, 1)

            def skip(parity):
                for d in range(D):
                    pe.matmul(ps_y[:, d, :], ident[:, :], ud[parity][:, d, :], start=False, stop=False)

            def add(c, n):
                pe.wait_ge(hC_ready, c * STATE + (n + 1))
                for d in range(D):
                    mm = pe.matmul(ps_y[:, d, :], ident[:, :], X[n % XRING][:, d, :],
                                   start=(n == 0), stop=(n == STATE - 1))
                mm.then_inc(X_used, 1)

            def output(c):
                pe.wait_ge(y_ready, c + 1)
                for b in range(BLOCKS):
                    for d in range(D):
                        mm = pe.matmul(ps_o[:, b * P:(b + 1) * P], yv[:, d, b * P:(b + 1) * P],
                                       w_out[:, d, :], start=(d == 0), stop=(d == D - 1))
                mm.then_inc(o_done, 1)

            def body(c, parity, first):
                for n in range(STATE):
                    if n < STATE - 1:
                        spread(c, parity, n + 1)
                    elif not is_last(c):
                        spread(c + 1, 1 - parity, 0)
                    if n == LAG and not first:
                        pe.wait_ge(y_ready, c)
                    if n >= LAG:
                        add(c, n - LAG)
                    elif not first:
                        add(c - 1, STATE + n - LAG)
                    if n == LAG + 1 and not first:
                        output(c - 1)
                    if n == STATE // 2:
                        skip(parity)

            spread(0, 0, 0)
            chunk_loop(pe, body)
            for n in range(STATE - LAG, STATE):
                add(STEPS - 1, n)
            output(STEPS - 1)

        @block.vector
        def _(dve):
            dve.memset(state[:, :, :], 0.0)
            dve.drain()

            def drive(c, parity, n):
                if n == 0:
                    dve.wait_ge(in_loaded[parity], chunk_loads(c, parity))
                if not (isinstance(c, int) and c == 0 and n < XRING):
                    dve.wait_ge(X_used, c * STATE + (n - XRING + 1))
                dve.wait_ge(bc_spread, c * STATE + (n + 1))
                dve.tensor_tensor(X[n % XRING][:, :, :], du[parity][:, :, :], per_tile(B[n % 2][:, :]),
                                  ALU.mult).then_inc(B_used, 1)

            def y_readout(c, parity):
                dve.wait_ge(X_used, c * STATE + STATE)
                dve.tensor_tensor(yv[:, :, :], ps_y[:, :, :], sz[parity][:, :, :], ALU.mult)\
                    .then_inc(y_ready, 1)

            def residual(c):
                dve.wait_ge(x_loaded, 16 * c + 16)
                dve.wait_ge(o_done, c + 1)
                dve.tensor_tensor(xt[:, :, :], xt[:, :, :],
                                  ps_o[:, :].rearrange("p (b f) -> p b f", b=BLOCKS), ALU.add)
                dve.drain()
                norm_moments(dve, xt, stats, mv, var_ready, rstd)

            def normalize(c):
                norm_apply(dve, xt, xt, mv, rstd_ready, c + 1, rstd).then_inc(x2_ready, 1)

            def body(c, parity, first):
                for n in range(STATE):
                    x = X[n % XRING]
                    dve.wait_ge(B_used, c * STATE + (n + 1))
                    dve.wait_ge(dA_ready, c * STATE + (n + 1))
                    for d in range(D):
                        last = dve.tensor_tensor_scan(x[:, d, :], dA[n % 2][:, d, :], x[:, d, :],
                                                      state[:, n, d:d + 1], ALU.mult, ALU.add)
                    last.then_inc(scanned, 1)
                    if not first and n == 2:
                        y_readout(c - 1, 1 - parity)
                    if n < STATE - 1:
                        drive(c, parity, n + 1)
                    elif not is_last(c):
                        drive(c + 1, 1 - parity, 0)
                    dve.wait_ge(scanned, c * STATE + (n + 1))
                    dve.tensor_copy(state[:, n, :], x[:, :, CHUNK - 1]).then_inc(h_ready, 1)
                    if not first and n == 6:
                        residual(c - 1)
                    if not first and n == 9:
                        normalize(c - 1)

            drive(0, 0, 0)
            dve.drain()
            chunk_loop(dve, body)
            dve.drain()
            y_readout(STEPS - 1, 1)
            residual(STEPS - 1)
            normalize(STEPS - 1)


def gcn_stage(nc, kept, dram):
    QU = CHUNK // 4
    SLOTS = 4
    SCALE = 1024.0
    adj_u32 = kept["adj"][:, :].bitcast(U32).rearrange("p (t n) -> p t n", t=TILES)
    x2_g = dram["x2"].rearrange("(g t p) f -> g p t f", p=P, t=GROUP)
    s1c, s2c, coe, Dc = kept["s1c"], kept["s2c"], kept["coe"], kept["Dc"]

    with Arena(nc, "gcn") as a:
        Gx = a.sb("Gx", [P, TILES, 2, FEAT], F16)
        xin = [a.sb(f"xin{k}", [P, GROUP, FEAT], F32) for k in range(GROUPS)]
        stage = a.sb("stage", [P, SLOTS, GROUP, QU], U32)
        stage8 = stage[:, :, :, :].bitcast(F8)
        ident = kept["ident"]
        W = a.sb("W", [P, FEAT], F32)
        a3 = a.sb("a3", [P, 2], F32)
        bias = a.sb("bias", [P, FEAT], F32)
        Ds = a.sb("Ds", [P, TILES], F32)
        halves = a.sb("halves", [P, TILES], F32)
        xn = a.sb("xn", [P, BLOCKS, FEAT], F32)
        xs = a.sb("xs", [P, BLOCKS, FEAT], F32)
        xt = a.sb("xt", [P, BLOCKS, FEAT], F32)
        y = a.sb("y", [P, BLOCKS, FEAT], F32)
        ax = a.sb("ax", [P, CHUNK], F32)
        x3T = a.sb("x3T", [P, CHUNK], F32)
        row = a.sb("row", [TILES, P], F32)
        stats = a.sb("stats", [P, BLOCKS, 6], F32)
        mv = a.sb("mv", [P, BLOCKS, 2], F32)
        rstd = a.sb("rstd", [P, BLOCKS, 2], F32)
        ps_ax = a.ps("ax_ps", [P, 512])
        ps_o = a.ps("o_ps", [P, 512])
        ps_T = a.ps("T_ps", [P, 512])
        ps_c = a.ps("c_ps", [P, 512])
        ps_r = a.ps("r_ps", [P, 512])

        w_loaded = a.sem("w_loaded")
        consts = a.sem("consts")
        x_loaded = [a.sem(f"x_loaded{k}") for k in range(GROUPS)]
        x_scaled = a.sem("x_scaled")
        x_hi = a.sem("x_hi")
        x_split = a.sem("x_split")
        adj_staged = [a.sem(f"adj_staged{k}") for k in range(SLOTS)]
        adj_used = a.sem("adj_used")
        next_loaded = a.sem("next_loaded")
        own_ready = a.sem("own_ready")
        gcn_done = a.sem("gcn_done")
        ax_ready = a.sem("ax_ready")
        o_done = a.sem("o_done")
        res_loaded = a.sem("res_loaded")
        res_used = a.sem("res_used")
        var_ready = a.sem("var_ready")
        rstd_ready = a.sem("rstd_ready")
        x3_ready = a.sem("x3_ready")
        x3_stored = a.sem("x3_stored")
        T_done = a.sem("T_done")
        T_ready = a.sem("T_ready")
        scores_done = a.sem("scores_done")
        cols_copied = a.sem("cols_copied")
        row_done = a.sem("row_done")
        row_ready = a.sem("row_ready")
        row_stored = a.sem("row_stored")
        temp_exp = a.sem("temp_exp")
        y_free = a.sem("y_free")
        pool_passed = a.sem("pool_passed")
        pe_passed = a.sem("pe_passed")
        block = a.block()

        def rows(name, c):
            here = slice(c * CHUNK, (c + 1) * CHUNK) if isinstance(c, int) else bass.ds(c * CHUNK, CHUNK)
            return dram[name][here, :].rearrange("(b p) f -> p b f", p=P)

        @block.sync
        def _(sp):
            for g in range(GROUPS):
                sp.dma_start(xin[g][:, :, :], x2_g[g]).then_inc(x_loaded[g], 16)
            sp.dma_start(W[:, :], dram["W2"]).then_inc(w_loaded, 16)
            sp.dma_start(a3[:, :], dram["a3"]).then_inc(w_loaded, 16)
            sp.dma_start(bias[:, :], dram["b2"].broadcast_to([P, FEAT])).then_inc(w_loaded, 16)
            sp.dma_start(coe[:, 0, :], dram["temp"].broadcast_to([P, 5])).then_inc(w_loaded, 16)
            with sp.Fori(0, STEPS) as c:
                for g in range(GROUPS):
                    if g == SLOTS - 1:
                        sp.wait_ge(ax_ready, c + 1)
                    else:
                        sp.wait_ge(adj_used, c * (GROUPS - 1) + (g + GROUPS - SLOTS + (g < SLOTS)))
                    sp.dma_start(stage[:, g % SLOTS, :, :],
                                 adj_u32[:, GROUP * g:GROUP * (g + 1), bass.ds(c * QU, QU)])\
                        .then_inc(adj_staged[g % SLOTS], 16)

        @block.gpsimd
        def _(pool):
            pool.memset(halves[:, :], -0.5).then_inc(consts, 1)
            pool.wait_ge(consts, 1)
            pool.dma_start(xn[:, :, :], rows("x2", 0)).then_inc(next_loaded, 16)

            def chunk(c, more):
                pool.wait_ge(res_used, c + 1)
                pool.sem_inc(pool_passed, 1)
                pool.dma_start(xt[:, :, :], rows("x2", c)).then_inc(res_loaded, 16)
                if more:
                    pool.wait_ge(own_ready, c + 1)
                    pool.sem_inc(pool_passed, 1)
                    pool.dma_start(xn[:, :, :], rows("x2", c + 1)).then_inc(next_loaded, 16)
                pool.wait_ge(var_ready, c + 1)
                pool.tensor_tensor(rstd[:, :, 1], rstd[:, :, 0], halves[:, 0:BLOCKS], ALU.pow)\
                    .then_inc(rstd_ready, 1)
                pool.wait_ge(x3_ready, c + 1)
                pool.sem_inc(pool_passed, 1)
                pool.dma_start(rows("x3", c), y[:, :, :]).then_inc(x3_stored, 16)
                pool.wait_ge(x3_stored, 16 * c + 16)
                pool.sem_inc(y_free, 1)

            with pool.Fori(0, STEPS - 1) as c:
                chunk(c, True)
            chunk(STEPS - 1, False)

        @block.tensor
        def _(pe):
            pe.sem_inc(adj_used, GROUPS - 1)

            def gcn(c, g, first):
                pe.wait_ge(adj_staged[g % SLOTS], c * (16 * GROUPS // SLOTS) + 16 * (g // SLOTS + 1))
                if first:
                    pe.wait_ge(x_split, g + 1)
                if g == 0:
                    pe.wait_ge(ax_ready, c + 1)
                pe.sem_inc(pe_passed, 1)
                for t in range(GROUP):
                    i = GROUP * g + t
                    for k in range(2):
                        mm = pe.matmul(ps_ax[:, :], Gx[:, i, k, :], stage8[:, g % SLOTS, t, :],
                                       start=(i == 0 and k == 0), stop=False)
                if g < GROUPS - 1:
                    mm.then_inc(adj_used, 1)
                else:
                    pe.wait_ge(own_ready, c + 1)
                    for b in range(BLOCKS):
                        mm = pe.matmul(ps_ax[:, b * P:(b + 1) * P], xs[:, b, :], ident[:, :],
                                       start=False, stop=(b == BLOCKS - 1))
                    mm.then_inc(gcn_done, 1)

            def weigh(c):
                pe.wait_ge(ax_ready, c + 2)
                for b in range(BLOCKS):
                    mm = pe.matmul(ps_o[:, b * P:(b + 1) * P], ax[:, b * P:(b + 1) * P], W[:, :],
                                   start=True, stop=True)
                mm.then_inc(o_done, 1)

            def turn(c):
                pe.wait_ge(x3_ready, c + 1)
                for b in range(BLOCKS):
                    mm = pe.transpose(ps_T[:, b * P:(b + 1) * P], y[:, b, :], ident[:, :])
                mm.then_inc(T_done, 1)

            def scores(c):
                pe.wait_ge(T_ready, c + 1)
                for b in range(BLOCKS):
                    mm = pe.matmul(ps_c[:, 2 * b:2 * b + 2], x3T[:, b * P:(b + 1) * P], a3[:, :],
                                   start=True, stop=True)
                mm.then_inc(scores_done, 1)

            pe.wait_ge(w_loaded, 64)
            for g in range(GROUPS):
                gcn(0, g, True)
            with pe.Fori(0, STEPS - 1) as c:
                gcn(c + 1, 0, False)
                weigh(c)
                for g in range(1, 5):
                    gcn(c + 1, g, False)
                turn(c)
                gcn(c + 1, 5, False)
                scores(c)
                gcn(c + 1, 6, False)
                gcn(c + 1, 7, False)
            for piece in (weigh, turn, scores):
                piece(STEPS - 1)
            pe.wait_ge(cols_copied, STEPS)
            pe.transpose(ps_r[0:TILES, 0:P], s1c[:, :], ident[:, :]).then_inc(row_done, 1)

        @block.scalar
        def _(act):
            act.sem_inc(ax_ready, 1)
            for g in range(GROUPS):
                act.wait_ge(x_scaled, g + 1)
                act.activation(Gx[:, GROUP * g:GROUP * (g + 1), 0, :], xin[g][:, :, :], ACT.Copy,
                               scale=SCALE).then_inc(x_hi, 1)
            act.wait_ge(w_loaded, 64)
            act.activation(coe[:, 0, :], coe[:, 0, :], ACT.Exp, scale=-1.0).then_inc(temp_exp, 1)
            with act.Fori(0, STEPS) as c:
                act.wait_ge(gcn_done, c + 1)
                act.activation(ax[:, :], ps_ax[:, :], ACT.Copy, scale=1.0 / SCALE).then_inc(ax_ready, 1)
                act.wait_ge(T_done, c + 1)
                act.activation(x3T[:, :], ps_T[:, :], ACT.Copy).then_inc(T_ready, 1)
            act.wait_ge(row_done, 1)
            act.activation(row[:, :], ps_r[0:TILES, 0:P], ACT.Copy).then_inc(row_ready, 1)
            act.wait_ge(row_ready, 1)
            act.dma_start(dram["s_row_spread"].rearrange("o (t n) -> (o t) n", t=TILES), row[:, :])\
                .then_inc(row_stored, 16)
            act.wait_ge(row_stored, 16)

        @block.vector
        def _(dve):
            dve.tensor_scalar(Ds[:, :], Dc[:, :], SCALE, None, ALU.mult)
            for g in range(GROUPS):
                here = slice(GROUP * g, GROUP * (g + 1))
                x = xin[g][:, :, :]
                dve.wait_ge(x_loaded[g], 16)
                dve.tensor_tensor(x, x, bcast_cols(Dc[:, here], FEAT), ALU.mult).then_inc(x_scaled, 1)
                dve.wait_ge(x_hi, g + 1)
                dve.scalar_tensor_tensor(Gx[:, here, 1, :], x, SCALE, Gx[:, here, 0, :],
                                         ALU.mult, ALU.subtract).then_inc(x_split, 1)
            dve.wait_ge(temp_exp, 1)
            dve.tensor_scalar(coe[:, 1, :], coe[:, 0, :], 1.0, None, ALU.add)
            dve.drain()
            dve.reciprocal(coe[:, 0, :], coe[:, 1, :])
            dve.drain()
            dve.tensor_scalar(coe[:, 1, :], coe[:, 0, :], -1.0, 1.0, ALU.mult, ALU.add)
            dve.tensor_scalar(coe[:, 2, :], coe[:, 0, :], -1.0, None, ALU.mult)

            def own_rows(c):
                dve.wait_ge(next_loaded, 16 * c + 16)
                dve.tensor_tensor(xs[:, :, :], xn[:, :, :], bcast_cols(Ds[:, blocks_of(c)], FEAT), ALU.mult)\
                    .then_inc(own_ready, 1)

            def blocks_of(c):
                return slice(BLOCKS * c, BLOCKS * (c + 1)) if isinstance(c, int) else bass.ds(c * BLOCKS, BLOCKS)

            def finish(c):
                dve.wait_ge(o_done, c + 1)
                dve.wait_ge(y_free, c + 1)
                for b in range(BLOCKS):
                    at = slice(BLOCKS * c + b, BLOCKS * c + b + 1) if isinstance(c, int) \
                        else bass.ds(c * BLOCKS + b, 1)
                    dve.scalar_tensor_tensor(y[:, b, :], ps_o[:, b * P:(b + 1) * P], Dc[:, at], bias[:, :],
                                             ALU.mult, ALU.add)
                dve.drain()
                dve.wait_ge(res_loaded, 16 * c + 16)
                dve.scalar_tensor_tensor(y[:, :, :], y[:, :, :], 0.0, xt[:, :, :], ALU.max, ALU.add)
                dve.drain().then_inc(res_used, 1)
                norm_blocks(dve, y, y, stats, mv, var_ready, rstd_ready, c + 1, rstd).then_inc(x3_ready, 1)
                dve.wait_ge(scores_done, c + 1)
                cols = ps_c[:, 0:2 * BLOCKS].rearrange("p (b c) -> p c b", c=2)
                dve.tensor_copy(s1c[:, blocks_of(c)], cols[:, 0, :])
                dve.tensor_copy(s2c[:, blocks_of(c)], cols[:, 1, :])
                dve.drain().then_inc(cols_copied, 1)

            dve.sem_inc(y_free, 1)
            dve.sem_inc(res_used, 1)
            own_rows(0)
            with dve.Fori(0, STEPS - 1) as c:
                dve.wait_ge(gcn_done, c + 1)
                own_rows(c + 1)
                finish(c)
            finish(STEPS - 1)


def build_program(nc, dram):
    with Arena(nc, "kept") as a:
        kept = {"adj": a.sb("adj", [P, TILES * N], U8)}
        for name in ("s1c", "s2c", "F1", "F2", "alpha", "beta", "alpha_low", "beta_low", "deg", "Dc", "rden", "rowsum"):
            kept[name] = a.sb(name, [P, TILES], F32)
        kept["ident"] = a.sb("ident", [P, P], F32)
        kept["A"] = a.sb("A", [P, 2, 16], F32)
        kept["w_out"] = a.sb("w_out", [P, 2, FEAT], F32)
        kept["pick"] = a.sb("pick", [PARTS * 32, 32], BF16)
        kept["coe"] = a.sb("coe", [P, 3, 5], F32)
        kept["wide_flag"] = a.sb("wide_flag", [P, 1], mybir.dt.int32)
        attention_pass(nc, "gat", kept, dram)
        mamba_inputs_stage(nc, kept, dram)
        mamba_scan_stage(nc, kept, dram)
        gcn_stage(nc, kept, dram)
        attention_pass(nc, "spread", kept, dram)
        attention_pass(nc, "mix", kept, dram)


def kernel(**inputs):
    import numpy as _np
    import concourse.bacc as _bacc
    from concourse.bass_utils import run_bass_kernel_spmd as _run

    i = {k: _np.asarray(v) for k, v in inputs.items()}
    given = {
        "x": i["x"], "xT": i["x"].T, "adjT": i["adj"].T,
        "W0": i["L0_gnn_W"], "W0T": i["L0_gnn_W"].T, "a0": i["L0_gnn_a"].reshape(2, FEAT).T,
        "h0": i["L3_gnn_h0"],
        "W2": i["L2_gnn_W"], "b2": i["L2_gnn_b"].reshape(1, FEAT),
        "a3": i["L3_gnn_a"].reshape(2, FEAT).T, "temp": i["L3_gnn_temp"].reshape(1, 5),
        "gcn_w": i["L1_gnn_gcn_w"], "gcn_b": i["L1_gnn_gcn_b"].reshape(1, FEAT),
        "w_in": i["L1_gnn_w_in"],
        "w_xp": _np.concatenate([i["L1_gnn_w_xp"][:, 8:], i["L1_gnn_w_xp"][:, :8]], 1), "w_dt": i["L1_gnn_w_dt"],
        "A_log": i["L1_gnn_A_log"], "w_out": i["L1_gnn_w_out"],
        "cvec": _np.concatenate([i["L1_gnn_ln_g"][:, None], i["L1_gnn_ln_b"][:, None],
                                 _np.concatenate([i["L1_gnn_conv_w"], i["L1_gnn_conv_b"][:, None],
                                                  i["L1_gnn_b_dt"][:, None], i["L1_gnn_D_skip"][:, None]], 1)
                                 .reshape(2, P, 7).transpose(1, 0, 2).reshape(P, 14)], 1),
    }
    nc = _bacc.Bacc("TRN2", target_bir_lowering=False, num_devices=1)
    arrays, dram = {}, {}
    for name, v in given.items():
        v = _np.ascontiguousarray(v)
        arrays[f"in_{name}"] = v
        dram[name] = nc.dram_tensor(f"in_{name}", v.shape, mybir.dt.from_np(v.dtype), kind="ExternalInput").ap()
    for name, shape in (("x1", [N, FEAT]), ("x2", [N, FEAT]), ("x3", [N, FEAT]),
                        ("feat", [N, FEAT]), ("s_row_gat", [1, N]), ("s_row_spread", [1, N])):
        dram[name] = nc.dram_tensor(f"scratch_{name}", shape, F32, kind="Internal").ap()
    for name in ("dt", "du", "ud", "sz"):
        dram[name] = nc.dram_tensor(f"scratch_{name}", [2, P, N], F32, kind="Internal").ap()
    dram["bc_parts"] = nc.dram_tensor("scratch_bc_parts", [PARTS, 32, N], BF16, kind="Internal").ap()
    dram["out"] = nc.dram_tensor("out_x", [N, FEAT], F32, kind="ExternalOutput").ap()
    build_program(nc, dram)
    r = _run(nc, [arrays], core_ids=[0])
    return r.results[0]["out_x"]
```
